# Optimizing a Trainium2 kernel written in Bass

```python
import numpy as np
import jax
import jax.numpy as jnp

def _softmax(x, axis=-1):
    return jax.nn.softmax(x, axis=axis)

def _gelu(x):
    return jax.nn.gelu(x, approximate=True)

def _silu(x):
    return jax.nn.silu(x)

def _sigmoid(x):
    return jax.nn.sigmoid(x)

def _layernorm(x, axis=-1, eps=1e-05):
    m = jnp.mean(x, axis=axis, keepdims=True)
    v = jnp.var(x, axis=axis, keepdims=True)
    return (x - m) / jnp.sqrt(v + eps)

def _scatter_add(tgt, idx, src, axis=0):
    return tgt.at[idx].add(src)

def _segment_sum(src, seg, n):
    return jax.ops.segment_sum(src, seg, n)
kernel_name = 'mk_seq_postln_d2_jaxref_r4_19a700'

def setup_inputs(seed: int=0):
    np.random.seed(seed)
    _w = jnp.asarray

    def _L0_attn_setup():
        import jax, jax.numpy as jnp
        import numpy as np
        import math
        B, N, D, H, G = (4, 512, 256, 16, 512)
        HD = D // H
        MAX_SEQ = 512
        STRIDE = (G - 1) / max(MAX_SEQ - 1, 1)

        def _forward(x, Wqkvg, bqkvg, wave_frequency, wave_damping, wave_phase, field_coupling, Wout, bout):
            b, n, d = x.shape
            qkvg = x @ Wqkvg.T + bqkvg
            q, k, v, gate_raw = jnp.split(qkvg, 4, axis=-1)
            to_heads = lambda t: t.reshape(b, n, H, HD).transpose(0, 2, 1, 3)
            q, k, v = (to_heads(q), to_heads(k), to_heads(v))
            seq_pos = jnp.arange(n, dtype=jnp.float32)
            field_pos = jnp.clip(seq_pos * STRIDE, 0.0, G - 2)
            idx_lo = jnp.clip(field_pos.astype(jnp.int32), 0, G - 2)
            idx_hi = idx_lo + 1
            frac = jnp.clip(field_pos - idx_lo.astype(jnp.float32), 0.0, 1.0)
            w_lo = (1.0 - frac)[None, None, :, None]
            w_hi = frac[None, None, :, None]
            q_feat = jax.nn.elu(q) + 1.0
            k_feat = jax.nn.elu(k) + 1.0
            deposit = k_feat * v
            field = jnp.zeros((b, H, G, HD), deposit.dtype)
            field = field.at[:, :, idx_lo, :].add(deposit * w_lo)
            field = field.at[:, :, idx_hi, :].add(deposit * w_hi)
            t = jnp.arange(G, dtype=jnp.float32)
            alpha = jax.nn.softplus(wave_damping)[:, None]
            omega = wave_frequency[:, None]
            phi = wave_phase[:, None]
            kernels = jnp.exp(-alpha * t[None, :]) * jnp.cos(omega * t[None, :] + phi)
            kernels = kernels / jnp.clip(jnp.sum(jnp.abs(kernels), axis=1, keepdims=True), 1e-08)
            kernel_fft = jnp.fft.rfft(kernels, n=2 * G, axis=-1)
            field_fft = jnp.fft.rfft(field, n=2 * G, axis=2)
            convolved = jnp.fft.irfft(field_fft * kernel_fft[None, :, :, None], n=2 * G, axis=2)[:, :, :G, :]
            coupling = jax.nn.softmax(field_coupling, axis=-1)
            field_c = jnp.einsum('ij,bjgd->bigd', coupling, convolved)
            gathered = field_c[:, :, idx_lo, :] * w_lo + field_c[:, :, idx_hi, :] * w_hi
            wave_output = q_feat * gathered
            gate = jax.nn.sigmoid(gate_raw).reshape(b, n, H, HD).transpose(0, 2, 1, 3)
            output = (wave_output * gate).transpose(0, 2, 1, 3).reshape(b, n, d)
            return output @ Wout.T + bout
        key = jax.random.key(seed)
        ks = jax.random.split(key, 5)
        x = jax.random.normal(ks[0], (B, N, D), jnp.float32)
        Wqkvg = jax.random.normal(ks[1], (4 * D, D), jnp.float32) * 0.02
        Wqkvg = Wqkvg.at[3 * D:].set(0.0)
        bqkvg = jnp.concatenate([jnp.zeros(3 * D, jnp.float32), jnp.full((D,), 2.0, jnp.float32)])
        wave_frequency = jnp.linspace(0.3, 4.0, H, dtype=jnp.float32)
        wave_damping = jnp.linspace(-3.0, 0.5, H, dtype=jnp.float32)
        wave_phase = jnp.linspace(0.0, math.pi, H, dtype=jnp.float32)
        field_coupling = jnp.eye(H, dtype=jnp.float32) + jax.random.normal(ks[2], (H, H), jnp.float32) * 0.01
        Wout = jax.random.normal(ks[3], (D, D), jnp.float32) * 0.02
        bout = jnp.zeros(D, jnp.float32)
        return dict(x=x, Wqkvg=Wqkvg, bqkvg=bqkvg, wave_frequency=wave_frequency, wave_damping=wave_damping, wave_phase=wave_phase, field_coupling=field_coupling, Wout=Wout, bout=bout)
    _L0_attn_in = _L0_attn_setup()

    def _L0_ffn_setup():
        import jax, jax.numpy as jnp
        import numpy as np
        HIDDEN = 256
        HEAD_DIM = 64
        N_EXPERTS = 16
        MIN_EXPERTS = 2
        B, T = (4, 512)

        def _normalize(x, axis):
            n = jnp.sqrt(jnp.sum(x * x, axis=axis, keepdims=True))
            return x / jnp.maximum(n, 1e-12)

        def _ste(x):
            hard = jax.lax.stop_gradient((x > 0).astype(x.dtype))
            return hard + x - jax.lax.stop_gradient(x)

        def _gating(hidden_states, sim_matrix, gates):
            b, t, c = hidden_states.shape
            flat = hidden_states.reshape(b * t, c)
            logits = _normalize(flat, -1) @ _normalize(sim_matrix, 0) - jax.nn.sigmoid(gates)
            gated = jax.nn.relu(logits)
            mask = _ste(gated)
            inactive = jnp.sum(mask, axis=1) == 0
            _, fb_idx = jax.lax.top_k(logits, MIN_EXPERTS)
            fb = jnp.zeros_like(mask).at[jnp.arange(b * t)[:, None], fb_idx].set(1.0)
            fb_applied = inactive[:, None] & (fb > 0)
            mask = jnp.where(fb_applied, 1.0, mask)
            masked_logits = jnp.where(mask > 0, gated, -jnp.inf)
            return jax.nn.softmax(masked_logits, axis=-1).reshape(b, t, -1)
        key = jax.random.key(seed)
        ks = jax.random.split(key, 6)
        xav_qkv = float(np.sqrt(6.0 / (HIDDEN + HEAD_DIM)))
        return {'hidden_states': jax.random.normal(ks[0], (B, T, HIDDEN), dtype=jnp.float32), 'sim_matrix': jax.random.normal(ks[1], (HIDDEN, N_EXPERTS), dtype=jnp.float32), 'gates': jnp.zeros((N_EXPERTS,), dtype=jnp.float32), 'q_proj': jax.random.uniform(ks[2], (N_EXPERTS, HIDDEN, HEAD_DIM), jnp.float32, -xav_qkv, xav_qkv), 'k_proj': jax.random.uniform(ks[3], (N_EXPERTS, HIDDEN, HEAD_DIM), jnp.float32, -xav_qkv, xav_qkv), 'v_proj': jax.random.uniform(ks[4], (N_EXPERTS, HIDDEN, HEAD_DIM), jnp.float32, -xav_qkv, xav_qkv), 'o_proj': jax.random.uniform(ks[5], (N_EXPERTS, HEAD_DIM, HIDDEN), jnp.float32, -xav_qkv, xav_qkv)}
    _L0_ffn_in = _L0_ffn_setup()

    def _L1_attn_setup():
        import jax, jax.numpy as jnp
        import numpy as np
        from jax import lax
        D_MODEL, D_STATE, D_CONV, EXPAND = (256, 16, 4, 2)
        D_INNER = D_MODEL * EXPAND
        BATCH, SEQ = (4, 512)

        def _mamba_forward(x, W_in, conv_w, conv_b, W_x, W_dt, b_dt, A_log, D, W_out):
            batch, seq_len, _ = x.shape
            xz = x @ W_in
            x_in, z = jnp.split(xz, 2, axis=-1)
            x_c = lax.conv_general_dilated(x_in.transpose(0, 2, 1), conv_w, window_strides=(1,), padding=[(D_CONV - 1, 0)], feature_group_count=D_INNER, dimension_numbers=('NCH', 'OIH', 'NCH')) + conv_b[None, :, None]
            x_conv = jax.nn.silu(x_c.transpose(0, 2, 1))
            A = -jnp.exp(A_log)
            Bm, Cm = jnp.split(x_conv @ W_x, 2, axis=-1)
            dt = jax.nn.softplus(x_conv @ W_dt + b_dt)

            def step(h, ins):
                u_t, dt_t, B_t, C_t = ins
                dA = jnp.exp(dt_t[:, :, None] * A)
                h = dA * h + (dt_t * u_t)[:, :, None] * B_t[:, None, :]
                y_t = jnp.einsum('bdn,bn->bd', h, C_t)
                return (h, y_t)
            h0 = jnp.zeros((batch, D_INNER, D_STATE), dtype=x.dtype)
            xs = (x_conv.transpose(1, 0, 2), dt.transpose(1, 0, 2), Bm.transpose(1, 0, 2), Cm.transpose(1, 0, 2))
            _, ys = lax.scan(step, h0, xs)
            y = ys.transpose(1, 0, 2)
            y = y + x_conv * D
            y = y * jax.nn.silu(z)
            return y @ W_out
        key = jax.random.key(seed)
        ks = jax.random.split(key, 9)
        s = lambda fan_in: 1.0 / np.sqrt(fan_in)
        return {'x': jax.random.normal(ks[0], (BATCH, SEQ, D_MODEL), dtype=jnp.float32), 'W_in': jax.random.normal(ks[1], (D_MODEL, 2 * D_INNER), dtype=jnp.float32) * s(D_MODEL), 'conv_w': jax.random.normal(ks[2], (D_INNER, 1, D_CONV), dtype=jnp.float32) * s(D_CONV), 'conv_b': jax.random.normal(ks[3], (D_INNER,), dtype=jnp.float32) * 0.01, 'W_x': jax.random.normal(ks[4], (D_INNER, 2 * D_STATE), dtype=jnp.float32) * s(D_INNER), 'W_dt': jax.random.normal(ks[5], (D_INNER, D_INNER), dtype=jnp.float32) * s(D_INNER), 'b_dt': jax.random.normal(ks[6], (D_INNER,), dtype=jnp.float32) * 0.01, 'A_log': jnp.log(jnp.arange(1, D_STATE + 1, dtype=jnp.float32)), 'D': jnp.ones((D_INNER,), dtype=jnp.float32), 'W_out': jax.random.normal(ks[7], (D_INNER, D_MODEL), dtype=jnp.float32) * s(D_INNER)}
    _L1_attn_in = _L1_attn_setup()

    def _L1_ffn_setup():
        import jax, jax.numpy as jnp
        import numpy as np
        NUM_EXPERTS = 8
        HIDDEN = 256
        INTER = 256
        BATCH = 2
        SEQ = 256
        TOP_K = 2
        SWIGLU_ALPHA = 1.702
        LIMIT = 7.0

        def _grouped_mm(x, w, expert_ids):
            onehot = jax.nn.one_hot(expert_ids, w.shape[0], dtype=x.dtype)
            y_all = jnp.einsum('tk,ekn->etn', x, w)
            return jnp.einsum('te,etn->tn', onehot, y_all)

        def _gpt_oss_swiglu(x):
            gate = jnp.minimum(x[..., ::2], LIMIT)
            up = jnp.clip(x[..., 1::2], -LIMIT, LIMIT)
            glu = gate * jax.nn.sigmoid(gate * SWIGLU_ALPHA)
            return (up + 1.0) * glu
        key = jax.random.key(seed)
        ks = jax.random.split(key, 7)
        hidden_states = jax.random.normal(ks[0], (BATCH, SEQ, HIDDEN), jnp.float32)
        router_indices = jax.random.randint(ks[1], (BATCH * SEQ, TOP_K), 0, NUM_EXPERTS)
        routing_weights = jax.nn.softmax(jax.random.normal(ks[2], (BATCH * SEQ, NUM_EXPERTS), jnp.float32), axis=-1)
        scale = 0.02
        gate_up_proj = jax.random.normal(ks[3], (NUM_EXPERTS, HIDDEN, 2 * INTER), jnp.float32) * scale
        gate_up_proj_bias = jax.random.normal(ks[4], (NUM_EXPERTS, 2 * INTER), jnp.float32) * scale
        down_proj = jax.random.normal(ks[5], (NUM_EXPERTS, INTER, HIDDEN), jnp.float32) * scale
        down_proj_bias = jax.random.normal(ks[6], (NUM_EXPERTS, HIDDEN), jnp.float32) * scale
        return {'hidden_states': hidden_states, 'router_indices': router_indices, 'routing_weights': routing_weights, 'gate_up_proj': gate_up_proj, 'gate_up_proj_bias': gate_up_proj_bias, 'down_proj': down_proj, 'down_proj_bias': down_proj_bias}
    _L1_ffn_in = _L1_ffn_setup()
    _d = {'L0_attn_x': _L0_attn_in['x'], 'L0_attn_Wqkvg': _L0_attn_in['Wqkvg'], 'L0_attn_bqkvg': _L0_attn_in['bqkvg'], 'L0_attn_wave_frequency': _L0_attn_in['wave_frequency'], 'L0_attn_wave_damping': _L0_attn_in['wave_damping'], 'L0_attn_wave_phase': _L0_attn_in['wave_phase'], 'L0_attn_field_coupling': _L0_attn_in['field_coupling'], 'L0_attn_Wout': _L0_attn_in['Wout'], 'L0_attn_bout': _L0_attn_in['bout'], 'L0_ffn_sim_matrix': _L0_ffn_in['sim_matrix'], 'L0_ffn_gates': _L0_ffn_in['gates'], 'L0_ffn_q_proj': _L0_ffn_in['q_proj'], 'L0_ffn_k_proj': _L0_ffn_in['k_proj'], 'L0_ffn_v_proj': _L0_ffn_in['v_proj'], 'L0_ffn_o_proj': _L0_ffn_in['o_proj'], 'L1_attn_W_in': _L1_attn_in['W_in'], 'L1_attn_conv_w': _L1_attn_in['conv_w'], 'L1_attn_conv_b': _L1_attn_in['conv_b'], 'L1_attn_W_x': _L1_attn_in['W_x'], 'L1_attn_W_dt': _L1_attn_in['W_dt'], 'L1_attn_b_dt': _L1_attn_in['b_dt'], 'L1_attn_A_log': _L1_attn_in['A_log'], 'L1_attn_D': _L1_attn_in['D'], 'L1_attn_W_out': _L1_attn_in['W_out'], 'L1_ffn_router_indices': _L1_ffn_in['router_indices'], 'L1_ffn_routing_weights': _L1_ffn_in['routing_weights'], 'L1_ffn_gate_up_proj': _L1_ffn_in['gate_up_proj'], 'L1_ffn_gate_up_proj_bias': _L1_ffn_in['gate_up_proj_bias'], 'L1_ffn_down_proj': _L1_ffn_in['down_proj'], 'L1_ffn_down_proj_bias': _L1_ffn_in['down_proj_bias']}
    _x0 = _d['L0_attn_x']
    _d['L0_attn_x'] = jax.random.normal(jax.random.fold_in(jax.random.key(seed), 1), (4, 2048, 256), dtype=_x0.dtype)
    del _x0
    return _d

def reference(L0_attn_x, L0_attn_Wqkvg, L0_attn_bqkvg, L0_attn_wave_frequency, L0_attn_wave_damping, L0_attn_wave_phase, L0_attn_field_coupling, L0_attn_Wout, L0_attn_bout, L0_ffn_sim_matrix, L0_ffn_gates, L0_ffn_q_proj, L0_ffn_k_proj, L0_ffn_v_proj, L0_ffn_o_proj, L1_attn_W_in, L1_attn_conv_w, L1_attn_conv_b, L1_attn_W_x, L1_attn_W_dt, L1_attn_b_dt, L1_attn_A_log, L1_attn_D, L1_attn_W_out, L1_ffn_router_indices, L1_ffn_routing_weights, L1_ffn_gate_up_proj, L1_ffn_gate_up_proj_bias, L1_ffn_down_proj, L1_ffn_down_proj_bias):

    def _L0_attn_ref(x, Wqkvg, bqkvg, wave_frequency, wave_damping, wave_phase, field_coupling, Wout, bout):
        import jax, jax.numpy as jnp
        import numpy as np
        import math
        B, N, D, H, G = (4, 512, 256, 16, 512)
        HD = D // H
        MAX_SEQ = 512
        STRIDE = (G - 1) / max(MAX_SEQ - 1, 1)

        def _forward(x, Wqkvg, bqkvg, wave_frequency, wave_damping, wave_phase, field_coupling, Wout, bout):
            b, n, d = x.shape
            qkvg = x @ Wqkvg.T + bqkvg
            q, k, v, gate_raw = jnp.split(qkvg, 4, axis=-1)
            to_heads = lambda t: t.reshape(b, n, H, HD).transpose(0, 2, 1, 3)
            q, k, v = (to_heads(q), to_heads(k), to_heads(v))
            seq_pos = jnp.arange(n, dtype=jnp.float32)
            field_pos = jnp.clip(seq_pos * STRIDE, 0.0, G - 2)
            idx_lo = jnp.clip(field_pos.astype(jnp.int32), 0, G - 2)
            idx_hi = idx_lo + 1
            frac = jnp.clip(field_pos - idx_lo.astype(jnp.float32), 0.0, 1.0)
            w_lo = (1.0 - frac)[None, None, :, None]
            w_hi = frac[None, None, :, None]
            q_feat = jax.nn.elu(q) + 1.0
            k_feat = jax.nn.elu(k) + 1.0
            deposit = k_feat * v
            field = jnp.zeros((b, H, G, HD), deposit.dtype)
            field = field.at[:, :, idx_lo, :].add(deposit * w_lo)
            field = field.at[:, :, idx_hi, :].add(deposit * w_hi)
            t = jnp.arange(G, dtype=jnp.float32)
            alpha = jax.nn.softplus(wave_damping)[:, None]
            omega = wave_frequency[:, None]
            phi = wave_phase[:, None]
            kernels = jnp.exp(-alpha * t[None, :]) * jnp.cos(omega * t[None, :] + phi)
            kernels = kernels / jnp.clip(jnp.sum(jnp.abs(kernels), axis=1, keepdims=True), 1e-08)
            kernel_fft = jnp.fft.rfft(kernels, n=2 * G, axis=-1)
            field_fft = jnp.fft.rfft(field, n=2 * G, axis=2)
            convolved = jnp.fft.irfft(field_fft * kernel_fft[None, :, :, None], n=2 * G, axis=2)[:, :, :G, :]
            coupling = jax.nn.softmax(field_coupling, axis=-1)
            field_c = jnp.einsum('ij,bjgd->bigd', coupling, convolved)
            gathered = field_c[:, :, idx_lo, :] * w_lo + field_c[:, :, idx_hi, :] * w_hi
            wave_output = q_feat * gathered
            gate = jax.nn.sigmoid(gate_raw).reshape(b, n, H, HD).transpose(0, 2, 1, 3)
            output = (wave_output * gate).transpose(0, 2, 1, 3).reshape(b, n, d)
            return output @ Wout.T + bout
        return _forward(x, Wqkvg, bqkvg, wave_frequency, wave_damping, wave_phase, field_coupling, Wout, bout)

    def _L0_ffn_ref(hidden_states, sim_matrix, gates, q_proj, k_proj, v_proj, o_proj):
        import jax, jax.numpy as jnp
        import numpy as np
        HIDDEN = 256
        HEAD_DIM = 64
        N_EXPERTS = 16
        MIN_EXPERTS = 2
        B, T = (4, 512)

        def _normalize(x, axis):
            n = jnp.sqrt(jnp.sum(x * x, axis=axis, keepdims=True))
            return x / jnp.maximum(n, 1e-12)

        def _ste(x):
            hard = jax.lax.stop_gradient((x > 0).astype(x.dtype))
            return hard + x - jax.lax.stop_gradient(x)

        def _gating(hidden_states, sim_matrix, gates):
            b, t, c = hidden_states.shape
            flat = hidden_states.reshape(b * t, c)
            logits = _normalize(flat, -1) @ _normalize(sim_matrix, 0) - jax.nn.sigmoid(gates)
            gated = jax.nn.relu(logits)
            mask = _ste(gated)
            inactive = jnp.sum(mask, axis=1) == 0
            _, fb_idx = jax.lax.top_k(logits, MIN_EXPERTS)
            fb = jnp.zeros_like(mask).at[jnp.arange(b * t)[:, None], fb_idx].set(1.0)
            fb_applied = inactive[:, None] & (fb > 0)
            mask = jnp.where(fb_applied, 1.0, mask)
            masked_logits = jnp.where(mask > 0, gated, -jnp.inf)
            return jax.nn.softmax(masked_logits, axis=-1).reshape(b, t, -1)
        b, t, c = hidden_states.shape
        rw = _gating(hidden_states, sim_matrix, gates)
        q = jnp.einsum('bte,bted->btd', rw, jnp.einsum('btc,ecd->bted', hidden_states, q_proj))
        k = jnp.einsum('bte,bted->btd', rw, jnp.einsum('btc,ecd->bted', hidden_states, k_proj))
        v = jnp.einsum('bte,bted->btd', rw, jnp.einsum('btc,ecd->bted', hidden_states, v_proj))
        scale = 1.0 / jnp.sqrt(jnp.asarray(HEAD_DIM, dtype=q.dtype))
        scores = jnp.einsum('bqd,bkd->bqk', q, k) * scale
        causal = jnp.tril(jnp.ones((t, t), dtype=bool))
        scores = jnp.where(causal, scores, -jnp.inf)
        attn = jnp.einsum('bqk,bkd->bqd', jax.nn.softmax(scores, axis=-1), v)
        mixed = attn[:, :, None, :] * rw[..., None]
        return jnp.einsum('bted,edc->btc', mixed, o_proj)

    def _L1_attn_ref(x, W_in, conv_w, conv_b, W_x, W_dt, b_dt, A_log, D, W_out):
        import jax, jax.numpy as jnp
        import numpy as np
        from jax import lax
        D_MODEL, D_STATE, D_CONV, EXPAND = (256, 16, 4, 2)
        D_INNER = D_MODEL * EXPAND
        BATCH, SEQ = (4, 512)

        def _mamba_forward(x, W_in, conv_w, conv_b, W_x, W_dt, b_dt, A_log, D, W_out):
            batch, seq_len, _ = x.shape
            xz = x @ W_in
            x_in, z = jnp.split(xz, 2, axis=-1)
            x_c = lax.conv_general_dilated(x_in.transpose(0, 2, 1), conv_w, window_strides=(1,), padding=[(D_CONV - 1, 0)], feature_group_count=D_INNER, dimension_numbers=('NCH', 'OIH', 'NCH')) + conv_b[None, :, None]
            x_conv = jax.nn.silu(x_c.transpose(0, 2, 1))
            A = -jnp.exp(A_log)
            Bm, Cm = jnp.split(x_conv @ W_x, 2, axis=-1)
            dt = jax.nn.softplus(x_conv @ W_dt + b_dt)

            def step(h, ins):
                u_t, dt_t, B_t, C_t = ins
                dA = jnp.exp(dt_t[:, :, None] * A)
                h = dA * h + (dt_t * u_t)[:, :, None] * B_t[:, None, :]
                y_t = jnp.einsum('bdn,bn->bd', h, C_t)
                return (h, y_t)
            h0 = jnp.zeros((batch, D_INNER, D_STATE), dtype=x.dtype)
            xs = (x_conv.transpose(1, 0, 2), dt.transpose(1, 0, 2), Bm.transpose(1, 0, 2), Cm.transpose(1, 0, 2))
            _, ys = lax.scan(step, h0, xs)
            y = ys.transpose(1, 0, 2)
            y = y + x_conv * D
            y = y * jax.nn.silu(z)
            return y @ W_out
        return _mamba_forward(x, W_in, conv_w, conv_b, W_x, W_dt, b_dt, A_log, D, W_out)

    def _L1_ffn_ref(hidden_states, router_indices, routing_weights, gate_up_proj, gate_up_proj_bias, down_proj, down_proj_bias):
        import jax, jax.numpy as jnp
        import numpy as np
        NUM_EXPERTS = 8
        HIDDEN = 256
        INTER = 256
        BATCH = 2
        SEQ = 256
        TOP_K = 2
        SWIGLU_ALPHA = 1.702
        LIMIT = 7.0

        def _grouped_mm(x, w, expert_ids):
            onehot = jax.nn.one_hot(expert_ids, w.shape[0], dtype=x.dtype)
            y_all = jnp.einsum('tk,ekn->etn', x, w)
            return jnp.einsum('te,etn->tn', onehot, y_all)

        def _gpt_oss_swiglu(x):
            gate = jnp.minimum(x[..., ::2], LIMIT)
            up = jnp.clip(x[..., 1::2], -LIMIT, LIMIT)
            glu = gate * jax.nn.sigmoid(gate * SWIGLU_ALPHA)
            return (up + 1.0) * glu
        B = hidden_states.shape[0]
        H = hidden_states.shape[-1]
        x = hidden_states.reshape(-1, H)
        M = x.shape[0]
        top_k = router_indices.shape[1]
        num_experts = gate_up_proj.shape[0]
        topk_weights = jnp.take_along_axis(routing_weights, router_indices, axis=1)
        flat_experts = router_indices.reshape(-1)
        sort_idx = jnp.argsort(flat_experts)
        sorted_pos = sort_idx // top_k
        expert_sorted = flat_experts[sort_idx]
        grouped = x[sorted_pos]
        gate_up = _grouped_mm(grouped, gate_up_proj, expert_sorted)
        gate_up = gate_up + gate_up_proj_bias[expert_sorted]
        inter = _gpt_oss_swiglu(gate_up)
        down = _grouped_mm(inter, down_proj, expert_sorted)
        down = down + down_proj_bias[expert_sorted]
        down = down * topk_weights.reshape(-1)[sort_idx][:, None]
        out = jnp.zeros((M, H), x.dtype).at[sorted_pos].add(down)
        return out.reshape(B, -1, H)
    x = L0_attn_x
    x = _layernorm(x + _L0_attn_ref(x, L0_attn_Wqkvg, L0_attn_bqkvg, L0_attn_wave_frequency, L0_attn_wave_damping, L0_attn_wave_phase, L0_attn_field_coupling, L0_attn_Wout, L0_attn_bout), axis=-1)
    x = _layernorm(x + _L0_ffn_ref(x, L0_ffn_sim_matrix, L0_ffn_gates, L0_ffn_q_proj, L0_ffn_k_proj, L0_ffn_v_proj, L0_ffn_o_proj), axis=-1)
    x = _layernorm(x + _L1_attn_ref(x, L1_attn_W_in, L1_attn_conv_w, L1_attn_conv_b, L1_attn_W_x, L1_attn_W_dt, L1_attn_b_dt, L1_attn_A_log, L1_attn_D, L1_attn_W_out), axis=-1)
    x = _layernorm(x + _L1_ffn_ref(x, L1_ffn_router_indices, L1_ffn_routing_weights, L1_ffn_gate_up_proj, L1_ffn_gate_up_proj_bias, L1_ffn_down_proj, L1_ffn_down_proj_bias), axis=-1)
    return x

_drawn_inputs = setup_inputs


def setup_inputs(seed=0):
    import zlib

    import numpy as np

    out = dict(_drawn_inputs(seed))
    spreads = {'L0_attn_bout': (0.0, 0.1), 'L0_ffn_gates': (0.0, 0.1), 'L1_attn_D': (1.0, 0.2)}
    factors = {'L1_attn_conv_b': 8.0,
     'L1_attn_b_dt': 22.848,
     'L1_ffn_routing_weights': 8.0,
     'L1_ffn_gate_up_proj': 8.0,
     'L1_ffn_gate_up_proj_bias': 8.0,
     'L1_ffn_down_proj': 8.0,
     'L1_ffn_down_proj_bias': 64.0}
    for name, (base, spread) in spreads.items():
        noise = np.random.default_rng([zlib.crc32(name.encode()), seed]).standard_normal(out[name].shape)
        drawn = base * np.exp(spread * noise) if base else spread * noise
        out[name] = jnp.asarray(drawn.astype(out[name].dtype))
    for name, factor in factors.items():
        out[name] = (out[name] * factor).astype(out[name].dtype)
    return out
```

```python
import math
from contextlib import ExitStack

import concourse.bass as bass
from concourse import mybir

F32 = mybir.dt.float32
BF16 = mybir.dt.bfloat16
I32 = mybir.dt.int32
ALU = mybir.AluOpType
ACT = mybir.ActivationFunctionType
AX = mybir.AxisListType

P = 128
BATCH, SEQ, D = 4, 2048, 256
TILES = SEQ // P
CHUNK = 512
CHUNKS = SEQ // CHUNK
KC = D // P
EPS = 1e-5
HEADS, HD, FIELD = 16, 16, 512
LAST = FIELD - 2
EXPERTS, EHD = 16, 64
QKV = 3 * EHD
INNER, STATE, TAPS = 512, 16, 4
KI = INNER // P
MOE_E, MOE_TOK, MOE_F = 8, 512, 256
LIMIT, ALPHA = 7.0, 1.702
MASKED = -1e30
HALF = SEQ // 2


def build_program(nc, t, out):
    kpad = nc.dram_tensor("kernel_rows", (HEADS, 640), F32).ap()
    x2_dram = nc.dram_tensor("x_after_layer0", (BATCH, SEQ, D), F32).ap()
    x2T_dram = nc.dram_tensor("xT_after_layer0", (BATCH, D, SEQ), F32).ap()

    top = ExitStack()
    with top:
        def tile(stack, name, shape, dt=F32):
            return stack.enter_context(nc.sbuf_tensor(name, shape, dt))

        sems = {}

        def sem(name):
            if name not in sems:
                sems[name] = top.enter_context(nc.semaphore(name))
            return sems[name]

        def clear(names_before):
            numbers = [h.num for n, h in sems.items() if n not in names_before]
            nc.gpsimd.sem_clear(range(min(numbers), max(numbers) + 1))
            nc.all_engine_barrier(sem_only=True)

        PS = top.enter_context(nc.psum_tensor("PS", [P, 8 * CHUNK], F32))

        def bank(i, n=1):
            return PS[:, i * CHUNK:(i + n) * CHUNK]

        ident = tile(top, "ident", [P, P])
        ones = tile(top, "ones", [P, P])
        eps_pow = tile(top, "eps_pow", [P, TILES])
        half_pow = tile(top, "half_pow", [P, TILES])

        def normalize(name, tok, xT, tiles=TILES, also=None):
            with ExitStack() as s:
                stats = tile(s, name + "_stats", [P, TILES, 6])
                mv = tile(s, name + "_mv", [P, TILES, 2])
                var = tile(s, name + "_var", [P, TILES])
                rstd = tile(s, name + "_rstd", [P, TILES])
                var_ready, rstd_ready = sem(name + "_var_ready"), sem(name + "_rstd_ready")
                norm_done, tr_ready = sem(name + "_norm_done"), sem(name + "_tr_ready")
                tr_copied = sem(name + "_tr_copied")
                with nc.Block() as block:
                    @block.vector
                    def _(dve):
                        def scale(g):
                            dve.wait_ge(rstd_ready, g + 1)
                            for i in range(4 * g, 4 * g + 4):
                                dve.tensor_scalar(tok[:, i, :], tok[:, i, :], mv[:, i, 0:1], rstd[:, i:i + 1],
                                                  ALU.subtract, ALU.mult).then_inc(norm_done, 1)

                        for g in range(tiles // 4):
                            for i in range(4 * g, 4 * g + 4):
                                dve.bn_stats(stats[:, i, :], tok[:, i, :])
                            dve.drain()
                            for i in range(4 * g, 4 * g + 4):
                                dve.bn_aggr(mv[:, i, :], stats[:, i, :])
                            dve.drain()
                            dve.tensor_scalar(var[:, 4 * g:4 * g + 4], mv[:, 4 * g:4 * g + 4, 1], EPS, None,
                                              ALU.add).then_inc(var_ready, 1)
                            if g:
                                scale(g - 1)
                        scale(tiles // 4 - 1)

                    @block.gpsimd
                    def _(pool):
                        for g in range(tiles // 4):
                            pool.wait_ge(var_ready, g + 1)
                            w = slice(4 * g, 4 * g + 4)
                            pool.tensor_tensor(rstd[:, w], var[:, w], eps_pow[:, w], ALU.pow)\
                                .then_inc(rstd_ready, 1)

                    if xT is not None:
                        @block.tensor
                        def _(pe):
                            for p in range(tiles // 2):
                                pe.wait_ge(norm_done, 2 * p + 2)
                                if p >= 4:
                                    pe.wait_ge(tr_copied, p - 3)
                                for k in range(KC):
                                    for j in range(2):
                                        o = bank(p % 4)[:, k * 256 + j * P:k * 256 + (j + 1) * P]
                                        last = pe.transpose(o, tok[:, 2 * p + j, k * P:(k + 1) * P], ident[:, :])
                                last.then_inc(tr_ready, 1)

                        @block.scalar
                        def _(act):
                            for p in range(tiles // 2):
                                act.wait_ge(tr_ready, p + 1)
                                act.activation(xT[:, :, 256 * p:256 * p + 256],
                                               bank(p % 4).rearrange("p (k n) -> p k n", k=KC),
                                               ACT.Copy).then_inc(tr_copied, 1)

        with nc.Block() as block:
            c0, c1 = sem("const_zeroed"), sem("const_ready")

            @block.gpsimd
            def _(pool):
                pool.memset(ident[:, :], 0.0)
                pool.memset(ones[:, :], 1.0)
                pool.memset(eps_pow[:, :], -0.5)
                pool.memset(half_pow[:, :], 0.5).then_inc(c0, 1)
                pool.wait_ge(c0, 1)
                pool.affine_select(out=ident[:, :], in_=ident[:, :], compare_op=ALU.not_equal, fill=1.0,
                                   base=0, pattern=[[-1, P]], channel_multiplier=1).then_inc(c1, 1)

        layer0(nc, t, out, top, tile, sem, sems, clear, bank, ident, ones, half_pow, normalize, kpad, x2_dram,
               x2T_dram)
        layer1(nc, t, out, top, tile, sem, sems, clear, bank, ident, ones, normalize, x2_dram, x2T_dram)


def layer0(nc, t, out, top, tile, sem, sems, clear, bank, ident, ones, half_pow, normalize, kpad, x2_dram,
           x2T_dram):
    with ExitStack() as L:
        wqkvg = tile(L, "wqkvg", [P, KC, 4 * D])
        wout = tile(L, "wout", [P, KC, D])
        wmoh = tile(L, "wmoh", [P, KC, EXPERTS * QKV])
        wo = tile(L, "wo", [P, EXPERTS * EHD // P, D])
        bq = tile(L, "bq", [P, 4 * KC])
        bg_half = tile(L, "bg_half", [P, KC])
        bout = tile(L, "bout", [P, D])
        toep = tile(L, "toep", [P, HEADS, FIELD])
        cct = tile(L, "cct", [P, KC, D])
        simn = tile(L, "simn", [P, KC, P])
        gate_sig = tile(L, "gate_sig", [P, EXPERTS])
        causal = tile(L, "causal", [P, P])
        dpad = tile(L, "dpad", [P, 4, HEADS, 32])

        with ExitStack() as s:
            freq, damp, phase = (tile(s, n, [HEADS, 1]) for n in ("freq", "damp", "phase"))
            ti = tile(s, "ti", [HEADS, FIELD], I32)
            tf = tile(s, "tf", [HEADS, FIELD])
            ang = tile(s, "ang", [HEADS, FIELD])
            turns = tile(s, "turns", [HEADS, FIELD])
            decay = tile(s, "decay", [HEADS, FIELD])
            krow = tile(s, "krow", [HEADS, 640])
            sm = tile(s, "sm", [HEADS, 8])
            fc = tile(s, "fc", [HEADS, HEADS])
            fcx = tile(s, "fcx", [HEADS, HEADS, HD])
            dm = tile(s, "dm", [P, HD])
            sim = tile(s, "sim", [P, KC, EXPERTS])
            simsq = tile(s, "simsq", [P, KC, EXPERTS])
            simr = tile(s, "simr", [P, EXPERTS])
            gts = tile(s, "gts", [P, EXPERTS])
            small, big, c_zero, c_mask = sem("small_loaded"), sem("big_loaded"), sem("dpad_zero"), sem("mask_ready")
            iota_ready, a1, v1 = sem("iota_ready"), sem("setup_act"), sem("setup_dve")
            sq_ready = sem("squares_ready")
            pw, m1, kst, tl = sem("setup_pow"), sem("setup_mm"), sem("kernel_stored"), sem("toep_loaded")
            with nc.Block() as block:
                @block.sync
                def _(sp):
                    for dst, name in ((freq, "wave_frequency"), (damp, "wave_damping"), (phase, "wave_phase")):
                        sp.dma_start(dst[:, :], t[name].rearrange("(h o) -> h o", o=1)).then_inc(small, 16)
                    sp.dma_start(fc[:, :], t["field_coupling"]).then_inc(small, 16)
                    sp.dma_start(sim[:, :, :], t["sim_matrix"].rearrange("(k p) e -> p k e", p=P)).then_inc(small, 16)
                    sp.dma_start(gts[:, :], t["gates"].partition_broadcast(P)).then_inc(small, 16)
                    with nc.allow_non_contiguous_dma(reason="a bias, once"):
                        sp.dma_start(bq[:, :], t["bqkvg"].rearrange("(m p) -> p m", p=P)).then_inc(small, 16)
                    sp.dma_start(bout[:, :], t["bout"].partition_broadcast(P)).then_inc(big, 16)
                    for dst, name in ((wqkvg, "WqkvgT"), (wout, "WoutT"), (wmoh, "Wmoh"), (wo, "Wo")):
                        sp.dma_start(dst[:, :, :], t[name].rearrange("(k p) n -> p k n", p=P)).then_inc(big, 16)
                    sp.wait_ge(v1, 6)
                    sp.dma_start(kpad, krow[:, :]).then_inc(kst, 16)
                    sp.wait_ge(kst, 16)
                    sp.dma_start(toep[:, :, :], bass.AP(tensor=kpad.tensor, offset=0,
                                                        ap=[[1, P], [640, HEADS], [1, FIELD]])).then_inc(tl, 16)
                    sp.wait_ge(tl, 16)
                    sp.wait_ge(big, 16 * 5)

                @block.gpsimd
                def _(pool):
                    pool.iota(ti[:, :], pattern=[[1, FIELD]], base=0, channel_multiplier=0).then_inc(iota_ready, 1)
                    pool.memset(dpad[:, :, :, :], 0.0)
                    pool.memset(simn[:, :, EXPERTS:P], 0.0)
                    pool.memset(krow[:, :], 0.0)
                    pool.memset(causal[:, :], 0.0).then_inc(c_zero, 1)
                    pool.wait_ge(c_zero, 1)
                    pool.affine_select(out=causal[:, :], in_=causal[:, :], compare_op=ALU.is_ge, fill=MASKED,
                                       base=0, pattern=[[-1, P]], channel_multiplier=1).then_inc(c_mask, 1)
                    pool.wait_ge(v1, 7)
                    pool.tensor_tensor(simr[:, :], simr[:, :], half_pow[:, 0:EXPERTS], ALU.pow).then_inc(pw, 1)

                @block.scalar
                def _(act):
                    act.wait_ge(small, 16 * 7)
                    act.mul(bg_half[:, :], bq[:, 3 * KC:4 * KC], 0.5)
                    act.activation(gate_sig[:, :], gts[:, :], ACT.Tanh, scale=0.5)
                    act.activation(sm[:, 0:1], damp[:, :], ACT.Abs).then_inc(a1, 1)
                    act.wait_ge(a1, 1)
                    act.activation(sm[:, 1:2], sm[:, 0:1], ACT.Exp, scale=-1.0).then_inc(a1, 1)
                    act.wait_ge(a1, 2)
                    act.activation(sm[:, 2:3], sm[:, 1:2], ACT.Ln, bias=1.0).then_inc(a1, 1)
                    act.wait_ge(v1, 2)
                    act.activation(decay[:, :], tf[:, :], ACT.Exp, scale=sm[:, 3:4]).then_inc(a1, 1)
                    act.wait_ge(v1, 3)
                    act.activation(fc[:, :], fc[:, :], ACT.Exp, accum_out=sm[:, 6:7]).then_inc(a1, 1)
                    act.wait_ge(v1, 4)
                    act.activation(ang[:, :], ang[:, :], ACT.Sin).then_inc(a1, 1)

                @block.vector
                def _(dve):
                    dve.wait_ge(iota_ready, 1)
                    dve.tensor_copy(tf[:, :], ti[:, :]).then_inc(v1, 1)
                    dve.wait_ge(small, 16 * 7)
                    dve.wait_ge(a1, 3)
                    dve.scalar_tensor_tensor(sm[:, 3:4], damp[:, :], 0.0, sm[:, 2:3], ALU.max, ALU.add)
                    dve.drain()
                    dve.tensor_scalar(sm[:, 3:4], sm[:, 3:4], -1.0, None, ALU.mult).then_inc(v1, 1)
                    dve.reduce_max(sm[:, 4:5], fc[:, :], axis=AX.X)
                    dve.drain()
                    dve.tensor_scalar(fc[:, :], fc[:, :], sm[:, 4:5], None, ALU.subtract).then_inc(v1, 1)
                    two_pi = 2 * math.pi
                    hi = 6.28125
                    mid = float(round((two_pi - hi) * 2 ** 21) / 2 ** 21)
                    lo = two_pi - hi - mid
                    magic = 1.5 * 2 ** 23
                    dve.tensor_scalar(ang[:, :], tf[:, :], freq[:, :], phase[:, :], ALU.mult, ALU.add)
                    dve.drain()
                    dve.tensor_scalar(turns[:, :], ang[:, :], 1 / two_pi, 0.25, ALU.mult, ALU.add)
                    dve.drain()
                    dve.tensor_scalar(turns[:, :], turns[:, :], magic, None, ALU.add)
                    dve.drain()
                    dve.tensor_scalar(turns[:, :], turns[:, :], magic, None, ALU.subtract)
                    for part in (hi, mid, lo):
                        dve.drain()
                        dve.scalar_tensor_tensor(ang[:, :], turns[:, :], -part, ang[:, :], ALU.mult, ALU.add)
                    dve.drain()
                    dve.tensor_scalar(ang[:, :], ang[:, :], math.pi / 2, 3.1415925, ALU.add, ALU.min)
                    dve.drain()
                    dve.tensor_scalar(ang[:, :], ang[:, :], -3.1415925, None, ALU.max).then_inc(v1, 1)
                    dve.wait_ge(a1, 5)
                    dve.reciprocal(sm[:, 6:7], sm[:, 6:7])
                    dve.drain()
                    dve.tensor_scalar(fc[:, :], fc[:, :], sm[:, 6:7], 0.5, ALU.mult, ALU.mult)
                    dve.drain()
                    dve.tensor_copy(fcx[:, :, :], fc[:, :].unsqueeze(2).broadcast_to([HEADS, HEADS, HD]))\
                       .then_inc(v1, 1)
                    dve.wait_ge(a1, 6)
                    dve.tensor_tensor(decay[:, :], decay[:, :], ang[:, :], ALU.mult)
                    dve.drain()
                    dve.tensor_reduce(sm[:, 7:8], decay[:, :], AX.X, ALU.add, apply_absolute_value=True)
                    dve.drain()
                    dve.tensor_scalar(sm[:, 7:8], sm[:, 7:8], 1e-8, None, ALU.max)
                    dve.drain()
                    dve.reciprocal(sm[:, 7:8], sm[:, 7:8])
                    dve.drain()
                    dve.wait_ge(c_zero, 1)
                    dve.tensor_scalar(krow[:, P - 1:P - 1 + FIELD], decay[:, :], sm[:, 7:8], None, ALU.mult)\
                       .then_inc(v1, 1)
                    dve.tensor_tensor(simsq[:, :, :], sim[:, :, :], sim[:, :, :], ALU.mult)
                    dve.tensor_scalar(gate_sig[:, :], gate_sig[:, :], 0.5, 0.5, ALU.mult, ALU.add)
                    dve.tensor_reduce(dm[:, :], ident[:, :].rearrange("p (j d) -> p d j", d=HD), AX.X, ALU.add)\
                       .then_inc(sq_ready, 1)
                    dve.wait_ge(m1, 1)
                    dve.tensor_copy(simr[:, :], bank(0)[:, 0:EXPERTS]).then_inc(v1, 1)
                    dve.wait_ge(pw, 1)
                    dve.tensor_scalar(simr[:, :], simr[:, :], 1e-12, None, ALU.max)
                    dve.drain()
                    dve.reciprocal(simr[:, :], simr[:, :])
                    dve.drain()
                    for k in range(KC):
                        dve.tensor_tensor(simn[:, k, 0:EXPERTS], sim[:, k, :], simr[:, :], ALU.mult)
                    dve.wait_ge(m1, 2)
                    for k in range(KC):
                        dve.tensor_tensor(cct[:, k, :].rearrange("p (i d) -> p i d", d=HD),
                                          bank(1 + k)[:, 0:HEADS].unsqueeze(2).broadcast_to([P, HEADS, HD]),
                                          dm[:, :].unsqueeze(1).broadcast_to([P, HEADS, HD]), ALU.mult)

                @block.tensor
                def _(pe):
                    pe.wait_ge(sq_ready, 1)
                    for k in range(KC):
                        last = pe.matmul(bank(0)[:, 0:EXPERTS], ones[:, :], simsq[:, k, :],
                                         start=(k == 0), stop=(k == KC - 1))
                    last.then_inc(m1, 1)
                    fr = fcx[:, :, :].rearrange("i j d -> i (j d)")
                    for k in range(KC):
                        last = pe.matmul(bank(1 + k)[:, 0:HEADS], fr[:, k * P:(k + 1) * P],
                                         ident[0:HEADS, 0:HEADS], start=True, stop=True)
                    last.then_inc(m1, 1)

        outside = set(sems)
        tok = tile(L, "tok", [P, TILES, D])
        xT = tile(L, "xT", [P, KC, SEQ])
        with nc.Fori(0, BATCH) as b:
            with ExitStack() as s:
                wave_branch(nc, t, b, s, tile, sem, bank, ident, tok, xT, wqkvg, bq, bg_half, bout, wout, toep,
                            cct, dpad)
            normalize("ln1", tok, xT)
            with ExitStack() as s:
                head_mixture(nc, s, tile, sem, bank, ident, half_pow, tok, xT, wmoh, wo, simn, gate_sig, causal)
            normalize("ln2", tok, xT)
            st = sem("x2_stored")
            with nc.Block() as block:
                @block.sync
                def _(sp):
                    sp.dma_start(x2_dram[b].rearrange("(i p) d -> p i d", p=P), tok[:, :, :]).then_inc(st, 16)
                    sp.dma_start(x2T_dram[b].rearrange("(k p) n -> p k n", p=P), xT[:, :, :]).then_inc(st, 16)
                    sp.wait_ge(st, 32)
            clear(outside)


def wave_branch(nc, t, b, s, tile, sem, bank, ident, tok, xT, wqkvg, bq, bg_half, bout, wout, toep, cct, dpad):
    qg = tile(s, "qg", [P, KC, SEQ])
    dep = tile(s, "dep", [P, KC, SEQ])
    tmp = tile(s, "feat_tmp", [P, 2, 5, CHUNK])
    qf = tile(s, "qf", [P, 2, CHUNK])
    tail = tile(s, "tail", [P, KC])
    conv = tile(s, "conv", [P, KC, FIELD])
    lastg = tile(s, "lastg", [P, KC])
    x_in, proj, feat, used = sem("x_loaded"), sem("proj_ready"), sem("feat_ready"), sem("proj_used")
    units = [(c, n) for c in range(KC) for n in range(CHUNKS)]
    with nc.Block() as block:
        @block.sync
        def _(sp):
            sp.dma_start(xT[:, :, :], t["xT"][b].rearrange("(k p) n -> p k n", p=P)).then_inc(x_in, 16)
            sp.dma_start(tok[:, :, :], t["x"][b].rearrange("(i p) d -> p i d", p=P)).then_inc(sem("tok_in"), 16)
            sp.wait_ge(sem("tok_in"), 16)

        @block.gpsimd
        def _(pool):
            pool.wait_ge(sem("tok_in"), 16)
            pool.tensor_tensor(tok[:, :, :], tok[:, :, :], bout[:, :].unsqueeze(1).broadcast_to([P, TILES, D]),
                               ALU.add)

        @block.tensor
        def _(pe):
            pe.wait_ge(x_in, 16)
            for u, (c, n) in enumerate(units):
                if u >= 2:
                    pe.wait_ge(used, u - 1)
                for kind in range(4):
                    m = kind * KC + c
                    for k in range(KC):
                        last = pe.matmul(bank(4 * (u % 2) + kind), wqkvg[:, k, m * P:(m + 1) * P],
                                         xT[:, k, n * CHUNK:(n + 1) * CHUNK], start=(k == 0), stop=(k == KC - 1))
                last.then_inc(proj, 1)

        @block.scalar
        def _(act):
            for u, (c, n) in enumerate(units):
                act.wait_ge(proj, u + 1)
                if u >= 2:
                    act.wait_ge(used, u - 1)
                w = u % 2
                q, k, g = bank(4 * w), bank(4 * w + 1), bank(4 * w + 3)
                act.activation(tmp[:, w, 0, :], q, ACT.Exp, bias=bq[:, c:c + 1])
                act.activation(tmp[:, w, 1, :], q, ACT.Relu, bias=bq[:, c:c + 1])
                act.activation(tmp[:, w, 2, :], k, ACT.Exp, bias=bq[:, KC + c:KC + c + 1])
                act.activation(tmp[:, w, 3, :], k, ACT.Relu, bias=bq[:, KC + c:KC + c + 1])
                act.activation(tmp[:, w, 4, :], g, ACT.Tanh, bias=bg_half[:, c:c + 1], scale=0.5)\
                   .then_inc(feat, 1)

        @block.vector
        def _(dve):
            for u, (c, n) in enumerate(units):
                w, at = u % 2, slice(n * CHUNK, (n + 1) * CHUNK)
                dve.wait_ge(feat, u + 1)
                dve.drain()
                dve.scalar_tensor_tensor(qf[:, 0, :], tmp[:, w, 0, :], 1.0, tmp[:, w, 1, :], ALU.min, ALU.add)
                dve.scalar_tensor_tensor(qf[:, 1, :], tmp[:, w, 2, :], 1.0, tmp[:, w, 3, :], ALU.min, ALU.add)
                dve.drain()
                dve.scalar_tensor_tensor(qg[:, c, at], tmp[:, w, 4, :], 1.0, qf[:, 0, :], ALU.add, ALU.mult)
                dve.scalar_tensor_tensor(dep[:, c, at], bank(4 * w + 2), bq[:, 2 * KC + c:2 * KC + c + 1],
                                         qf[:, 1, :], ALU.add, ALU.mult).then_inc(used, 1)
            dve.drain()
            for c in range(KC):
                dve.tensor_reduce(tail[:, c:c + 1], dep[:, c, LAST:SEQ], AX.X, ALU.add)
            dve.drain()
            for c in range(KC):
                dve.tensor_copy(dep[:, c, LAST:LAST + 1], tail[:, c:c + 1])
            dve.drain()
            for c in range(KC):
                for sc in range(FIELD // P):
                    cells = dep[:, c, sc * P:(sc + 1) * P]
                    dve.tensor_copy(conv[:, c, sc * P:(sc + 1) * P],
                                    bass.AP(tensor=cells.tensor, offset=cells.offset + P - 1,
                                            ap=[list(cells.ap[0]), [-1, P]]))

    tr, trc, cv, cvc, fcr = (sem(n) for n in ("dep_tr", "dep_copied", "conv_ready", "conv_copied", "field_ready"))
    wd, mm, su = sem("wave_done"), sem("wout_ready"), sem("wout_used")
    with nc.Block() as block:
        @block.tensor
        def _(pe):
            for sc in range(4):
                for c in range(KC):
                    last = pe.transpose(bank(sc)[:, c * P:(c + 1) * P], conv[:, c, sc * P:(sc + 1) * P], ident[:, :])
                last.then_inc(tr, 1)
            pe.wait_ge(trc, 4)
            for c in range(KC):
                for j in range(4):
                    steps = [(c * 8 + 2 * j, 0)] + [(c * 8 + 2 * j + e, sc) for sc in range(1, 4) for e in range(2)]
                    steps += [(c * 8 + 2 * j + 1, 0)]
                    for q, (h, sc) in enumerate(steps):
                        last = pe.matmul(bank(4 + c)[32 * j:32 * j + 32, sc * P:FIELD], dpad[:, sc, h, :],
                                         toep[:, h, 0:FIELD - sc * P], start=(q == 0), stop=(q == len(steps) - 1),
                                         tile_position=(0, 32 * j))
                last.then_inc(cv, 1)
            pe.wait_ge(cvc, KC)
            for m in range(KC):
                for k in range(KC):
                    last = pe.matmul(bank(6 + m), cct[:, k, m * P:(m + 1) * P], conv[:, k, :],
                                     start=(k == 0), stop=(k == KC - 1))
                last.then_inc(fcr, 1)
            pe.wait_ge(wd, 2)
            for i in range(TILES):
                if i >= 8:
                    pe.wait_ge(su, i - 7)
                for k in range(KC):
                    last = pe.matmul(bank(i % 8)[:, 0:D],
                                     qg[:, k, i * P:(i + 1) * P], wout[:, k, :], start=(k == 0), stop=(k == KC - 1))
                last.then_inc(mm, 1)

        @block.scalar
        def _(act):
            for c in range(KC):
                act.wait_ge(cv, c + 1)
                act.activation(conv[:, c, :], bank(4 + c), ACT.Copy).then_inc(cvc, 1)

        @block.vector
        def _(dve):
            for sc in range(4):
                dve.wait_ge(tr, sc + 1)
                src = bank(sc)[:, 0:D].rearrange("p (j e d) -> p j e d", e=2, d=HD)
                dst = dpad[:, sc, :, :].rearrange("p (j e) c -> p j e c", e=2)
                dve.tensor_copy(dst[:, :, 0, 0:HD], src[:, :, 0, :])
                dve.tensor_copy(dst[:, :, 1, HD:2 * HD], src[:, :, 1, :]).then_inc(trc, 1)
            for m in range(KC):
                dve.wait_ge(fcr, m + 1)
                dve.tensor_copy(lastg[:, m:m + 1], bank(6 + m)[:, LAST:LAST + 1])
                dve.tensor_tensor(qg[:, m, 0:LAST + 1], qg[:, m, 0:LAST + 1], bank(6 + m)[:, 0:LAST + 1], ALU.mult)
                dve.drain()
                dve.tensor_scalar(qg[:, m, LAST + 1:SEQ], qg[:, m, LAST + 1:SEQ], lastg[:, m:m + 1], None,
                                  ALU.mult).then_inc(wd, 1)
            for i in range(TILES):
                dve.wait_ge(mm, i + 1)
                dve.tensor_tensor(tok[:, i, :], tok[:, i, :], bank(i % 8)[:, 0:D],
                                  ALU.add).then_inc(su, 1)


def head_mixture(nc, s, tile, sem, bank, ident, half_pow, tok, xT, wmoh, wo, simn, gate_sig, causal):
    rw = tile(s, "rw", [P, TILES, EXPERTS])
    qT = tile(s, "qT", [EHD, SEQ])
    kT = tile(s, "kT", [EHD, SEQ])
    v = tile(s, "v", [P, TILES, P])
    attn = tile(s, "attn", [P, TILES, EHD])
    with ExitStack() as g:
        lg, ex, fb, rep = (tile(g, n, [P, TILES, EXPERTS]) for n in ("lg", "ex", "fb", "rep"))
        top8 = tile(g, "top8", [P, TILES, 8])
        best = tile(g, "best", [P, TILES])
        ss, rs = tile(g, "ss", [P, TILES]), tile(g, "rs", [P, TILES])
        sq = tile(g, "sq", [P, 2, D])
        sr, sp_, lr, le, lx = (sem(n) for n in ("norm_sums", "norm_root", "logits_mm", "logits", "logits_exp"))
        with nc.Block() as block:
            @block.tensor
            def _(pe):
                for i in range(TILES):
                    for k in range(KC):
                        last = pe.matmul(bank(0, 4)[:, i * P:(i + 1) * P], xT[:, k, i * P:(i + 1) * P],
                                         simn[:, k, :], start=(k == 0), stop=(k == KC - 1))
                last.then_inc(lr, 1)

            @block.scalar
            def _(act):
                for i in range(TILES):
                    if i >= 2:
                        act.wait_ge(sr, i - 1)
                    act.activation(sq[:, i % 2, :], tok[:, i, :], ACT.Square, accum_out=ss[:, i:i + 1])\
                       .then_inc(sr, 1)
                act.wait_ge(le, 1)
                act.activation(ex[:, :, :], lg[:, :, :], ACT.Exp).then_inc(lx, 1)

            @block.gpsimd
            def _(pool):
                pool.wait_ge(sr, TILES)
                pool.tensor_tensor(rs[:, :], ss[:, :], half_pow[:, :], ALU.pow).then_inc(sp_, 1)

            @block.vector
            def _(dve):
                def wide(a):
                    return a.unsqueeze(2).broadcast_to([P, TILES, EXPERTS])

                dve.wait_ge(sp_, 1)
                dve.tensor_scalar(rs[:, :], rs[:, :], 1e-12, None, ALU.max)
                dve.drain()
                dve.reciprocal(rs[:, :], rs[:, :])
                dve.drain()
                dve.wait_ge(lr, 1)
                dve.tensor_tensor(lg[:, :, :], bank(0, 4).rearrange("p (i e) -> p i e", e=P)[:, :, 0:EXPERTS],
                                  wide(rs[:, :]), ALU.mult)
                dve.drain()
                dve.tensor_tensor(lg[:, :, :], lg[:, :, :],
                                  gate_sig[:, :].unsqueeze(1).broadcast_to([P, TILES, EXPERTS]), ALU.subtract)\
                   .then_inc(le, 1)
                dve.drain()
                for i in range(TILES):
                    dve.max(top8[:, i, :], lg[:, i, :])
                dve.drain()
                dve.tensor_copy(best[:, :], top8[:, :, 0])
                dve.drain()
                dve.memset(top8[:, :, 2:8], -3e38)
                dve.drain()
                for i in range(TILES):
                    dve.match_replace(rep[:, i, :], top8[:, i, :], lg[:, i, :], 1e30)
                dve.drain()
                dve.tensor_scalar(fb[:, :, :], rep[:, :, :], 1e29, None, ALU.is_gt)
                dve.tensor_scalar(best[:, :], best[:, :], 0.0, None, ALU.is_le)
                dve.drain()
                dve.tensor_tensor(fb[:, :, :], fb[:, :, :], wide(best[:, :]), ALU.mult)
                dve.wait_ge(lx, 1)
                dve.scalar_tensor_tensor(ex[:, :, :], lg[:, :, :], 0.0, ex[:, :, :], ALU.is_gt, ALU.mult)
                dve.drain()
                dve.tensor_tensor(ex[:, :, :], ex[:, :, :], fb[:, :, :], ALU.add)
                dve.drain()
                dve.tensor_reduce(ss[:, :], ex[:, :, :], AX.X, ALU.add)
                dve.drain()
                dve.reciprocal(ss[:, :], ss[:, :])
                dve.drain()
                dve.tensor_tensor(rw[:, :, :], ex[:, :, :], wide(ss[:, :]), ALU.mult)

    with ExitStack() as g:
        acc = tile(g, "acc", [P, 4, QKV])
        acc2 = tile(g, "acc2", [P, 2, QKV])
        qk = tile(g, "qk", [P, 2, 2 * EHD])
        pairs = EXPERTS // 2
        pr, pu, qr, qt, qc = (sem(n) for n in ("pair_ready", "pair_used", "qk_ready", "qk_tr", "qk_copied"))
        with nc.Block() as block:
            @block.gpsimd
            def _(pool):
                pool.memset(v[:, :, EHD:P], 0.0)

            @block.tensor
            def _(pe):
                def flip(i):
                    pe.wait_ge(qr, i + 1)
                    if i >= 2:
                        pe.wait_ge(qc, i - 1)
                    pe.transpose(bank(6 + i % 2)[0:EHD, 0:P], qk[:, i % 2, 0:EHD], ident[:, :])
                    pe.transpose(bank(6 + i % 2)[0:EHD, P:2 * P], qk[:, i % 2, EHD:2 * EHD], ident[:, :])\
                      .then_inc(qt, 1)

                for i in range(TILES):
                    for j in range(pairs):
                        n = i * pairs + j
                        if n >= 6:
                            pe.wait_ge(pu, n - 5)
                        for k in range(KC):
                            last = pe.matmul(bank(n % 6)[:, 0:2 * QKV], xT[:, k, i * P:(i + 1) * P],
                                             wmoh[:, k, 2 * j * QKV:(2 * j + 2) * QKV],
                                             start=(k == 0), stop=(k == KC - 1))
                        last.then_inc(pr, 1)
                    if i:
                        flip(i - 1)
                flip(TILES - 1)

            @block.vector
            def _(dve):
                for i in range(TILES):
                    for e in range(EXPERTS):
                        n = i * pairs + e // 2
                        if e % 2 == 0:
                            dve.wait_ge(pr, n + 1)
                        if e % 4 == 0:
                            dve.drain()
                        src = bank(n % 6)[:, (e % 2) * QKV:(e % 2 + 1) * QKV]
                        if e < 4:
                            op = dve.tensor_scalar(acc[:, e, :], src, rw[:, i, e:e + 1], None, ALU.mult)
                        else:
                            op = dve.scalar_tensor_tensor(acc[:, e % 4, :], src, rw[:, i, e:e + 1], acc[:, e % 4, :],
                                                          ALU.mult, ALU.add)
                        if e % 2:
                            op.then_inc(pu, 1)
                    dve.drain()
                    dve.tensor_tensor(acc2[:, :, :], acc[:, 0:2, :], acc[:, 2:4, :], ALU.add)
                    dve.drain()
                    if i >= 2:
                        dve.wait_ge(qt, i - 1)
                    dve.tensor_tensor(v[:, i, 0:EHD], acc2[:, 0, 2 * EHD:QKV], acc2[:, 1, 2 * EHD:QKV], ALU.add)
                    dve.tensor_tensor(qk[:, i % 2, :], acc2[:, 0, 0:2 * EHD], acc2[:, 1, 0:2 * EHD], ALU.add)\
                       .then_inc(qr, 1)

            @block.scalar
            def _(act):
                for i in range(TILES):
                    act.wait_ge(qt, i + 1)
                    act.activation(qT[:, i * P:(i + 1) * P], bank(6 + i % 2)[0:EHD, 0:P], ACT.Copy)
                    act.activation(kT[:, i * P:(i + 1) * P], bank(6 + i % 2)[0:EHD, P:2 * P], ACT.Copy)\
                       .then_inc(qc, 1)

    with ExitStack() as g:
        prob = tile(g, "prob", [P, 2, SEQ])
        probT = tile(g, "probT", [P, 2, CHUNK])
        mx, den = tile(g, "mx", [P, TILES]), tile(g, "den", [P, TILES])
        scale = 1.0 / math.sqrt(EHD)
        sr, mr, pr, tr, tc, pv, orr, ou = (sem(n) for n in (
            "scores_ready", "max_ready", "probs_ready", "probs_tr", "probs_copied", "pv_done", "attn_ready",
            "attn_used"))
        groups = []
        for i in range(TILES):
            groups += [(i, a, min(4, i + 1 - a)) for a in range(0, i + 1, 4)]
        first = {i: min(n for n, x in enumerate(groups) if x[0] == i) for i in range(TILES)}
        first[TILES] = len(groups)
        with nc.Block() as block:
            @block.tensor
            def _(pe):
                def scores(i):
                    width = (i + 1) * P
                    for a in range(0, width, CHUNK):
                        z = min(width, a + CHUNK)
                        last = pe.matmul(bank(0, 4)[:, a:z], qT[:, i * P:(i + 1) * P], kT[:, a:z],
                                         start=True, stop=True)
                    last.then_inc(sr, 1)

                def values(n):
                    i, a, m = groups[n]
                    pe.wait_ge(tc, n + 1)
                    if a == 0 and i >= 2:
                        pe.wait_ge(ou, i - 1)
                    for j in range(m):
                        last = pe.matmul(bank(6 + i % 2)[:, 0:P], probT[:, n % 2, j * P:(j + 1) * P],
                                         v[:, a + j, :], start=(a + j == 0), stop=(a + j == i))
                    last.then_inc(pv, 1)

                scores(0)
                for i in range(TILES):
                    pe.wait_ge(pr, i + 1)
                    if i + 1 < TILES:
                        scores(i + 1)
                    for n in range(first[i], first[i + 1]):
                        _, a, m = groups[n]
                        if n >= 2:
                            pe.wait_ge(tc, n - 1)
                        for j in range(m):
                            last = pe.transpose(bank(4 + n % 2)[:, j * P:(j + 1) * P],
                                                prob[:, i % 2, (a + j) * P:(a + j + 1) * P], ident[:, :])
                        last.then_inc(tr, 1)
                        if n > first[i]:
                            values(n - 1)
                    values(first[i + 1] - 1)

            @block.vector
            def _(dve):
                def maximum(i):
                    width = (i + 1) * P
                    dve.wait_ge(sr, i + 1)
                    dve.tensor_tensor(bank(0, 4)[:, i * P:width], bank(0, 4)[:, i * P:width], causal[:, :], ALU.add)
                    dve.drain()
                    dve.reduce_max(mx[:, i:i + 1], bank(0, 4)[:, 0:width], axis=AX.X)
                    dve.drain()
                    dve.tensor_scalar(mx[:, i:i + 1], mx[:, i:i + 1], -scale, None, ALU.mult).then_inc(mr, 1)

                maximum(0)
                for i in range(TILES):
                    if i + 1 < TILES:
                        maximum(i + 1)
                    for n in range(first[i], first[i + 1]):
                        m = groups[n][2]
                        dve.wait_ge(tr, n + 1)
                        if n >= 2:
                            dve.wait_ge(pv, n - 1)
                        dve.tensor_copy(probT[:, n % 2, 0:m * P], bank(4 + n % 2)[:, 0:m * P]).then_inc(tc, 1)
                    dve.reciprocal(den[:, i:i + 1], den[:, i:i + 1])
                    dve.drain()
                    dve.wait_ge(pv, first[i + 1])
                    dve.tensor_scalar(attn[:, i, :], bank(6 + i % 2)[:, 0:EHD], den[:, i:i + 1], None, ALU.mult)\
                       .then_inc(ou, 1)

            @block.scalar
            def _(act):
                for i in range(TILES):
                    width = (i + 1) * P
                    act.wait_ge(mr, i + 1)
                    act.activation(prob[:, i % 2, 0:width], bank(0, 4)[:, 0:width], ACT.Exp, bias=mx[:, i:i + 1],
                                   scale=scale, accum_out=den[:, i:i + 1]).then_inc(pr, 1)

    with ExitStack() as g:
        mix = tile(g, "mix", [P, 2, EXPERTS, EHD])
        mixT = tile(g, "mixT", [P, 2, 8, P])
        mr, tr, tc, yr, yu = (sem(n) for n in ("mix_ready", "mix_tr", "mix_copied", "o_ready", "o_used"))
        with nc.Block() as block:
            @block.tensor
            def _(pe):
                def project(i):
                    pe.wait_ge(tc, 2 * i + 2)
                    if i >= 2:
                        pe.wait_ge(yu, i - 1)
                    for k in range(8):
                        last = pe.matmul(bank(4 + i % 2)[:, 0:D], mixT[:, i % 2, k, :], wo[:, k, :],
                                         start=(k == 0), stop=(k == 7))
                    last.then_inc(yr, 1)

                for i in range(TILES):
                    pe.wait_ge(mr, i + 1)
                    if i >= 2:
                        pe.wait_ge(tc, 2 * i - 2)
                    flat = mix[:, i % 2, :, :].rearrange("p e d -> p (e d)")
                    for h in range(2):
                        for k in range(4 * h, 4 * h + 4):
                            last = pe.transpose(bank(2 * (i % 2) + h)[:, (k % 4) * P:(k % 4 + 1) * P],
                                                flat[:, k * P:(k + 1) * P], ident[:, :])
                        last.then_inc(tr, 1)
                    if i:
                        project(i - 1)
                project(TILES - 1)

            @block.vector
            def _(dve):
                def add(i):
                    dve.wait_ge(yr, i + 1)
                    dve.tensor_tensor(tok[:, i, :], tok[:, i, :], bank(4 + i % 2)[:, 0:D], ALU.add).then_inc(yu, 1)

                for i in range(TILES):
                    if i >= 2:
                        dve.wait_ge(tr, 2 * i - 2)
                    dve.tensor_tensor(mix[:, i % 2, :, :], attn[:, i, :].unsqueeze(1).broadcast_to([P, EXPERTS, EHD]),
                                      rw[:, i, :].unsqueeze(2).broadcast_to([P, EXPERTS, EHD]), ALU.mult)\
                       .then_inc(mr, 1)
                    if i:
                        add(i - 1)
                add(TILES - 1)

            @block.scalar
            def _(act):
                for i in range(TILES):
                    for h in range(2):
                        act.wait_ge(tr, 2 * i + h + 1)
                        if i >= 2:
                            act.wait_ge(yr, i - 1)
                        act.activation(mixT[:, i % 2, 4 * h:4 * h + 4, :],
                                       bank(2 * (i % 2) + h).rearrange("p (k n) -> p k n", k=4),
                                       ACT.Copy).then_inc(tc, 1)


def layer1(nc, t, out, top, tile, sem, sems, clear, bank, ident, ones, normalize, x2_dram, x2T_dram):
    with ExitStack() as L:
        tok = tile(L, "tok1", [P, TILES, D])
        with ExitStack() as W:
            w_in = tile(W, "w_in", [P, KC, 2 * INNER])
            w_dt = tile(W, "w_dt", [P, KI, INNER])
            w_x = tile(W, "w_x", [P, KI, 2 * STATE])
            w_out = tile(W, "w_out", [P, KI, D])
            cw = tile(W, "cw", [P, KI, TAPS])
            cb, bdt, dskip = (tile(W, n, [P, KI]) for n in ("cb", "bdt", "dskip"))
            a_neg = tile(W, "a_neg", [P, STATE])
            pick = tile(W, "pick", [P, 2 * STATE, P], BF16)
            bc3 = tile(W, "bc3", [P, SEQ], BF16)
            zero_bf = tile(W, "zero_bf", [P, P], BF16)
            ld, pz, pk, av = sem("l1_loaded"), sem("pick_zeroed"), sem("pick_ready"), sem("a_ready")
            with nc.Block() as block:
                @block.sync
                def _(sp):
                    for dst, name in ((w_in, "W_in"), (w_dt, "W_dt"), (w_x, "W_x"), (w_out, "W_out")):
                        sp.dma_start(dst[:, :, :], t[name].rearrange("(k p) n -> p k n", p=P)).then_inc(ld, 16)
                    with nc.allow_non_contiguous_dma(reason="vectors, once"):
                        sp.dma_start(cw[:, :, :], t["conv_w"].rearrange("(m p) j -> p m j", p=P)).then_inc(ld, 16)
                        for dst, name in ((cb, "conv_b"), (bdt, "b_dt"), (dskip, "D")):
                            sp.dma_start(dst[:, :], t[name].rearrange("(m p) -> p m", p=P)).then_inc(ld, 16)
                    sp.dma_start(a_neg[:, :], t["A_log"].partition_broadcast(P)).then_inc(ld, 16)

                @block.gpsimd
                def _(pool):
                    pool.memset(pick[:, :, :], 0.0)
                    pool.memset(zero_bf[:, :], 0.0)
                    pool.memset(bc3[:, :], 0.0).then_inc(pz, 1)
                    for part in range(3):
                        pool.wait_ge(pz, part + 1)
                        pool.affine_select(out=pick[:, :, :], in_=pick[:, :, :], compare_op=ALU.not_equal,
                                           fill=1.0, base=-32 * part, pattern=[[-1, 2 * STATE], [0, P]],
                                           channel_multiplier=1).then_inc(pz, 1)

                @block.scalar
                def _(act):
                    act.wait_ge(ld, 16 * 9)
                    act.activation(a_neg[:, :], a_neg[:, :], ACT.Exp).then_inc(av, 1)
                    act.mul(cw[:, :, :], cw[:, :, :], 0.5)
                    act.mul(cb[:, :], cb[:, :], 0.5)
                    act.mul(w_out[:, :, :], w_out[:, :, :], 0.5)

                @block.vector
                def _(dve):
                    dve.wait_ge(av, 1)
                    dve.tensor_scalar(a_neg[:, :], a_neg[:, :], -1.0, None, ALU.mult)

            outside = set(sems)
            with nc.Fori(0, BATCH) as it:
                b = BATCH - 1 - it
                with ExitStack() as s:
                    state_space(nc, b, s, tile, sem, bank, ident, tok, w_in, w_dt, w_x, w_out, cw, cb, bdt, dskip,
                                a_neg, pick, bc3, zero_bf, x2_dram, x2T_dram)
                normalize("ln3", tok, None)
                with ExitStack() as s:
                    fin = tile(s, "fin", [P, TILES, D])
                    with nc.Block() as block:
                        @block.scalar
                        def _(act):
                            act.activation(fin[:, :, :], tok[:, :, :], ACT.Copy)
                    normalize("ln4", fin, None)
                    st = sem("out_stored")
                    with nc.Block() as block:
                        @block.sync
                        def _(sp):
                            sp.dma_start(out[b].rearrange("(i p) d -> p i d", p=P), fin[:, :, :]).then_inc(st, 16)
                            sp.wait_ge(st, 16)
                clear(outside)
        with ExitStack() as s:
            experts(nc, t, out, s, tile, sem, bank, ident, ones, tok, normalize)


def state_space(nc, b, s, tile, sem, bank, ident, tok, w_in, w_dt, w_x, w_out, cw, cb, bdt, dskip, a_neg, pick, bc3,
                zero_bf, x2_dram, x2T_dram):
    xT = tile(s, "x2T", [P, KC, SEQ])
    u = tile(s, "u", [P, KI, SEQ])
    with ExitStack() as g:
        xin = tile(g, "xin", [P, 2, TAPS - 1 + SEQ])
        xc = tile(g, "xc", [P, 2, SEQ])
        th = tile(g, "th", [P, 2, SEQ])
        x_in, pr, cp, cv, tr, uu, z = (sem(n) for n in (
            "x2_loaded", "in_proj", "in_copied", "conv_done", "tanh_ready", "u_ready", "pad_zeroed"))
        with nc.Block() as block:
            @block.sync
            def _(sp):
                sp.dma_start(xT[:, :, :], x2T_dram[b].rearrange("(k p) n -> p k n", p=P)).then_inc(x_in, 16)
                sp.dma_start(tok[:, :, :], x2_dram[b].rearrange("(i p) d -> p i d", p=P))\
                  .then_inc(sem("tok2_in"), 16)
                sp.wait_ge(sem("tok2_in"), 16)

            @block.gpsimd
            def _(pool):
                pool.memset(xin[:, :, 0:TAPS - 1], 0.0).then_inc(z, 1)

            @block.tensor
            def _(pe):
                pe.wait_ge(x_in, 16)
                for m in range(KI):
                    if m >= 2:
                        pe.wait_ge(cp, m - 1)
                    for n in range(CHUNKS):
                        for k in range(KC):
                            last = pe.matmul(bank(4 * (m % 2) + n), w_in[:, k, m * P:(m + 1) * P],
                                             xT[:, k, n * CHUNK:(n + 1) * CHUNK], start=(k == 0), stop=(k == KC - 1))
                    last.then_inc(pr, 1)

            @block.scalar
            def _(act):
                def tanh(m):
                    act.wait_ge(cv, m + 1)
                    if m >= 2:
                        act.wait_ge(uu, m - 1)
                    act.activation(th[:, m % 2, :], xc[:, m % 2, :], ACT.Tanh).then_inc(tr, 1)

                for m in range(KI):
                    act.wait_ge(pr, m + 1)
                    if m >= 2:
                        act.wait_ge(uu, m - 1)
                    act.activation(xc[:, m % 2, :], bank(4 * (m % 2), 4), ACT.Identity,
                                   bias=cb[:, m:m + 1], scale=cw[:, m, TAPS - 1:TAPS])
                    act.activation(xin[:, m % 2, TAPS - 1:], bank(4 * (m % 2), 4), ACT.Copy).then_inc(cp, 1)
                    if m:
                        tanh(m - 1)
                tanh(KI - 1)

            @block.vector
            def _(dve):
                dve.wait_ge(z, 1)

                def silu(m):
                    dve.wait_ge(tr, m + 1)
                    dve.scalar_tensor_tensor(u[:, m, :], th[:, m % 2, :], 1.0, xc[:, m % 2, :], ALU.add, ALU.mult)\
                       .then_inc(uu, 1)

                for m in range(KI):
                    dve.wait_ge(cp, m + 1)
                    for j in range(TAPS - 1):
                        op = dve.scalar_tensor_tensor(xc[:, m % 2, :], xin[:, m % 2, j:j + SEQ], cw[:, m, j:j + 1],
                                                      xc[:, m % 2, :], ALU.mult, ALU.add)
                        if j < TAPS - 2:
                            dve.drain()
                    op.then_inc(cv, 1)
                    if m:
                        silu(m - 1)
                silu(KI - 1)

    dt = tile(s, "dt", [P, KI, SEQ])
    dtu = tile(s, "dtu", [P, KI, SEQ])
    with ExitStack() as g:
        bc = tile(g, "bc", [2 * STATE, SEQ])
        mid = tile(g, "mid", [2 * STATE, SEQ], BF16)
        DT = [4, 0, 4, 0]
        bcr, bcc, dr, mn, ln, du = (sem(n) for n in ("bc_ready", "bc_copied", "dt_mm", "dt_min", "dt_ln", "dt_used"))
        with nc.Block() as block:
            @block.tensor
            def _(pe):
                for n in range(CHUNKS):
                    for k in range(KI):
                        last = pe.matmul(bank(n)[0:2 * STATE, :], w_x[:, k, :], u[:, k, n * CHUNK:(n + 1) * CHUNK],
                                         start=(k == 0), stop=(k == KI - 1))
                last.then_inc(bcr, 1)
                for m in range(KI):
                    if m == 1:
                        pe.wait_ge(bcc, 1)
                    if m >= 2:
                        pe.wait_ge(du, m - 1)
                    for n in range(CHUNKS):
                        for k in range(KI):
                            last = pe.matmul(bank(DT[m] + n), w_dt[:, k, m * P:(m + 1) * P],
                                             u[:, k, n * CHUNK:(n + 1) * CHUNK], start=(k == 0), stop=(k == KI - 1))
                    last.then_inc(dr, 1)

            @block.scalar
            def _(act):
                act.wait_ge(bcr, 1)
                act.activation(bc[:, :], bank(0, 4)[0:2 * STATE, :], ACT.Copy).then_inc(bcc, 1)
                for m in range(KI):
                    act.wait_ge(mn, m + 1)
                    act.activation(dtu[:, m, :], dtu[:, m, :], ACT.Exp).then_inc(ln, 1)
                    act.wait_ge(ln, 2 * m + 1)
                    act.activation(dtu[:, m, :], dtu[:, m, :], ACT.Ln, bias=1.0).then_inc(ln, 1)

            @block.vector
            def _(dve):
                dve.wait_ge(bcc, 1)
                dve.tensor_copy(bc3[0:32, :], bc[:, :])
                dve.drain()
                dve.tensor_tensor(bc[:, :], bc[:, :], bc3[0:32, :], ALU.subtract)
                dve.drain()
                dve.tensor_copy(mid[:, :], bc[:, :])
                dve.drain()
                dve.tensor_copy(bc3[32:64, :], mid[:, :])
                dve.tensor_tensor(bc3[64:96, :], bc[:, :], mid[:, :], ALU.subtract)
                def clip(m):
                    dve.wait_ge(dr, m + 1)
                    dve.tensor_scalar(dtu[:, m, :], bank(DT[m], 4), bdt[:, m:m + 1], 40.0, ALU.add, ALU.min)\
                       .then_inc(mn, 1)

                def softplus(m):
                    dve.wait_ge(ln, 2 * m + 2)
                    dve.scalar_tensor_tensor(dt[:, m, :], bank(DT[m], 4), bdt[:, m:m + 1], dtu[:, m, :],
                                             ALU.add, ALU.max).then_inc(du, 1)
                    dve.drain()
                    dve.tensor_tensor(dtu[:, m, :], dt[:, m, :], u[:, m, :], ALU.mult)

                clip(0)
                for m in range(1, KI):
                    softplus(m - 1)
                    clip(m)
                softplus(KI - 1)

    with ExitStack() as g:
        da, bb, h, hc = (tile(g, n, [P, 2, HALF]) for n in ("da", "bb", "h", "hc"))
        c_sb = tile(g, "c_sb", [P, HALF])
        state = tile(g, "state", [P, KI, STATE])
        br, cr, cc, yz, yd = (sem(n) for n in (
            "b_spread", "c_spread", "c_copied", "y_ready", "y_done"))
        bd = [sem(f"b_times_u{d}") for d in range(2)]
        sd = [sem(f"scan_done{d}") for d in range(2)]
        ar = [sem(f"decay_ready{d}") for d in range(2)]
        sv = [sem(f"state_free{d}") for d in range(2)]
        hr = [sem(f"product{d}") for d in range(2)]
        yr = [sem(f"product_free{d}") for d in range(2)]
        Y, BS, CS = 0, 4, 6
        rounds = [(pair, half) for pair in range(KI // 2) for half in range(2)]
        N = STATE
        with nc.Block() as block:
            @block.tensor
            def _(pe):
                for d in range(2):
                    pe.sem_inc(yr[d], 1)
                for g_, (pair, half) in enumerate(rounds):
                    o = g_ * N

                    def spread(row, where, ready):
                        for j in range(2):
                            last = pe.matmul(bank(where + j), pick[:, row, :],
                                             bc3[:, half * HALF + j * CHUNK:half * HALF + (j + 1) * CHUNK],
                                             start=True, stop=True)
                        last.then_inc(ready, 1)

                    def next_b(n):
                        pe.wait_ge(bd[0], n + o)
                        spread(n, BS, br)

                    def next_c(n):
                        pe.wait_ge(cc, n + o)
                        pe.wait_ge(hr[0], n + (o + 1))
                        spread(n + N, CS, cr)

                    def gather(n, d):
                        pe.wait_ge(hr[d], n + (o + 2))
                        for j in range(2):
                            last = pe.matmul(bank(Y + 2 * d + j), ident[:, :], hc[:, d, j * CHUNK:(j + 1) * CHUNK],
                                             start=False, stop=False)
                        last.then_inc(yr[d], 1)

                    if g_:
                        pe.wait_ge(yd, g_)
                    for j in range(4):
                        pe.matmul(bank(Y + j), zero_bf[:, :], bc3[:, 0:CHUNK], start=True, stop=False)
                    spread(0, BS, br)
                    spread(N, CS, cr)
                    next_b(1)
                    with pe.Fori(0, N - 2) as n:
                        next_c(n + 1)
                        gather(n, 0)
                        next_b(n + 2)
                        gather(n, 1)
                    next_c(N - 1)
                    for n in (N - 2, N - 1):
                        gather(n, 0)
                        gather(n, 1)
                    for j in range(4):
                        last = pe.matmul(bank(Y + j), zero_bf[:, :], bc3[:, 0:CHUNK], start=False, stop=True)
                    last.then_inc(yz, 1)

            @block.scalar
            def _(act):
                for d in range(2):
                    act.sem_inc(sv[d], 1)
                for g_, (pair, half) in enumerate(rounds):
                    o = g_ * N

                    def decay(n, d):
                        act.activation(da[:, d, :], dt[:, 2 * pair + d, half * HALF:(half + 1) * HALF], ACT.Exp,
                                       scale=a_neg[:, bass.ds(n, 1)]).then_inc(ar[d], 1)

                    def save(n, d):
                        act.wait_ge(sd[d], n + (o + 1))
                        act.activation(state[:, 2 * pair + d, bass.ds(n, 1)], h[:, d, HALF - 1:HALF], ACT.Copy)\
                           .then_inc(sv[d], 1)

                    def copy_c(n):
                        act.wait_ge(cr, n + (o + 1))
                        act.wait_ge(hr[1], n + (o + 1))
                        act.activation(c_sb[:, :], bank(CS, 2), ACT.Copy).then_inc(cc, 1)

                    decay(0, 1)
                    decay(0, 0)
                    copy_c(0)
                    with act.Fori(0, N - 1) as n:
                        for d in (1, 0):
                            save(n, d)
                            decay(n + 1, d)
                        copy_c(n + 1)
                    save(N - 1, 0)
                    save(N - 1, 1)

            @block.gpsimd
            def _(pool):
                for d in range(2):
                    pool.sem_inc(hr[d], 1)
                for g_ in range(len(rounds)):
                    o = g_ * N
                    with pool.Fori(0, N) as n:
                        now = pool.snap(n + (o + 1))
                        pool.wait_ge(cc, now)
                        pool.wait_ge(sd[1], now)
                        pool.wait_ge(yr[1], now)
                        pool.tensor_tensor(hc[:, 1, :], h[:, 1, :], c_sb[:, :], ALU.mult).then_inc(hr[1], 1)

            @block.vector
            def _(dve):
                for g_, (pair, half) in enumerate(rounds):
                    o = g_ * N
                    at = slice(half * HALF, (half + 1) * HALF)

                    def spread_u(now, d):
                        dve.wait_ge(br, now)
                        return dve.tensor_tensor(bb[:, d, :], dtu[:, 2 * pair + d, at], bank(BS, 2), ALU.mult)

                    def scan(n, now, d):
                        dve.wait_ge(ar[d], now)
                        dve.wait_ge(sv[d], now)
                        dve.wait_ge(bd[d], now)
                        dve.wait_ge(hr[d], now)
                        first = 0.0 if half == 0 else state[:, 2 * pair + d, bass.ds(n, 1)]
                        dve.tensor_tensor_scan(h[:, d, :], da[:, d, :], bb[:, d, :], first, ALU.mult, ALU.add)\
                           .then_inc(sd[d], 1)

                    def product(now):
                        dve.wait_ge(cc, now)
                        dve.wait_ge(yr[0], now)
                        dve.wait_ge(sd[0], now)
                        dve.tensor_tensor(hc[:, 0, :], h[:, 0, :], bank(CS, 2), ALU.mult).then_inc(hr[0], 1)

                    spread_u(o + 1, 1).then_inc(bd[1], 1)
                    spread_u(o + 1, 0).then_inc(bd[0], 1)
                    with dve.Fori(0, N - 1) as n:
                        now = dve.snap(n + (o + 1))
                        after = dve.snap(n + (o + 2))
                        scan(n, now, 1)
                        scan(n, now, 0)
                        dve.wait_ge(sd[1], now)
                        spread_u(after, 1).then_inc(bd[1], 1)
                        product(now)
                        spread_u(after, 0).then_inc(bd[0], 1)
                    scan(N - 1, o + N, 1)
                    scan(N - 1, o + N, 0)
                    product(o + N)
                    dve.wait_ge(yz, g_ + 1)
                    for d in range(2):
                        m = 2 * pair + d
                        op = dve.scalar_tensor_tensor(dt[:, m, at], u[:, m, at], dskip[:, m:m + 1],
                                                      bank(Y + 2 * d, 2), ALU.mult, ALU.add)
                    op.then_inc(yd, 1)

    with ExitStack() as g:
        th = tile(g, "thz", [P, 2, SEQ])
        pr, tr, zu, mm, su = (sem(n) for n in ("z_proj", "z_tanh", "z_used", "out_mm", "out_used"))
        with nc.Block() as block:
            @block.tensor
            def _(pe):
                for m in range(KI):
                    if m >= 2:
                        pe.wait_ge(zu, m - 1)
                    for n in range(CHUNKS):
                        for k in range(KC):
                            last = pe.matmul(bank(4 * (m % 2) + n), w_in[:, k, INNER + m * P:INNER + (m + 1) * P],
                                             xT[:, k, n * CHUNK:(n + 1) * CHUNK], start=(k == 0), stop=(k == KC - 1))
                    last.then_inc(pr, 1)
                pe.wait_ge(zu, KI)
                for i in range(TILES):
                    if i >= 8:
                        pe.wait_ge(su, i - 7)
                    for k in range(KI):
                        last = pe.matmul(bank(i % 8)[:, 0:D], dt[:, k, i * P:(i + 1) * P], w_out[:, k, :],
                                         start=(k == 0), stop=(k == KI - 1))
                    last.then_inc(mm, 1)

            @block.scalar
            def _(act):
                for m in range(KI):
                    act.wait_ge(pr, m + 1)
                    if m >= 2:
                        act.wait_ge(zu, m - 1)
                    act.activation(th[:, m % 2, :], bank(4 * (m % 2), 4), ACT.Tanh, scale=0.5).then_inc(tr, 1)

            @block.vector
            def _(dve):
                for m in range(KI):
                    dve.wait_ge(tr, m + 1)
                    dve.scalar_tensor_tensor(th[:, m % 2, :], th[:, m % 2, :], 1.0, bank(4 * (m % 2), 4),
                                             ALU.add, ALU.mult)
                    dve.drain()
                    dve.tensor_tensor(dt[:, m, :], dt[:, m, :], th[:, m % 2, :], ALU.mult).then_inc(zu, 1)
                for i in range(TILES):
                    dve.wait_ge(mm, i + 1)
                    dve.tensor_tensor(tok[:, i, :], tok[:, i, :], bank(i % 8)[:, 0:D], ALU.add).then_inc(su, 1)


def experts(nc, t, out, s, tile, sem, bank, ident, ones, tok, normalize):
    MT = MOE_TOK // P
    gup = tile(s, "gup", [P, KC, MOE_E, 2, MOE_F])
    down = tile(s, "down", [P, MOE_F // P, MOE_E, D])
    gub = tile(s, "gub", [P, MOE_E, 2, KC])
    db = tile(s, "db", [1, MOE_E, D])
    two = tile(s, "two", [1, P])
    ri = tile(s, "ri", [P, MT, 2], I32)
    rif = tile(s, "rif", [P, MT, 2])
    rwt = tile(s, "rwt", [P, MT, MOE_E])
    cnt = tile(s, "cnt", [P, MT, MOE_E])
    x3T = tile(s, "x3T", [P, KC, MOE_TOK])
    gate = tile(s, "gate", [P, 2, KC, MOE_TOK])
    up = tile(s, "up", [P, 2, KC, MOE_TOK])
    th = tile(s, "moe_th", [P, 2, KC, MOE_TOK])
    inter = tile(s, "inter", [P, 2, KC, MOE_TOK])
    ld, tr, tc = sem("moe_loaded"), sem("x3_tr"), sem("x3_copied")
    gr, gm, gt, iu, ir, dr, du, rt = (sem(n) for n in (
        "gu_ready", "gate_clipped", "gate_tanh", "gu_used", "inter_ready", "down_ready", "down_used", "route_ready"))
    with nc.Block() as block:
        @block.sync
        def _(sp):
            for k in range(KC):
                rows = slice(k * P, (k + 1) * P)
                sp.dma_start(gup[:, k, :, :, :].rearrange("p e g f -> p e (g f)"),
                             t["gate_up"][:, rows, :].rearrange("e p n -> p e n")).then_inc(ld, 16)
                sp.dma_start(down[:, k, :, :], t["down"][:, rows, :].rearrange("e p n -> p e n")).then_inc(ld, 16)
            with nc.allow_non_contiguous_dma(reason="biases, once"):
                sp.dma_start(gub[:, :, :, :].rearrange("p e g k -> p (e g k)"),
                             t["gate_up_bias"].rearrange("(x p) -> p x", p=P)).then_inc(ld, 16)
            sp.dma_start(db[:, :, :], t["down_bias"].rearrange("(o e) d -> o e d", o=1)).then_inc(ld, 16)
            sp.dma_start(ri[:, :, :], t["router_indices"].rearrange("(i p) k -> p i k", p=P)).then_inc(ld, 16)
            sp.dma_start(rwt[:, :, :], t["routing_weights"].rearrange("(i p) e -> p i e", p=P)).then_inc(ld, 16)

        @block.gpsimd
        def _(pool):
            pool.memset(two[:, :], 2.0).then_inc(sem("two_ready"), 1)

        @block.tensor
        def _(pe):
            for k in range(KC):
                for i in range(MT):
                    last = pe.transpose(bank(k)[:, i * P:(i + 1) * P], tok[:, i, k * P:(k + 1) * P], ident[:, :])
            last.then_inc(tr, 1)
            pe.wait_ge(tc, 1)
            pe.wait_ge(ld, 16 * 8)
            pe.wait_ge(sem("two_ready"), 1)

            def down_proj(e):
                pe.wait_ge(ir, e + 1)
                for i in range(MT):
                    if e >= 1:
                        pe.wait_ge(du, MT * (e - 1) + i + 1)
                    o = bank(4 + i)[:, 0:D]
                    for k in range(KC):
                        pe.matmul(o, inter[:, e % 2, k, i * P:(i + 1) * P], down[:, k, e, :], start=(k == 0),
                                  stop=False)
                    pe.matmul(o, two[:, :], db[:, e, :], start=False, stop=True).then_inc(dr, 1)

            for e in range(MOE_E):
                if e >= 1:
                    pe.wait_ge(iu, e)
                for g in range(2):
                    for m in range(KC):
                        for k in range(KC):
                            last = pe.matmul(bank(2 * g + m), gup[:, k, e, g, m * P:(m + 1) * P], x3T[:, k, :],
                                             start=(k == 0), stop=(k == KC - 1))
                last.then_inc(gr, 1)
                if e:
                    down_proj(e - 1)
            down_proj(MOE_E - 1)

        @block.scalar
        def _(act):
            act.wait_ge(tr, 1)
            act.activation(x3T[:, :, :], bank(0, 2).rearrange("p (k n) -> p k n", k=KC), ACT.Copy).then_inc(tc, 1)
            for e in range(MOE_E):
                act.wait_ge(gm, e + 1)
                act.activation(th[:, e % 2, :, :], gate[:, e % 2, :, :], ACT.Tanh, scale=ALPHA / 2).then_inc(gt, 1)

        @block.vector
        def _(dve):
            dve.wait_ge(ld, 16 * 8)
            dve.tensor_copy(rif[:, :, :], ri[:, :, :])
            dve.drain()
            for e in range(MOE_E):
                dve.tensor_scalar(gate[:, 0, 0, 2 * MT * e:2 * MT * (e + 1)], rif[:, :, :].rearrange("p i k -> p (i k)"),
                                  float(e), None, ALU.is_equal)
            dve.drain()
            for e in range(MOE_E):
                dve.tensor_reduce(cnt[:, :, e], gate[:, 0, 0, 2 * MT * e:2 * MT * (e + 1)]
                                  .rearrange("p (i k) -> p i k", k=2), AX.X, ALU.add)
            dve.drain()
            dve.scalar_tensor_tensor(cnt[:, :, :], cnt[:, :, :], 0.5, rwt[:, :, :], ALU.mult, ALU.mult)
            dve.drain()

            def collect(e):
                for i in range(MT):
                    dve.wait_ge(dr, MT * e + i + 1)
                    dve.scalar_tensor_tensor(tok[:, i, :], bank(4 + i)[:, 0:D], cnt[:, i, e:e + 1], tok[:, i, :],
                                             ALU.mult, ALU.add).then_inc(du, 1)

            for e in range(MOE_E):
                w = e % 2
                dve.wait_ge(gr, e + 1)
                for k in range(KC):
                    op = dve.tensor_scalar(gate[:, w, k, :], bank(k), gub[:, e, 0, k:k + 1], LIMIT, ALU.add, ALU.min)
                op.then_inc(gm, 1)
                for k in range(KC):
                    op = dve.tensor_scalar(up[:, w, k, :], bank(2 + k), gub[:, e, 1, k:k + 1], LIMIT, ALU.add,
                                           ALU.min)
                op.then_inc(iu, 1)
                dve.drain()
                dve.tensor_scalar(up[:, w, :, :], up[:, w, :, :], -LIMIT, 1.0, ALU.max, ALU.add)
                dve.wait_ge(gt, e + 1)
                dve.drain()
                dve.scalar_tensor_tensor(gate[:, w, :, :], th[:, w, :, :], 1.0, gate[:, w, :, :], ALU.add, ALU.mult)
                dve.drain()
                if e >= 2:
                    dve.wait_ge(dr, MT * (e - 1))
                dve.tensor_tensor(inter[:, w, :, :], gate[:, w, :, :], up[:, w, :, :], ALU.mult).then_inc(ir, 1)
                if e:
                    collect(e - 1)
            collect(MOE_E - 1)

    normalize("ln5", tok, None, tiles=MT)
    st = sem("moe_out_stored")
    with nc.Block() as block:
        @block.sync
        def _(sp):
            sp.dma_start(out[0, 0:MOE_TOK, :].rearrange("(i p) d -> p i d", p=P), tok[:, 0:MT, :]).then_inc(st, 16)
            sp.wait_ge(st, 16)


def _layout(x):
    import numpy as np

    a = {k: np.asarray(v) for k, v in x.items()}
    g = lambda n: a[n]
    gu, gub = g("L1_ffn_gate_up_proj"), g("L1_ffn_gate_up_proj_bias")
    qkv = np.concatenate([g("L0_ffn_q_proj"), g("L0_ffn_k_proj"), g("L0_ffn_v_proj")], axis=2)
    return {
        "x": g("L0_attn_x"),
        "xT": g("L0_attn_x").transpose(0, 2, 1),
        "WqkvgT": g("L0_attn_Wqkvg").T,
        "bqkvg": g("L0_attn_bqkvg"),
        "wave_frequency": g("L0_attn_wave_frequency"),
        "wave_damping": g("L0_attn_wave_damping"),
        "wave_phase": g("L0_attn_wave_phase"),
        "field_coupling": g("L0_attn_field_coupling"),
        "WoutT": g("L0_attn_Wout").T,
        "bout": g("L0_attn_bout"),
        "sim_matrix": g("L0_ffn_sim_matrix"),
        "gates": g("L0_ffn_gates"),
        "Wmoh": qkv.transpose(1, 0, 2).reshape(D, EXPERTS * QKV),
        "Wo": g("L0_ffn_o_proj").reshape(EXPERTS * EHD, D),
        "W_in": g("L1_attn_W_in"),
        "conv_w": g("L1_attn_conv_w").reshape(INNER, TAPS),
        "conv_b": g("L1_attn_conv_b"),
        "W_x": g("L1_attn_W_x"),
        "W_dt": g("L1_attn_W_dt"),
        "b_dt": g("L1_attn_b_dt"),
        "A_log": g("L1_attn_A_log"),
        "D": g("L1_attn_D"),
        "W_out": g("L1_attn_W_out"),
        "router_indices": g("L1_ffn_router_indices"),
        "routing_weights": g("L1_ffn_routing_weights"),
        "gate_up": gu.reshape(MOE_E, D, MOE_F, 2).transpose(0, 1, 3, 2).reshape(MOE_E, D, 2 * MOE_F),
        "gate_up_bias": gub.reshape(MOE_E, MOE_F, 2).transpose(0, 2, 1).reshape(-1),
        "down": g("L1_ffn_down_proj"),
        "down_bias": g("L1_ffn_down_proj_bias"),
    }


def kernel(**inputs):
    import concourse.bacc as _bacc
    import numpy as _np
    from concourse.bass_utils import run_bass_kernel_spmd as _run

    nc = _bacc.Bacc("TRN2", target_bir_lowering=False, num_devices=1)
    arrays, args = {}, {}
    for name, a in _layout(inputs).items():
        a = _np.ascontiguousarray(a)
        arrays[f"in_{name}"] = a
        args[name] = nc.dram_tensor(f"in_{name}", a.shape, mybir.dt.from_np(a.dtype), kind="ExternalInput").ap()
    out = nc.dram_tensor("out", (BATCH, SEQ, D), F32, kind="ExternalOutput").ap()
    build_program(nc, args, out)
    r = _run(nc, [arrays], core_ids=[0])
    return r.results[0]["out"]
```

```python
import math
from contextlib import ExitStack

import concourse.bass as bass
from concourse import mybir

F32 = mybir.dt.float32
F32R = mybir.dt.float32r
BF16 = mybir.dt.bfloat16
I32 = mybir.dt.int32
ALU = mybir.AluOpType
ACT = mybir.ActivationFunctionType
AX = mybir.AxisListType

P = 128
BATCH, SEQ, D = 4, 2048, 256
TILES = SEQ // P
CHUNK = 512
CHUNKS = SEQ // CHUNK
KC = D // P
EPS = 1e-5
HEADS, HD, FIELD = 16, 16, 512
LAST = FIELD - 2
EXPERTS, EHD = 16, 64
QKV = 3 * EHD
INNER, STATE, TAPS = 512, 16, 4
KI = INNER // P
MOE_E, MOE_TOK, MOE_F = 8, 512, 256
LIMIT, ALPHA = 7.0, 1.702
MASKED = -1e30
HALF = SEQ // 2


def build_program(nc, t, out):
    kpad = nc.dram_tensor("kernel_rows", (HEADS, 640), F32).ap()
    x2_dram = nc.dram_tensor("x_after_layer0", (BATCH, SEQ, D), F32).ap()
    x2T_dram = nc.dram_tensor("xT_after_layer0", (BATCH, D, SEQ), F32).ap()

    top = ExitStack()
    with top:
        def tile(stack, name, shape, dt=F32):
            return stack.enter_context(nc.sbuf_tensor(name, shape, dt))

        sems = {}

        def sem(name):
            if name not in sems:
                sems[name] = top.enter_context(nc.semaphore(name))
            return sems[name]

        def clear(names_before):
            numbers = [h.num for n, h in sems.items() if n not in names_before]
            nc.gpsimd.sem_clear(range(min(numbers), max(numbers) + 1))
            nc.all_engine_barrier(sem_only=True)

        PS = top.enter_context(nc.psum_tensor("PS", [P, 8 * CHUNK], F32))

        def bank(i, n=1):
            return PS[:, i * CHUNK:(i + n) * CHUNK]

        ident = tile(top, "ident", [P, P])
        ones = tile(top, "ones", [P, P])
        eps_pow = tile(top, "eps_pow", [P, TILES])
        half_pow = tile(top, "half_pow", [P, TILES])

        def layer_norm(name, s, tok, xT=None, tiles=TILES, tr_bank=6):
            stats = tile(s, name + "_stats", [P, tiles, 6])
            mv = tile(s, name + "_mv", [P, tiles, 2])
            var = tile(s, name + "_var", [P, tiles])
            rstd = tile(s, name + "_rstd", [P, tiles])
            var_ready, rstd_ready = sem(name + "_var_ready"), sem(name + "_rstd_ready")
            norm_done, tr_ready = sem(name + "_norm_done"), sem(name + "_tr_ready")
            tr_copied = sem(name + "_tr_copied")

            class Steps:
                done = norm_done
                copied = tr_copied

                @staticmethod
                def statistics(dve, g):
                    dve.drain()
                    for i in range(4 * g, 4 * g + 4):
                        dve.bn_stats(stats[:, i, :], tok[:, i, :])
                    dve.drain()
                    for i in range(4 * g, 4 * g + 4):
                        dve.bn_aggr(mv[:, i, :], stats[:, i, :])
                    dve.drain()
                    dve.tensor_scalar(var[:, 4 * g:4 * g + 4], mv[:, 4 * g:4 * g + 4, 1], EPS, None,
                                      ALU.add).then_inc(var_ready, 1)

                @staticmethod
                def root(pool, g):
                    pool.wait_ge(var_ready, g + 1)
                    w = slice(4 * g, 4 * g + 4)
                    pool.tensor_tensor(rstd[:, w], var[:, w], eps_pow[:, w], ALU.pow).then_inc(rstd_ready, 1)

                @staticmethod
                def scale(dve, g):
                    dve.wait_ge(rstd_ready, g + 1)
                    for i in range(4 * g, 4 * g + 4):
                        last = dve.tensor_scalar(tok[:, i, :], tok[:, i, :], mv[:, i, 0:1], rstd[:, i:i + 1],
                                                 ALU.subtract, ALU.mult)
                    last.then_inc(norm_done, 1)

                @staticmethod
                def transpose(pe, g):
                    pe.wait_ge(norm_done, g + 1)
                    for p in (2 * g, 2 * g + 1):
                        if p >= 2:
                            pe.wait_ge(tr_copied, p - 1)
                        for k in range(KC):
                            for j in range(2):
                                o = bank(tr_bank + p % 2)[:, k * 256 + j * P:k * 256 + (j + 1) * P]
                                last = pe.transpose(o, tok[:, 2 * p + j, k * P:(k + 1) * P], ident[:, :])
                        last.then_inc(tr_ready, 1)

                @staticmethod
                def copy(act, g):
                    for p in (2 * g, 2 * g + 1):
                        act.wait_ge(tr_ready, p + 1)
                        act.activation(xT[:, :, 256 * p:256 * p + 256],
                                       bank(tr_bank + p % 2).rearrange("p (k n) -> p k n", k=KC),
                                       ACT.Copy).then_inc(tr_copied, 1)

            return Steps

        with nc.Block() as block:
            c0, c1 = sem("const_zeroed"), sem("const_ready")

            @block.gpsimd
            def _(pool):
                pool.memset(ident[:, :], 0.0)
                pool.memset(ones[:, :], 1.0)
                pool.memset(eps_pow[:, :], -0.5)
                pool.memset(half_pow[:, :], 0.5).then_inc(c0, 1)
                pool.wait_ge(c0, 1)
                pool.affine_select(out=ident[:, :], in_=ident[:, :], compare_op=ALU.not_equal, fill=1.0,
                                   base=0, pattern=[[-1, P]], channel_multiplier=1).then_inc(c1, 1)

        layer0(nc, t, out, top, tile, sem, sems, clear, bank, ident, ones, half_pow, layer_norm, kpad, x2_dram,
               x2T_dram)
        layer1(nc, t, out, top, tile, sem, sems, clear, bank, ident, ones, layer_norm, x2_dram, x2T_dram)


def layer0(nc, t, out, top, tile, sem, sems, clear, bank, ident, ones, half_pow, layer_norm, kpad, x2_dram,
           x2T_dram):
    with ExitStack() as L:
        wqkvg = tile(L, "wqkvg", [P, KC, 4 * D])
        wout = tile(L, "wout", [P, KC, D])
        wmoh = [tile(L, "wmoh_" + part, [P, KC, EXPERTS * QKV], F32R) for part in ("hi", "lo")]
        wo = tile(L, "wo", [P, EXPERTS * EHD // P, D])
        bq = tile(L, "bq", [P, 4 * KC])
        bg_half = tile(L, "bg_half", [P, KC])
        bout = tile(L, "bout", [P, D])
        toep = tile(L, "toep", [P, HEADS, FIELD])
        cct = tile(L, "cct", [P, KC, D])
        simn = tile(L, "simn", [P, KC, P])
        gate_sig = tile(L, "gate_sig", [P, EXPERTS])
        causal = tile(L, "causal", [P, P])
        dpad = tile(L, "dpad", [P, 4, HEADS, 32])

        with ExitStack() as s:
            freq, damp, phase = (tile(s, n, [HEADS, 1]) for n in ("freq", "damp", "phase"))
            ti = tile(s, "ti", [HEADS, FIELD], I32)
            tf = tile(s, "tf", [HEADS, FIELD])
            ang = tile(s, "ang", [HEADS, FIELD])
            turns = tile(s, "turns", [HEADS, FIELD])
            decay = tile(s, "decay", [HEADS, FIELD])
            krow = tile(s, "krow", [HEADS, 640])
            sm = tile(s, "sm", [HEADS, 8])
            fc = tile(s, "fc", [HEADS, HEADS])
            fcx = tile(s, "fcx", [HEADS, HEADS, HD])
            dm = tile(s, "dm", [P, HD])
            sim = tile(s, "sim", [P, KC, EXPERTS])
            simsq = tile(s, "simsq", [P, KC, EXPERTS])
            simr = tile(s, "simr", [P, EXPERTS])
            gts = tile(s, "gts", [P, EXPERTS])
            wmoh_in = tile(s, "wmoh_in", [P, KC, EXPERTS * QKV])
            hi_ready = sem("wmoh_hi_ready")
            small, big, c_zero, c_mask = sem("small_loaded"), sem("big_loaded"), sem("dpad_zero"), sem("mask_ready")
            iota_ready, a1, v1 = sem("iota_ready"), sem("setup_act"), sem("setup_dve")
            sq_ready = sem("squares_ready")
            pw, m1, kst, tl = sem("setup_pow"), sem("setup_mm"), sem("kernel_stored"), sem("toep_loaded")
            with nc.Block() as block:
                @block.sync
                def _(sp):
                    for dst, name in ((freq, "wave_frequency"), (damp, "wave_damping"), (phase, "wave_phase")):
                        sp.dma_start(dst[:, :], t[name].rearrange("(h o) -> h o", o=1)).then_inc(small, 16)
                    sp.dma_start(fc[:, :], t["field_coupling"]).then_inc(small, 16)
                    sp.dma_start(sim[:, :, :], t["sim_matrix"].rearrange("(k p) e -> p k e", p=P)).then_inc(small, 16)
                    sp.dma_start(gts[:, :], t["gates"].partition_broadcast(P)).then_inc(small, 16)
                    with nc.allow_non_contiguous_dma(reason="a bias, once"):
                        sp.dma_start(bq[:, :], t["bqkvg"].rearrange("(m p) -> p m", p=P)).then_inc(small, 16)
                    sp.dma_start(bout[:, :], t["bout"].partition_broadcast(P)).then_inc(big, 16)
                    for dst, name in ((wmoh_in, "Wmoh"), (wqkvg, "WqkvgT"), (wout, "WoutT"), (wo, "Wo")):
                        sp.dma_start(dst[:, :, :], t[name].rearrange("(k p) n -> p k n", p=P)).then_inc(big, 16)
                    sp.wait_ge(v1, 6)
                    sp.dma_start(kpad, krow[:, :]).then_inc(kst, 16)
                    sp.wait_ge(kst, 16)
                    sp.dma_start(toep[:, :, :], bass.AP(tensor=kpad.tensor, offset=0,
                                                        ap=[[1, P], [640, HEADS], [1, FIELD]])).then_inc(tl, 16)
                    sp.wait_ge(tl, 16)
                    sp.wait_ge(big, 16 * 5)

                @block.gpsimd
                def _(pool):
                    pool.iota(ti[:, :], pattern=[[1, FIELD]], base=0, channel_multiplier=0).then_inc(iota_ready, 1)
                    pool.memset(dpad[:, :, :, :], 0.0)
                    pool.memset(simn[:, :, EXPERTS:P], 0.0)
                    pool.memset(krow[:, :], 0.0)
                    pool.memset(causal[:, :], 0.0).then_inc(c_zero, 1)
                    pool.wait_ge(c_zero, 1)
                    pool.affine_select(out=causal[:, :], in_=causal[:, :], compare_op=ALU.is_ge, fill=MASKED,
                                       base=0, pattern=[[-1, P]], channel_multiplier=1).then_inc(c_mask, 1)
                    pool.wait_ge(v1, 7)
                    pool.tensor_tensor(simr[:, :], simr[:, :], half_pow[:, 0:EXPERTS], ALU.pow).then_inc(pw, 1)

                @block.scalar
                def _(act):
                    act.wait_ge(small, 16 * 7)
                    act.mul(bg_half[:, :], bq[:, 3 * KC:4 * KC], 0.5)
                    act.activation(gate_sig[:, :], gts[:, :], ACT.Tanh, scale=0.5)
                    act.activation(sm[:, 0:1], damp[:, :], ACT.Abs).then_inc(a1, 1)
                    act.wait_ge(a1, 1)
                    act.activation(sm[:, 1:2], sm[:, 0:1], ACT.Exp, scale=-1.0).then_inc(a1, 1)
                    act.wait_ge(a1, 2)
                    act.activation(sm[:, 2:3], sm[:, 1:2], ACT.Ln, bias=1.0).then_inc(a1, 1)
                    act.wait_ge(v1, 2)
                    act.activation(decay[:, :], tf[:, :], ACT.Exp, scale=sm[:, 3:4]).then_inc(a1, 1)
                    act.wait_ge(v1, 3)
                    act.activation(fc[:, :], fc[:, :], ACT.Exp, accum_out=sm[:, 6:7]).then_inc(a1, 1)
                    act.wait_ge(v1, 4)
                    act.activation(ang[:, :], ang[:, :], ACT.Sin).then_inc(a1, 1)
                    act.wait_ge(big, 16 * 5)
                    act.activation(wmoh[0][:, :, :], wmoh_in[:, :, :], ACT.Copy).then_inc(hi_ready, 1)

                @block.vector
                def _(dve):
                    dve.wait_ge(iota_ready, 1)
                    dve.tensor_copy(tf[:, :], ti[:, :]).then_inc(v1, 1)
                    dve.wait_ge(small, 16 * 7)
                    dve.wait_ge(a1, 3)
                    dve.scalar_tensor_tensor(sm[:, 3:4], damp[:, :], 0.0, sm[:, 2:3], ALU.max, ALU.add)
                    dve.drain()
                    dve.tensor_scalar(sm[:, 3:4], sm[:, 3:4], -1.0, None, ALU.mult).then_inc(v1, 1)
                    dve.reduce_max(sm[:, 4:5], fc[:, :], axis=AX.X)
                    dve.drain()
                    dve.tensor_scalar(fc[:, :], fc[:, :], sm[:, 4:5], None, ALU.subtract).then_inc(v1, 1)
                    two_pi = 2 * math.pi
                    hi = 6.28125
                    mid = float(round((two_pi - hi) * 2 ** 21) / 2 ** 21)
                    lo = two_pi - hi - mid
                    magic = 1.5 * 2 ** 23
                    dve.tensor_scalar(ang[:, :], tf[:, :], freq[:, :], phase[:, :], ALU.mult, ALU.add)
                    dve.drain()
                    dve.tensor_scalar(turns[:, :], ang[:, :], 1 / two_pi, 0.25, ALU.mult, ALU.add)
                    dve.drain()
                    dve.tensor_scalar(turns[:, :], turns[:, :], magic, None, ALU.add)
                    dve.drain()
                    dve.tensor_scalar(turns[:, :], turns[:, :], magic, None, ALU.subtract)
                    for part in (hi, mid, lo):
                        dve.drain()
                        dve.scalar_tensor_tensor(ang[:, :], turns[:, :], -part, ang[:, :], ALU.mult, ALU.add)
                    dve.drain()
                    dve.tensor_scalar(ang[:, :], ang[:, :], math.pi / 2, 3.1415925, ALU.add, ALU.min)
                    dve.drain()
                    dve.tensor_scalar(ang[:, :], ang[:, :], -3.1415925, None, ALU.max).then_inc(v1, 1)
                    dve.wait_ge(a1, 5)
                    dve.reciprocal(sm[:, 6:7], sm[:, 6:7])
                    dve.drain()
                    dve.tensor_scalar(fc[:, :], fc[:, :], sm[:, 6:7], 0.5, ALU.mult, ALU.mult)
                    dve.drain()
                    dve.tensor_copy(fcx[:, :, :], fc[:, :].unsqueeze(2).broadcast_to([HEADS, HEADS, HD]))\
                       .then_inc(v1, 1)
                    dve.wait_ge(a1, 6)
                    dve.tensor_tensor(decay[:, :], decay[:, :], ang[:, :], ALU.mult)
                    dve.drain()
                    dve.tensor_reduce(sm[:, 7:8], decay[:, :], AX.X, ALU.add, apply_absolute_value=True)
                    dve.drain()
                    dve.tensor_scalar(sm[:, 7:8], sm[:, 7:8], 1e-8, None, ALU.max)
                    dve.drain()
                    dve.reciprocal(sm[:, 7:8], sm[:, 7:8])
                    dve.drain()
                    dve.wait_ge(c_zero, 1)
                    dve.tensor_scalar(krow[:, P - 1:P - 1 + FIELD], decay[:, :], sm[:, 7:8], None, ALU.mult)\
                       .then_inc(v1, 1)
                    dve.tensor_tensor(simsq[:, :, :], sim[:, :, :], sim[:, :, :], ALU.mult)
                    dve.tensor_scalar(gate_sig[:, :], gate_sig[:, :], 0.5, 0.5, ALU.mult, ALU.add)
                    dve.tensor_reduce(dm[:, :], ident[:, :].rearrange("p (j d) -> p d j", d=HD), AX.X, ALU.add)\
                       .then_inc(sq_ready, 1)
                    dve.wait_ge(m1, 1)
                    dve.tensor_copy(simr[:, :], bank(0)[:, 0:EXPERTS]).then_inc(v1, 1)
                    dve.wait_ge(pw, 1)
                    dve.tensor_scalar(simr[:, :], simr[:, :], 1e-12, None, ALU.max)
                    dve.drain()
                    dve.reciprocal(simr[:, :], simr[:, :])
                    dve.drain()
                    for k in range(KC):
                        dve.tensor_tensor(simn[:, k, 0:EXPERTS], sim[:, k, :], simr[:, :], ALU.mult)
                    dve.wait_ge(m1, 2)
                    for k in range(KC):
                        dve.tensor_tensor(cct[:, k, :].rearrange("p (i d) -> p i d", d=HD),
                                          bank(1 + k)[:, 0:HEADS].unsqueeze(2).broadcast_to([P, HEADS, HD]),
                                          dm[:, :].unsqueeze(1).broadcast_to([P, HEADS, HD]), ALU.mult)
                    dve.wait_ge(hi_ready, 1)
                    dve.tensor_tensor(wmoh[1][:, :, :], wmoh_in[:, :, :], wmoh[0][:, :, :].bitcast(F32), ALU.subtract)

                @block.tensor
                def _(pe):
                    pe.wait_ge(sq_ready, 1)
                    for k in range(KC):
                        last = pe.matmul(bank(0)[:, 0:EXPERTS], ones[:, :], simsq[:, k, :],
                                         start=(k == 0), stop=(k == KC - 1))
                    last.then_inc(m1, 1)
                    fr = fcx[:, :, :].rearrange("i j d -> i (j d)")
                    for k in range(KC):
                        last = pe.matmul(bank(1 + k)[:, 0:HEADS], fr[:, k * P:(k + 1) * P],
                                         ident[0:HEADS, 0:HEADS], start=True, stop=True)
                    last.then_inc(m1, 1)

        outside = set(sems)
        tok = tile(L, "tok", [P, TILES, D])
        xT = tile(L, "xT", [P, KC, SEQ])
        with nc.Fori(0, BATCH) as b:
            with ExitStack() as s:
                wave_branch(nc, t, b, s, tile, sem, bank, ident, tok, xT, wqkvg, bq, bg_half, bout, wout, toep,
                            cct, dpad, layer_norm)
            with ExitStack() as s:
                head_mixture(nc, b, s, tile, sem, bank, ident, half_pow, tok, xT, wmoh, wo, simn, gate_sig, causal,
                             layer_norm, x2_dram, x2T_dram)
            clear(outside)


def wave_branch(nc, t, b, s, tile, sem, bank, ident, tok, xT, wqkvg, bq, bg_half, bout, wout, toep, cct, dpad,
                layer_norm):
    qg = tile(s, "qg", [P, KC, SEQ])
    dep = tile(s, "dep", [P, KC, SEQ])
    tmp = tile(s, "feat_tmp", [P, 2, 5, CHUNK])
    qf = tile(s, "qf", [P, 2, CHUNK])
    tail = tile(s, "tail", [P, KC])
    conv = tile(s, "conv", [P, KC, FIELD])
    lastg = tile(s, "lastg", [P, KC])
    proj, feat, used = sem("proj_ready"), sem("feat_ready"), sem("proj_used")
    x_in = [sem(f"x_loaded{n}") for n in range(CHUNKS)]
    units = [(c, n) for c in range(KC) for n in range(CHUNKS)]
    with nc.Block() as block:
        @block.sync
        def _(sp):
            for n in range(CHUNKS):
                at = slice(n * CHUNK, (n + 1) * CHUNK)
                sp.dma_start(xT[:, :, at], t["xT"][b].rearrange("(k p) n -> p k n", p=P)[:, :, at])\
                  .then_inc(x_in[n], 16)
            sp.dma_start(tok[:, :, :], t["x"][b].rearrange("(i p) d -> p i d", p=P)).then_inc(sem("tok_in"), 16)
            sp.wait_ge(sem("tok_in"), 16)

        @block.gpsimd
        def _(pool):
            pool.wait_ge(sem("tok_in"), 16)
            pool.tensor_tensor(tok[:, :, :], tok[:, :, :], bout[:, :].unsqueeze(1).broadcast_to([P, TILES, D]),
                               ALU.add)

        @block.tensor
        def _(pe):
            for u, (c, n) in enumerate(units):
                if c == 0:
                    pe.wait_ge(x_in[n], 16)
                if u >= 2:
                    pe.wait_ge(used, u - 1)
                for kind in range(4):
                    m = kind * KC + c
                    for k in range(KC):
                        last = pe.matmul(bank(4 * (u % 2) + kind), wqkvg[:, k, m * P:(m + 1) * P],
                                         xT[:, k, n * CHUNK:(n + 1) * CHUNK], start=(k == 0), stop=(k == KC - 1))
                last.then_inc(proj, 1)

        @block.scalar
        def _(act):
            for u, (c, n) in enumerate(units):
                act.wait_ge(proj, u + 1)
                if u >= 2:
                    act.wait_ge(used, u - 1)
                w = u % 2
                q, k, g = bank(4 * w), bank(4 * w + 1), bank(4 * w + 3)
                act.activation(tmp[:, w, 0, :], q, ACT.Exp, bias=bq[:, c:c + 1])
                act.activation(tmp[:, w, 1, :], q, ACT.Relu, bias=bq[:, c:c + 1])
                act.activation(tmp[:, w, 2, :], k, ACT.Exp, bias=bq[:, KC + c:KC + c + 1])
                act.activation(tmp[:, w, 3, :], k, ACT.Relu, bias=bq[:, KC + c:KC + c + 1])
                act.activation(tmp[:, w, 4, :], g, ACT.Tanh, bias=bg_half[:, c:c + 1], scale=0.5)\
                   .then_inc(feat, 1)

        @block.vector
        def _(dve):
            for u, (c, n) in enumerate(units):
                w, at = u % 2, slice(n * CHUNK, (n + 1) * CHUNK)
                dve.wait_ge(feat, u + 1)
                dve.drain()
                dve.scalar_tensor_tensor(qf[:, 0, :], tmp[:, w, 0, :], 1.0, tmp[:, w, 1, :], ALU.min, ALU.add)
                dve.scalar_tensor_tensor(qf[:, 1, :], tmp[:, w, 2, :], 1.0, tmp[:, w, 3, :], ALU.min, ALU.add)
                dve.drain()
                dve.scalar_tensor_tensor(qg[:, c, at], tmp[:, w, 4, :], 1.0, qf[:, 0, :], ALU.add, ALU.mult)
                dve.scalar_tensor_tensor(dep[:, c, at], bank(4 * w + 2), bq[:, 2 * KC + c:2 * KC + c + 1],
                                         qf[:, 1, :], ALU.add, ALU.mult).then_inc(used, 1)
            dve.drain()
            for c in range(KC):
                dve.tensor_reduce(tail[:, c:c + 1], dep[:, c, LAST:SEQ], AX.X, ALU.add)
            dve.drain()
            for c in range(KC):
                dve.tensor_copy(dep[:, c, LAST:LAST + 1], tail[:, c:c + 1])
            dve.drain()
            for c in range(KC):
                for sc in range(FIELD // P):
                    cells = dep[:, c, sc * P:(sc + 1) * P]
                    dve.tensor_copy(conv[:, c, sc * P:(sc + 1) * P],
                                    bass.AP(tensor=cells.tensor, offset=cells.offset + P - 1,
                                            ap=[list(cells.ap[0]), [-1, P]]))

    tr, trc, cv, cvc, fcr = (sem(n) for n in ("dep_tr", "dep_copied", "conv_ready", "conv_copied", "field_ready"))
    wd, mm, su = sem("wave_done"), sem("wout_ready"), sem("wout_used")
    ln1 = layer_norm("ln1", s, tok, xT)
    with nc.Block() as block:
        @block.tensor
        def _(pe):
            for sc in range(4):
                for c in range(KC):
                    last = pe.transpose(bank(sc)[:, c * P:(c + 1) * P], conv[:, c, sc * P:(sc + 1) * P], ident[:, :])
                last.then_inc(tr, 1)
            pe.wait_ge(trc, 4)
            for c in range(KC):
                for j in range(4):
                    steps = [(c * 8 + 2 * j, 0)] + [(c * 8 + 2 * j + e, sc) for sc in range(1, 4) for e in range(2)]
                    steps += [(c * 8 + 2 * j + 1, 0)]
                    for q, (h, sc) in enumerate(steps):
                        last = pe.matmul(bank(4 + c)[32 * j:32 * j + 32, sc * P:FIELD], dpad[:, sc, h, :],
                                         toep[:, h, 0:FIELD - sc * P], start=(q == 0), stop=(q == len(steps) - 1),
                                         tile_position=(0, 32 * j))
                last.then_inc(cv, 1)
            pe.wait_ge(cvc, KC)
            for m in range(KC):
                for k in range(KC):
                    last = pe.matmul(bank(6 + m), cct[:, k, m * P:(m + 1) * P], conv[:, k, :],
                                     start=(k == 0), stop=(k == KC - 1))
                last.then_inc(fcr, 1)
            pe.wait_ge(wd, 2)
            for i in range(TILES):
                if i >= 6:
                    pe.wait_ge(su, i - 5)
                for k in range(KC):
                    last = pe.matmul(bank(i % 6)[:, 0:D],
                                     qg[:, k, i * P:(i + 1) * P], wout[:, k, :], start=(k == 0), stop=(k == KC - 1))
                last.then_inc(mm, 1)
                if i in (10, 14):
                    ln1.transpose(pe, (i - 10) // 4)
            ln1.transpose(pe, 2)
            ln1.transpose(pe, 3)

        @block.scalar
        def _(act):
            for c in range(KC):
                act.wait_ge(cv, c + 1)
                act.activation(conv[:, c, :], bank(4 + c), ACT.Copy).then_inc(cvc, 1)
            for g in range(TILES // 4):
                ln1.copy(act, g)

        @block.gpsimd
        def _(pool):
            for g in range(TILES // 4):
                ln1.root(pool, g)

        @block.vector
        def _(dve):
            for sc in range(4):
                dve.wait_ge(tr, sc + 1)
                src = bank(sc)[:, 0:D].rearrange("p (j e d) -> p j e d", e=2, d=HD)
                dst = dpad[:, sc, :, :].rearrange("p (j e) c -> p j e c", e=2)
                dve.tensor_copy(dst[:, :, 0, 0:HD], src[:, :, 0, :])
                dve.tensor_copy(dst[:, :, 1, HD:2 * HD], src[:, :, 1, :]).then_inc(trc, 1)
            for m in range(KC):
                dve.wait_ge(fcr, m + 1)
                dve.tensor_copy(lastg[:, m:m + 1], bank(6 + m)[:, LAST:LAST + 1])
                dve.tensor_tensor(qg[:, m, 0:LAST + 1], qg[:, m, 0:LAST + 1], bank(6 + m)[:, 0:LAST + 1], ALU.mult)
                dve.drain()
                dve.tensor_scalar(qg[:, m, LAST + 1:SEQ], qg[:, m, LAST + 1:SEQ], lastg[:, m:m + 1], None,
                                  ALU.mult).then_inc(wd, 1)
            for g in range(TILES // 4):
                for i in range(4 * g, 4 * g + 4):
                    dve.wait_ge(mm, i + 1)
                    dve.tensor_tensor(tok[:, i, :], tok[:, i, :], bank(i % 6)[:, 0:D], ALU.add).then_inc(su, 1)
                ln1.statistics(dve, g)
                if g:
                    ln1.scale(dve, g - 1)
            ln1.scale(dve, TILES // 4 - 1)


def head_mixture(nc, b, s, tile, sem, bank, ident, half_pow, tok, xT, wmoh, wo, simn, gate_sig, causal,
                 layer_norm, x2_dram, x2T_dram):
    rw = tile(s, "rw", [P, TILES, EXPERTS])
    qT = tile(s, "qT", [EHD, SEQ])
    kT = tile(s, "kT", [EHD, SEQ])
    v = tile(s, "v", [P, TILES, P])
    attn = tile(s, "attn", [P, TILES, EHD])
    with ExitStack() as g:
        lg, ex, fb, rep = (tile(g, n, [P, TILES, EXPERTS]) for n in ("lg", "ex", "fb", "rep"))
        top8 = tile(g, "top8", [P, TILES, 8])
        best = tile(g, "best", [P, TILES])
        ss, rs = tile(g, "ss", [P, TILES]), tile(g, "rs", [P, TILES])
        sq = tile(g, "sq", [P, 2, D])
        sr, sp_, lr, le, lx = (sem(n) for n in ("norm_sums", "norm_root", "logits_mm", "logits", "logits_exp"))
        with nc.Block() as block:
            @block.tensor
            def _(pe):
                for i in range(TILES):
                    for k in range(KC):
                        last = pe.matmul(bank(0, 4)[:, i * P:(i + 1) * P], xT[:, k, i * P:(i + 1) * P],
                                         simn[:, k, :], start=(k == 0), stop=(k == KC - 1))
                last.then_inc(lr, 1)

            @block.scalar
            def _(act):
                for i in range(TILES):
                    if i >= 2:
                        act.wait_ge(sr, i - 1)
                    act.activation(sq[:, i % 2, :], tok[:, i, :], ACT.Square, accum_out=ss[:, i:i + 1])\
                       .then_inc(sr, 1)
                act.wait_ge(le, 1)
                act.activation(ex[:, :, :], lg[:, :, :], ACT.Exp).then_inc(lx, 1)

            @block.gpsimd
            def _(pool):
                pool.wait_ge(sr, TILES)
                pool.tensor_tensor(rs[:, :], ss[:, :], half_pow[:, :], ALU.pow).then_inc(sp_, 1)

            @block.vector
            def _(dve):
                def wide(a):
                    return a.unsqueeze(2).broadcast_to([P, TILES, EXPERTS])

                dve.wait_ge(sp_, 1)
                dve.tensor_scalar(rs[:, :], rs[:, :], 1e-12, None, ALU.max)
                dve.drain()
                dve.reciprocal(rs[:, :], rs[:, :])
                dve.drain()
                dve.wait_ge(lr, 1)
                dve.tensor_tensor(lg[:, :, :], bank(0, 4).rearrange("p (i e) -> p i e", e=P)[:, :, 0:EXPERTS],
                                  wide(rs[:, :]), ALU.mult)
                dve.drain()
                dve.tensor_tensor(lg[:, :, :], lg[:, :, :],
                                  gate_sig[:, :].unsqueeze(1).broadcast_to([P, TILES, EXPERTS]), ALU.subtract)\
                   .then_inc(le, 1)
                dve.drain()
                for i in range(TILES):
                    dve.max(top8[:, i, :], lg[:, i, :])
                dve.drain()
                dve.tensor_copy(best[:, :], top8[:, :, 0])
                dve.drain()
                dve.memset(top8[:, :, 2:8], -3e38)
                dve.drain()
                for i in range(TILES):
                    dve.match_replace(rep[:, i, :], top8[:, i, :], lg[:, i, :], 1e30)
                dve.drain()
                dve.tensor_scalar(fb[:, :, :], rep[:, :, :], 1e29, None, ALU.is_gt)
                dve.tensor_scalar(best[:, :], best[:, :], 0.0, None, ALU.is_le)
                dve.drain()
                dve.tensor_tensor(fb[:, :, :], fb[:, :, :], wide(best[:, :]), ALU.mult)
                dve.wait_ge(lx, 1)
                dve.scalar_tensor_tensor(ex[:, :, :], lg[:, :, :], 0.0, ex[:, :, :], ALU.is_gt, ALU.mult)
                dve.drain()
                dve.tensor_tensor(ex[:, :, :], ex[:, :, :], fb[:, :, :], ALU.add)
                dve.drain()
                dve.tensor_reduce(ss[:, :], ex[:, :, :], AX.X, ALU.add)
                dve.drain()
                dve.reciprocal(ss[:, :], ss[:, :])
                dve.drain()
                dve.tensor_tensor(rw[:, :, :], ex[:, :, :], wide(ss[:, :]), ALU.mult)

    with ExitStack() as g:
        acc = tile(g, "acc", [P, 4, QKV])
        acc2 = tile(g, "acc2", [P, 2, QKV])
        qk = tile(g, "qk", [P, 2, 2 * EHD])
        xhi, xlo = (tile(g, n, [P, 2, KC, P], F32R) for n in ("xhi", "xlo"))
        pairs = EXPERTS // 2
        pr, pu, qr, qt, qc, hi, lo = (sem(n) for n in ("pair_ready", "pair_used", "qk_ready", "qk_tr", "qk_copied",
                                                       "x_hi_ready", "x_lo_ready"))
        with nc.Block() as block:
            @block.gpsimd
            def _(pool):
                pool.memset(v[:, :, EHD:P], 0.0)
                for i in range(TILES):
                    pool.wait_ge(hi, i + 1)
                    if i >= 2:
                        pool.wait_ge(pr, pairs * (i - 1))
                    pool.tensor_tensor(xlo[:, i % 2, :, :], xT[:, :, i * P:(i + 1) * P],
                                       xhi[:, i % 2, :, :].bitcast(F32), ALU.subtract).then_inc(lo, 1)

            @block.tensor
            def _(pe):
                def flip(i):
                    pe.wait_ge(qr, i + 1)
                    if i >= 2:
                        pe.wait_ge(qc, i - 1)
                    pe.transpose(bank(6 + i % 2)[0:EHD, 0:P], qk[:, i % 2, 0:EHD], ident[:, :])
                    pe.transpose(bank(6 + i % 2)[0:EHD, P:2 * P], qk[:, i % 2, EHD:2 * EHD], ident[:, :])\
                      .then_inc(qt, 1)

                passes = [(x, part, k) for x, part in ((xhi, 0), (xhi, 1), (xlo, 0)) for k in range(KC)]
                for i in range(TILES):
                    pe.wait_ge(lo, i + 1)
                    for j in range(pairs):
                        n = i * pairs + j
                        if n >= 6:
                            pe.wait_ge(pu, n - 5)
                        for q, (x, part, k) in enumerate(passes):
                            last = pe.matmul(bank(n % 6)[:, 0:2 * QKV], x[:, i % 2, k, :],
                                             wmoh[part][:, k, 2 * j * QKV:(2 * j + 2) * QKV],
                                             start=(q == 0), stop=(q == len(passes) - 1))
                        last.then_inc(pr, 1)
                    if i:
                        flip(i - 1)
                flip(TILES - 1)

            @block.vector
            def _(dve):
                for i in range(TILES):
                    for e in range(EXPERTS):
                        n = i * pairs + e // 2
                        if e % 2 == 0:
                            dve.wait_ge(pr, n + 1)
                        if e % 4 == 0:
                            dve.drain()
                        src = bank(n % 6)[:, (e % 2) * QKV:(e % 2 + 1) * QKV]
                        if e < 4:
                            op = dve.tensor_scalar(acc[:, e, :], src, rw[:, i, e:e + 1], None, ALU.mult)
                        else:
                            op = dve.scalar_tensor_tensor(acc[:, e % 4, :], src, rw[:, i, e:e + 1], acc[:, e % 4, :],
                                                          ALU.mult, ALU.add)
                        if e % 2:
                            op.then_inc(pu, 1)
                    dve.drain()
                    dve.tensor_tensor(acc2[:, :, :], acc[:, 0:2, :], acc[:, 2:4, :], ALU.add)
                    dve.drain()
                    if i >= 2:
                        dve.wait_ge(qt, i - 1)
                    dve.tensor_tensor(v[:, i, 0:EHD], acc2[:, 0, 2 * EHD:QKV], acc2[:, 1, 2 * EHD:QKV], ALU.add)
                    dve.tensor_tensor(qk[:, i % 2, :], acc2[:, 0, 0:2 * EHD], acc2[:, 1, 0:2 * EHD], ALU.add)\
                       .then_inc(qr, 1)

            @block.scalar
            def _(act):
                def round_x(i):
                    if i >= 2:
                        act.wait_ge(pr, pairs * (i - 1))
                    act.activation(xhi[:, i % 2, :, :], xT[:, :, i * P:(i + 1) * P], ACT.Copy).then_inc(hi, 1)

                round_x(0)
                round_x(1)
                for i in range(TILES):
                    if i + 2 < TILES:
                        round_x(i + 2)
                    act.wait_ge(qt, i + 1)
                    act.activation(qT[:, i * P:(i + 1) * P], bank(6 + i % 2)[0:EHD, 0:P], ACT.Copy)
                    act.activation(kT[:, i * P:(i + 1) * P], bank(6 + i % 2)[0:EHD, P:2 * P], ACT.Copy)\
                       .then_inc(qc, 1)

    with ExitStack() as g:
        prob = tile(g, "prob", [P, 2, SEQ])
        probT = tile(g, "probT", [P, 2, CHUNK])
        mx, den = tile(g, "mx", [P, TILES]), tile(g, "den", [P, TILES])
        scale = 1.0 / math.sqrt(EHD)
        sr, mr, pr, tr, tc, pv, orr, ou = (sem(n) for n in (
            "scores_ready", "max_ready", "probs_ready", "probs_tr", "probs_copied", "pv_done", "attn_ready",
            "attn_used"))
        groups = []
        for i in range(TILES):
            groups += [(i, a, min(4, i + 1 - a)) for a in range(0, i + 1, 4)]
        first = {i: min(n for n, x in enumerate(groups) if x[0] == i) for i in range(TILES)}
        first[TILES] = len(groups)
        with nc.Block() as block:
            @block.tensor
            def _(pe):
                def scores(i):
                    width = (i + 1) * P
                    for a in range(0, width, CHUNK):
                        z = min(width, a + CHUNK)
                        last = pe.matmul(bank(0, 4)[:, a:z], qT[:, i * P:(i + 1) * P], kT[:, a:z],
                                         start=True, stop=True)
                    last.then_inc(sr, 1)

                def values(n):
                    i, a, m = groups[n]
                    pe.wait_ge(tc, n + 1)
                    if a == 0 and i >= 2:
                        pe.wait_ge(ou, i - 1)
                    for j in range(m):
                        last = pe.matmul(bank(6 + i % 2)[:, 0:P], probT[:, n % 2, j * P:(j + 1) * P],
                                         v[:, a + j, :], start=(a + j == 0), stop=(a + j == i))
                    last.then_inc(pv, 1)

                scores(0)
                for i in range(TILES):
                    pe.wait_ge(pr, i + 1)
                    if i + 1 < TILES:
                        scores(i + 1)
                    for n in range(first[i], first[i + 1]):
                        _, a, m = groups[n]
                        if n >= 2:
                            pe.wait_ge(tc, n - 1)
                        for j in range(m):
                            last = pe.transpose(bank(4 + n % 2)[:, j * P:(j + 1) * P],
                                                prob[:, i % 2, (a + j) * P:(a + j + 1) * P], ident[:, :])
                        last.then_inc(tr, 1)
                        if n > first[i]:
                            values(n - 1)
                    values(first[i + 1] - 1)

            @block.vector
            def _(dve):
                def maximum(i):
                    width = (i + 1) * P
                    dve.wait_ge(sr, i + 1)
                    dve.tensor_tensor(bank(0, 4)[:, i * P:width], bank(0, 4)[:, i * P:width], causal[:, :], ALU.add)
                    dve.drain()
                    dve.reduce_max(mx[:, i:i + 1], bank(0, 4)[:, 0:width], axis=AX.X)
                    dve.drain()
                    dve.tensor_scalar(mx[:, i:i + 1], mx[:, i:i + 1], -scale, None, ALU.mult).then_inc(mr, 1)

                maximum(0)
                for i in range(TILES):
                    if i + 1 < TILES:
                        maximum(i + 1)
                    for n in range(first[i], first[i + 1]):
                        m = groups[n][2]
                        dve.wait_ge(tr, n + 1)
                        if n >= 2:
                            dve.wait_ge(pv, n - 1)
                        dve.tensor_copy(probT[:, n % 2, 0:m * P], bank(4 + n % 2)[:, 0:m * P]).then_inc(tc, 1)
                    dve.reciprocal(den[:, i:i + 1], den[:, i:i + 1])
                    dve.drain()
                    dve.wait_ge(pv, first[i + 1])
                    dve.tensor_scalar(attn[:, i, :], bank(6 + i % 2)[:, 0:EHD], den[:, i:i + 1], None, ALU.mult)\
                       .then_inc(ou, 1)

            @block.scalar
            def _(act):
                for i in range(TILES):
                    width = (i + 1) * P
                    act.wait_ge(mr, i + 1)
                    act.activation(prob[:, i % 2, 0:width], bank(0, 4)[:, 0:width], ACT.Exp, bias=mx[:, i:i + 1],
                                   scale=scale, accum_out=den[:, i:i + 1]).then_inc(pr, 1)

    with ExitStack() as g:
        mix = tile(g, "mix", [P, 2, EXPERTS, EHD])
        mixT = tile(g, "mixT", [P, 2, 8, P])
        mr, tr, tc, yr, yu, st = (sem(n) for n in ("mix_ready", "mix_tr", "mix_copied", "o_ready", "o_used",
                                                   "x2_stored"))
        ln2 = layer_norm("ln2", g, tok, xT)
        with nc.Block() as block:
            @block.sync
            def _(sp):
                for g in range(TILES // 4):
                    rows = slice(4 * g * P, 4 * (g + 1) * P)
                    sp.wait_ge(ln2.done, g + 1)
                    sp.dma_start(x2_dram[b][rows, :].rearrange("(i p) d -> p i d", p=P),
                                 tok[:, 4 * g:4 * g + 4, :]).then_inc(st, 16)
                    sp.wait_ge(ln2.copied, 2 * g + 2)
                    sp.dma_start(x2T_dram[b].rearrange("(k p) n -> p k n", p=P)[:, :, rows],
                                 xT[:, :, rows]).then_inc(st, 16)
                sp.wait_ge(st, 2 * 16 * TILES // 4)

            @block.gpsimd
            def _(pool):
                for g in range(TILES // 4):
                    ln2.root(pool, g)

            @block.tensor
            def _(pe):
                def project(i):
                    pe.wait_ge(tc, 2 * i + 2)
                    if i >= 2:
                        pe.wait_ge(yu, i - 1)
                    for k in range(8):
                        last = pe.matmul(bank(4 + i % 2)[:, 0:D], mixT[:, i % 2, k, :], wo[:, k, :],
                                         start=(k == 0), stop=(k == 7))
                    last.then_inc(yr, 1)

                for i in range(TILES):
                    pe.wait_ge(mr, i + 1)
                    if i >= 2:
                        pe.wait_ge(tc, 2 * i - 2)
                    flat = mix[:, i % 2, :, :].rearrange("p e d -> p (e d)")
                    for h in range(2):
                        for k in range(4 * h, 4 * h + 4):
                            last = pe.transpose(bank(2 * (i % 2) + h)[:, (k % 4) * P:(k % 4 + 1) * P],
                                                flat[:, k * P:(k + 1) * P], ident[:, :])
                        last.then_inc(tr, 1)
                    if i:
                        project(i - 1)
                    if i >= 9 and i % 4 == 1:
                        ln2.transpose(pe, (i - 9) // 4)
                project(TILES - 1)
                ln2.transpose(pe, 2)
                ln2.transpose(pe, 3)

            @block.vector
            def _(dve):
                def add(i):
                    dve.wait_ge(yr, i + 1)
                    dve.tensor_tensor(tok[:, i, :], tok[:, i, :], bank(4 + i % 2)[:, 0:D], ALU.add).then_inc(yu, 1)

                def weigh(i):
                    if i >= 2:
                        dve.wait_ge(tr, 2 * i - 2)
                    dve.tensor_tensor(mix[:, i % 2, :, :], attn[:, i, :].unsqueeze(1).broadcast_to([P, EXPERTS, EHD]),
                                      rw[:, i, :].unsqueeze(2).broadcast_to([P, EXPERTS, EHD]), ALU.mult)\
                       .then_inc(mr, 1)

                weigh(0)
                for i in range(TILES):
                    if i + 1 < TILES:
                        weigh(i + 1)
                    if i:
                        add(i - 1)
                    if i and i % 4 == 0:
                        ln2.statistics(dve, i // 4 - 1)
                        if i > 4:
                            ln2.scale(dve, i // 4 - 2)
                add(TILES - 1)
                ln2.statistics(dve, TILES // 4 - 1)
                ln2.scale(dve, TILES // 4 - 2)
                ln2.scale(dve, TILES // 4 - 1)

            @block.scalar
            def _(act):
                for i in range(TILES):
                    for h in range(2):
                        act.wait_ge(tr, 2 * i + h + 1)
                        if i >= 2:
                            act.wait_ge(yr, i - 1)
                        act.activation(mixT[:, i % 2, 4 * h:4 * h + 4, :],
                                       bank(2 * (i % 2) + h).rearrange("p (k n) -> p k n", k=4),
                                       ACT.Copy).then_inc(tc, 1)
                    if i >= 9 and i % 4 == 1:
                        ln2.copy(act, (i - 9) // 4)
                ln2.copy(act, 2)
                ln2.copy(act, 3)


def layer1(nc, t, out, top, tile, sem, sems, clear, bank, ident, ones, layer_norm, x2_dram, x2T_dram):
    with ExitStack() as L:
        kept = tile(L, "kept", [P, MOE_TOK // P, D])
        with ExitStack() as W:
            w_in = tile(W, "w_in", [P, KC, 2 * INNER])
            w_dt = tile(W, "w_dt", [P, KI, INNER])
            w_x = tile(W, "w_x", [P, KI, 2 * STATE])
            w_out = tile(W, "w_out", [P, KI, D])
            cw = tile(W, "cw", [P, KI, TAPS])
            cb, bdt, dskip = (tile(W, n, [P, KI]) for n in ("cb", "bdt", "dskip"))
            a_neg = tile(W, "a_neg", [P, STATE])
            pick = tile(W, "pick", [P, 2 * STATE, P], BF16)
            bc3 = tile(W, "bc3", [P, SEQ], BF16)
            zero_bf = tile(W, "zero_bf", [P, P], BF16)
            tok = tile(W, "tok1", [P, TILES, D])
            ld, pz, pk, av = sem("l1_loaded"), sem("pick_zeroed"), sem("pick_ready"), sem("a_ready")
            with nc.Block() as block:
                @block.sync
                def _(sp):
                    for dst, name in ((w_in, "W_in"), (w_dt, "W_dt"), (w_x, "W_x"), (w_out, "W_out")):
                        sp.dma_start(dst[:, :, :], t[name].rearrange("(k p) n -> p k n", p=P)).then_inc(ld, 16)
                    with nc.allow_non_contiguous_dma(reason="vectors, once"):
                        sp.dma_start(cw[:, :, :], t["conv_w"].rearrange("(m p) j -> p m j", p=P)).then_inc(ld, 16)
                        for dst, name in ((cb, "conv_b"), (bdt, "b_dt"), (dskip, "D")):
                            sp.dma_start(dst[:, :], t[name].rearrange("(m p) -> p m", p=P)).then_inc(ld, 16)
                    sp.dma_start(a_neg[:, :], t["A_log"].partition_broadcast(P)).then_inc(ld, 16)

                @block.gpsimd
                def _(pool):
                    pool.memset(pick[:, :, :], 0.0)
                    pool.memset(zero_bf[:, :], 0.0)
                    pool.memset(bc3[:, :], 0.0).then_inc(pz, 1)
                    for part in range(3):
                        pool.wait_ge(pz, part + 1)
                        pool.affine_select(out=pick[:, :, :], in_=pick[:, :, :], compare_op=ALU.not_equal,
                                           fill=1.0, base=-32 * part, pattern=[[-1, 2 * STATE], [0, P]],
                                           channel_multiplier=1).then_inc(pz, 1)

                @block.scalar
                def _(act):
                    act.wait_ge(ld, 16 * 9)
                    act.activation(a_neg[:, :], a_neg[:, :], ACT.Exp).then_inc(av, 1)
                    act.mul(cw[:, :, :], cw[:, :, :], 0.5)
                    act.mul(cb[:, :], cb[:, :], 0.5)
                    act.mul(w_out[:, :, :], w_out[:, :, :], 0.5)

                @block.vector
                def _(dve):
                    dve.wait_ge(av, 1)
                    dve.tensor_scalar(a_neg[:, :], a_neg[:, :], -1.0, None, ALU.mult)

            outside = set(sems)
            with nc.Fori(0, BATCH) as it:
                b = BATCH - 1 - it
                with ExitStack() as s:
                    state_space(nc, b, s, tile, sem, bank, ident, tok, w_in, w_dt, w_x, w_out, cw, cb, bdt, dskip,
                                a_neg, pick, bc3, zero_bf, x2_dram, x2T_dram, kept, layer_norm, out)
                clear(outside)
        with ExitStack() as s:
            experts(nc, t, out, s, tile, sem, bank, ident, ones, kept, layer_norm)


def state_space(nc, b, s, tile, sem, bank, ident, tok, w_in, w_dt, w_x, w_out, cw, cb, bdt, dskip, a_neg, pick, bc3,
                zero_bf, x2_dram, x2T_dram, kept, layer_norm, out):
    xT = tile(s, "x2T", [P, KC, SEQ])
    u = tile(s, "u", [P, KI, SEQ])
    with ExitStack() as g:
        xin = tile(g, "xin", [P, 2, TAPS - 1 + SEQ])
        xc = tile(g, "xc", [P, 2, SEQ])
        th = tile(g, "th", [P, 2, SEQ])
        x_in = [sem(f"x2_loaded{n}") for n in range(CHUNKS)]
        pr, cp, cv, tr, uu, z = (sem(n) for n in (
            "in_proj", "in_copied", "conv_done", "tanh_ready", "u_ready", "pad_zeroed"))
        with nc.Block() as block:
            @block.sync
            def _(sp):
                for n in range(CHUNKS):
                    at = slice(n * CHUNK, (n + 1) * CHUNK)
                    sp.dma_start(xT[:, :, at], x2T_dram[b].rearrange("(k p) n -> p k n", p=P)[:, :, at])\
                      .then_inc(x_in[n], 16)
                sp.dma_start(tok[:, :, :], x2_dram[b].rearrange("(i p) d -> p i d", p=P))\
                  .then_inc(sem("tok2_in"), 16)
                sp.wait_ge(sem("tok2_in"), 16)

            @block.gpsimd
            def _(pool):
                pool.memset(xin[:, :, 0:TAPS - 1], 0.0).then_inc(z, 1)

            @block.tensor
            def _(pe):
                for m in range(KI):
                    if m >= 2:
                        pe.wait_ge(cp, m - 1)
                    for n in range(CHUNKS):
                        if m == 0:
                            pe.wait_ge(x_in[n], 16)
                        for k in range(KC):
                            last = pe.matmul(bank(4 * (m % 2) + n), w_in[:, k, m * P:(m + 1) * P],
                                             xT[:, k, n * CHUNK:(n + 1) * CHUNK], start=(k == 0), stop=(k == KC - 1))
                    last.then_inc(pr, 1)

            @block.scalar
            def _(act):
                def tanh(m):
                    act.wait_ge(cv, m + 1)
                    if m >= 2:
                        act.wait_ge(uu, m - 1)
                    act.activation(th[:, m % 2, :], xc[:, m % 2, :], ACT.Tanh).then_inc(tr, 1)

                for m in range(KI):
                    act.wait_ge(pr, m + 1)
                    if m >= 2:
                        act.wait_ge(uu, m - 1)
                    act.activation(xc[:, m % 2, :], bank(4 * (m % 2), 4), ACT.Identity,
                                   bias=cb[:, m:m + 1], scale=cw[:, m, TAPS - 1:TAPS])
                    act.activation(xin[:, m % 2, TAPS - 1:], bank(4 * (m % 2), 4), ACT.Copy).then_inc(cp, 1)
                    if m:
                        tanh(m - 1)
                tanh(KI - 1)

            @block.vector
            def _(dve):
                dve.wait_ge(z, 1)

                def silu(m):
                    dve.wait_ge(tr, m + 1)
                    dve.scalar_tensor_tensor(u[:, m, :], th[:, m % 2, :], 1.0, xc[:, m % 2, :], ALU.add, ALU.mult)\
                       .then_inc(uu, 1)

                for m in range(KI):
                    dve.wait_ge(cp, m + 1)
                    for j in range(TAPS - 1):
                        op = dve.scalar_tensor_tensor(xc[:, m % 2, :], xin[:, m % 2, j:j + SEQ], cw[:, m, j:j + 1],
                                                      xc[:, m % 2, :], ALU.mult, ALU.add)
                        if j < TAPS - 2:
                            dve.drain()
                    op.then_inc(cv, 1)
                    if m:
                        silu(m - 1)
                silu(KI - 1)

    dt = tile(s, "dt", [P, KI, SEQ])
    dtu = tile(s, "dtu", [P, KI, SEQ])
    with ExitStack() as g:
        bc = tile(g, "bc", [2 * STATE, SEQ])
        mid = tile(g, "mid", [2 * STATE, SEQ], BF16)
        DT = [4, 0, 4, 0]
        bcr, bcc, dr, mn, ln, du = (sem(n) for n in ("bc_ready", "bc_copied", "dt_mm", "dt_min", "dt_ln", "dt_used"))
        with nc.Block() as block:
            @block.tensor
            def _(pe):
                for n in range(CHUNKS):
                    for k in range(KI):
                        last = pe.matmul(bank(n)[0:2 * STATE, :], w_x[:, k, :], u[:, k, n * CHUNK:(n + 1) * CHUNK],
                                         start=(k == 0), stop=(k == KI - 1))
                last.then_inc(bcr, 1)
                for m in range(KI):
                    if m == 1:
                        pe.wait_ge(bcc, 1)
                    if m >= 2:
                        pe.wait_ge(du, m - 1)
                    for n in range(CHUNKS):
                        for k in range(KI):
                            last = pe.matmul(bank(DT[m] + n), w_dt[:, k, m * P:(m + 1) * P],
                                             u[:, k, n * CHUNK:(n + 1) * CHUNK], start=(k == 0), stop=(k == KI - 1))
                    last.then_inc(dr, 1)

            @block.scalar
            def _(act):
                act.wait_ge(bcr, 1)
                act.activation(bc[:, :], bank(0, 4)[0:2 * STATE, :], ACT.Copy).then_inc(bcc, 1)
                for m in range(KI):
                    act.wait_ge(mn, m + 1)
                    act.activation(dtu[:, m, :], dtu[:, m, :], ACT.Exp).then_inc(ln, 1)
                    act.wait_ge(ln, 2 * m + 1)
                    act.activation(dtu[:, m, :], dtu[:, m, :], ACT.Ln, bias=1.0).then_inc(ln, 1)

            @block.vector
            def _(dve):
                dve.wait_ge(bcc, 1)
                dve.tensor_copy(bc3[0:32, :], bc[:, :])
                dve.drain()
                dve.tensor_tensor(bc[:, :], bc[:, :], bc3[0:32, :], ALU.subtract)
                dve.drain()
                dve.tensor_copy(mid[:, :], bc[:, :])
                dve.drain()
                dve.tensor_copy(bc3[32:64, :], mid[:, :])
                dve.tensor_tensor(bc3[64:96, :], bc[:, :], mid[:, :], ALU.subtract)
                def clip(m):
                    dve.wait_ge(dr, m + 1)
                    dve.tensor_scalar(dtu[:, m, :], bank(DT[m], 4), bdt[:, m:m + 1], 40.0, ALU.add, ALU.min)\
                       .then_inc(mn, 1)

                def softplus(m):
                    dve.wait_ge(ln, 2 * m + 2)
                    dve.scalar_tensor_tensor(dt[:, m, :], bank(DT[m], 4), bdt[:, m:m + 1], dtu[:, m, :],
                                             ALU.add, ALU.max).then_inc(du, 1)
                    dve.drain()
                    dve.tensor_tensor(dtu[:, m, :], dt[:, m, :], u[:, m, :], ALU.mult)

                clip(0)
                for m in range(1, KI):
                    softplus(m - 1)
                    clip(m)
                softplus(KI - 1)

    with ExitStack() as g:
        da, bb, h, hc = (tile(g, n, [P, 2, HALF]) for n in ("da", "bb", "h", "hc"))
        c_sb = tile(g, "c_sb", [P, HALF])
        state = tile(g, "state", [P, KI, STATE])
        br, cr, cc, yz, yd = (sem(n) for n in (
            "b_spread", "c_spread", "c_copied", "y_ready", "y_done"))
        bd = [sem(f"b_times_u{d}") for d in range(2)]
        sd = [sem(f"scan_done{d}") for d in range(2)]
        ar = [sem(f"decay_ready{d}") for d in range(2)]
        sv = [sem(f"state_free{d}") for d in range(2)]
        hr = [sem(f"product{d}") for d in range(2)]
        yr = [sem(f"product_free{d}") for d in range(2)]
        Y, BS, CS = 0, 4, 6
        rounds = [(pair, half) for pair in range(KI // 2) for half in range(2)]
        N = STATE
        with nc.Block() as block:
            @block.tensor
            def _(pe):
                for d in range(2):
                    pe.sem_inc(yr[d], 1)
                for g_, (pair, half) in enumerate(rounds):
                    o = g_ * N

                    def spread(row, where, ready):
                        for j in range(2):
                            last = pe.matmul(bank(where + j), pick[:, row, :],
                                             bc3[:, half * HALF + j * CHUNK:half * HALF + (j + 1) * CHUNK],
                                             start=True, stop=True)
                        last.then_inc(ready, 1)

                    def next_b(n):
                        pe.wait_ge(bd[0], n + o)
                        spread(n, BS, br)

                    def next_c(n):
                        pe.wait_ge(cc, n + o)
                        pe.wait_ge(hr[0], n + (o + 1))
                        spread(n + N, CS, cr)

                    def gather(n, d):
                        pe.wait_ge(hr[d], n + (o + 2))
                        for j in range(2):
                            last = pe.matmul(bank(Y + 2 * d + j), ident[:, :], hc[:, d, j * CHUNK:(j + 1) * CHUNK],
                                             start=False, stop=False)
                        last.then_inc(yr[d], 1)

                    if g_:
                        pe.wait_ge(yd, g_)
                    for j in range(4):
                        pe.matmul(bank(Y + j), zero_bf[:, :], bc3[:, 0:CHUNK], start=True, stop=False)
                    spread(0, BS, br)
                    spread(N, CS, cr)
                    next_b(1)
                    with pe.Fori(0, N - 2) as n:
                        next_c(n + 1)
                        gather(n, 0)
                        next_b(n + 2)
                        gather(n, 1)
                    next_c(N - 1)
                    for n in (N - 2, N - 1):
                        gather(n, 0)
                        gather(n, 1)
                    for j in range(4):
                        last = pe.matmul(bank(Y + j), zero_bf[:, :], bc3[:, 0:CHUNK], start=False, stop=True)
                    last.then_inc(yz, 1)

            @block.scalar
            def _(act):
                for d in range(2):
                    act.sem_inc(sv[d], 1)
                for g_, (pair, half) in enumerate(rounds):
                    o = g_ * N

                    def decay(n, d):
                        act.activation(da[:, d, :], dt[:, 2 * pair + d, half * HALF:(half + 1) * HALF], ACT.Exp,
                                       scale=a_neg[:, bass.ds(n, 1)]).then_inc(ar[d], 1)

                    def save(n, d):
                        act.wait_ge(sd[d], n + (o + 1))
                        act.activation(state[:, 2 * pair + d, bass.ds(n, 1)], h[:, d, HALF - 1:HALF], ACT.Copy)\
                           .then_inc(sv[d], 1)

                    def copy_c(n):
                        act.wait_ge(cr, n + (o + 1))
                        act.wait_ge(hr[1], n + (o + 1))
                        act.activation(c_sb[:, :], bank(CS, 2), ACT.Copy).then_inc(cc, 1)

                    decay(0, 1)
                    decay(0, 0)
                    copy_c(0)
                    with act.Fori(0, N - 1) as n:
                        for d in (1, 0):
                            save(n, d)
                            decay(n + 1, d)
                        copy_c(n + 1)
                    save(N - 1, 0)
                    save(N - 1, 1)

            @block.gpsimd
            def _(pool):
                for d in range(2):
                    pool.sem_inc(hr[d], 1)
                for g_ in range(len(rounds)):
                    o = g_ * N
                    with pool.Fori(0, N) as n:
                        now = pool.snap(n + (o + 1))
                        pool.wait_ge(cc, now)
                        pool.wait_ge(sd[1], now)
                        pool.wait_ge(yr[1], now)
                        pool.tensor_tensor(hc[:, 1, :], h[:, 1, :], c_sb[:, :], ALU.mult).then_inc(hr[1], 1)

            @block.vector
            def _(dve):
                for g_, (pair, half) in enumerate(rounds):
                    o = g_ * N
                    at = slice(half * HALF, (half + 1) * HALF)

                    def spread_u(now, d):
                        dve.wait_ge(br, now)
                        return dve.tensor_tensor(bb[:, d, :], dtu[:, 2 * pair + d, at], bank(BS, 2), ALU.mult)

                    def scan(n, now, d):
                        dve.wait_ge(ar[d], now)
                        dve.wait_ge(sv[d], now)
                        dve.wait_ge(bd[d], now)
                        dve.wait_ge(hr[d], now)
                        first = 0.0 if half == 0 else state[:, 2 * pair + d, bass.ds(n, 1)]
                        dve.tensor_tensor_scan(h[:, d, :], da[:, d, :], bb[:, d, :], first, ALU.mult, ALU.add)\
                           .then_inc(sd[d], 1)

                    def product(now):
                        dve.wait_ge(cc, now)
                        dve.wait_ge(yr[0], now)
                        dve.wait_ge(sd[0], now)
                        dve.tensor_tensor(hc[:, 0, :], h[:, 0, :], bank(CS, 2), ALU.mult).then_inc(hr[0], 1)

                    spread_u(o + 1, 1).then_inc(bd[1], 1)
                    spread_u(o + 1, 0).then_inc(bd[0], 1)
                    with dve.Fori(0, N - 1) as n:
                        now = dve.snap(n + (o + 1))
                        after = dve.snap(n + (o + 2))
                        scan(n, now, 1)
                        scan(n, now, 0)
                        dve.wait_ge(sd[1], now)
                        spread_u(after, 1).then_inc(bd[1], 1)
                        product(now)
                        spread_u(after, 0).then_inc(bd[0], 1)
                    scan(N - 1, o + N, 1)
                    scan(N - 1, o + N, 0)
                    product(o + N)
                    dve.wait_ge(yz, g_ + 1)
                    for d in range(2):
                        m = 2 * pair + d
                        op = dve.scalar_tensor_tensor(dt[:, m, at], u[:, m, at], dskip[:, m:m + 1],
                                                      bank(Y + 2 * d, 2), ALU.mult, ALU.add)
                    op.then_inc(yd, 1)

    with ExitStack() as g:
        th = tile(g, "thz", [P, 2, 2, CHUNK])
        pr, tr, zu, mm, su, kp, st = (sem(n) for n in ("z_proj", "z_tanh", "z_used", "out_mm", "out_used",
                                                       "tokens_kept", "out_stored"))
        ln3 = layer_norm("ln3", g, tok)
        ln4 = layer_norm("ln4", g, tok)
        units = [(n, h) for n in range(CHUNKS) for h in range(KI // 2)]
        with nc.Block() as block:
            @block.tensor
            def _(pe):
                def project(n):
                    pe.wait_ge(zu, 2 * n + 2)
                    for i in range(4 * n, 4 * n + 4):
                        if i >= 2:
                            pe.wait_ge(su, i - 1)
                        for k in range(KI):
                            last = pe.matmul(bank(6 + i % 2)[:, 0:D], dt[:, k, i * P:(i + 1) * P], w_out[:, k, :],
                                             start=(k == 0), stop=(k == KI - 1))
                        last.then_inc(mm, 1)

                for u, (n, h) in enumerate(units):
                    if u >= 3:
                        pe.wait_ge(zu, u - 2)
                    for j in range(2):
                        m = 2 * h + j
                        for k in range(KC):
                            last = pe.matmul(bank(2 * (u % 3) + j), w_in[:, k, INNER + m * P:INNER + (m + 1) * P],
                                             xT[:, k, n * CHUNK:(n + 1) * CHUNK], start=(k == 0), stop=(k == KC - 1))
                    last.then_inc(pr, 1)
                    if n and h:
                        project(n - 1)
                project(CHUNKS - 1)

            @block.scalar
            def _(act):
                def keep():
                    act.wait_ge(ln3.done, 1)
                    act.activation(kept[:, :, :], tok[:, 0:MOE_TOK // P, :], ACT.Copy).then_inc(kp, 1)

                for u in range(len(units)):
                    act.wait_ge(pr, u + 1)
                    if u >= 2:
                        act.wait_ge(zu, u - 1)
                    act.activation(th[:, u % 2, :, :], bank(2 * (u % 3), 2).rearrange("p (j n) -> p j n", j=2),
                                   ACT.Tanh, scale=0.5).then_inc(tr, 1)
                    if u == 5:
                        keep()

            @block.gpsimd
            def _(pool):
                for g in range(TILES // 4):
                    ln3.root(pool, g)
                    if g:
                        ln4.root(pool, g - 1)
                ln4.root(pool, TILES // 4 - 1)

            @block.vector
            def _(dve):
                def gate(u):
                    n, h = units[u]
                    at = slice(n * CHUNK, (n + 1) * CHUNK)
                    dve.wait_ge(tr, u + 1)
                    dve.scalar_tensor_tensor(th[:, u % 2, :, :], th[:, u % 2, :, :], 1.0,
                                             bank(2 * (u % 3), 2).rearrange("p (j n) -> p j n", j=2),
                                             ALU.add, ALU.mult)
                    dve.drain()
                    dve.tensor_tensor(dt[:, 2 * h:2 * h + 2, at], dt[:, 2 * h:2 * h + 2, at], th[:, u % 2, :, :],
                                      ALU.mult).then_inc(zu, 1)

                def second_statistics(g):
                    if g == 0:
                        dve.wait_ge(kp, 1)
                    ln4.statistics(dve, g)

                gate(0)
                gate(1)
                for g in range(TILES // 4):
                    if g + 1 < CHUNKS:
                        gate(2 * g + 2)
                        gate(2 * g + 3)
                    for i in range(4 * g, 4 * g + 4):
                        dve.wait_ge(mm, i + 1)
                        dve.tensor_tensor(tok[:, i, :], tok[:, i, :], bank(6 + i % 2)[:, 0:D], ALU.add)\
                           .then_inc(su, 1)
                        if g and i % 4 == 0:
                            ln3.scale(dve, g - 1)
                        if g and i % 4 == 1:
                            second_statistics(g - 1)
                        if g > 1 and i % 4 == 2:
                            ln4.scale(dve, g - 2)
                    ln3.statistics(dve, g)
                last = TILES // 4 - 1
                ln4.scale(dve, last - 1)
                ln3.scale(dve, last)
                second_statistics(last)
                ln4.scale(dve, last)

            @block.sync
            def _(sp):
                for g in range(TILES // 4):
                    sp.wait_ge(ln4.done, g + 1)
                    sp.dma_start(out[b][4 * g * P:4 * (g + 1) * P, :].rearrange("(i p) d -> p i d", p=P),
                                 tok[:, 4 * g:4 * g + 4, :]).then_inc(st, 16)
                sp.wait_ge(st, 16 * TILES // 4)


def experts(nc, t, out, s, tile, sem, bank, ident, ones, tok, layer_norm):
    MT = MOE_TOK // P
    st = sem("moe_out_stored")
    ln5 = layer_norm("ln5", s, tok, tiles=MT)
    gup = tile(s, "gup", [P, KC, MOE_E, 2, MOE_F])
    down = tile(s, "down", [P, MOE_F // P, MOE_E, D])
    gub = tile(s, "gub", [P, MOE_E, 2, KC])
    db = tile(s, "db", [1, MOE_E, D])
    two = tile(s, "two", [1, P])
    ri = tile(s, "ri", [P, MT, 2], I32)
    rif = tile(s, "rif", [P, MT, 2])
    rwt = tile(s, "rwt", [P, MT, MOE_E])
    cnt = tile(s, "cnt", [P, MT, MOE_E])
    x3T = tile(s, "x3T", [P, KC, MOE_TOK])
    gate = tile(s, "gate", [P, 2, KC, MOE_TOK])
    up = tile(s, "up", [P, 2, KC, MOE_TOK])
    th = tile(s, "moe_th", [P, 2, KC, MOE_TOK])
    inter = tile(s, "inter", [P, 2, KC, MOE_TOK])
    ld, tr, tc = sem("moe_loaded"), sem("x3_tr"), sem("x3_copied")
    gr, gm, gt, iu, ir, dr, du, rt = (sem(n) for n in (
        "gu_ready", "gate_clipped", "gate_tanh", "gu_used", "inter_ready", "down_ready", "down_used", "route_ready"))
    with nc.Block() as block:
        @block.sync
        def _(sp):
            for k in range(KC):
                rows = slice(k * P, (k + 1) * P)
                sp.dma_start(gup[:, k, :, :, :].rearrange("p e g f -> p e (g f)"),
                             t["gate_up"][:, rows, :].rearrange("e p n -> p e n")).then_inc(ld, 16)
                sp.dma_start(down[:, k, :, :], t["down"][:, rows, :].rearrange("e p n -> p e n")).then_inc(ld, 16)
            with nc.allow_non_contiguous_dma(reason="biases, once"):
                sp.dma_start(gub[:, :, :, :].rearrange("p e g k -> p (e g k)"),
                             t["gate_up_bias"].rearrange("(x p) -> p x", p=P)).then_inc(ld, 16)
            sp.dma_start(db[:, :, :], t["down_bias"].rearrange("(o e) d -> o e d", o=1)).then_inc(ld, 16)
            sp.dma_start(ri[:, :, :], t["router_indices"].rearrange("(i p) k -> p i k", p=P)).then_inc(ld, 16)
            sp.dma_start(rwt[:, :, :], t["routing_weights"].rearrange("(i p) e -> p i e", p=P)).then_inc(ld, 16)
            sp.wait_ge(ln5.done, 1)
            sp.dma_start(out[0, 0:MOE_TOK, :].rearrange("(i p) d -> p i d", p=P), tok[:, 0:MT, :]).then_inc(st, 16)
            sp.wait_ge(st, 16)

        @block.gpsimd
        def _(pool):
            pool.memset(two[:, :], 2.0).then_inc(sem("two_ready"), 1)
            ln5.root(pool, 0)

        @block.tensor
        def _(pe):
            for k in range(KC):
                for i in range(MT):
                    last = pe.transpose(bank(k)[:, i * P:(i + 1) * P], tok[:, i, k * P:(k + 1) * P], ident[:, :])
            last.then_inc(tr, 1)
            pe.wait_ge(tc, 1)
            pe.wait_ge(ld, 16 * 8)
            pe.wait_ge(sem("two_ready"), 1)

            def down_proj(e):
                pe.wait_ge(ir, e + 1)
                for i in range(MT):
                    if e >= 1:
                        pe.wait_ge(du, MT * (e - 1) + i + 1)
                    o = bank(4 + i)[:, 0:D]
                    for k in range(KC):
                        pe.matmul(o, inter[:, e % 2, k, i * P:(i + 1) * P], down[:, k, e, :], start=(k == 0),
                                  stop=False)
                    pe.matmul(o, two[:, :], db[:, e, :], start=False, stop=True).then_inc(dr, 1)

            for e in range(MOE_E):
                if e >= 1:
                    pe.wait_ge(iu, e)
                for g in range(2):
                    for m in range(KC):
                        for k in range(KC):
                            last = pe.matmul(bank(2 * g + m), gup[:, k, e, g, m * P:(m + 1) * P], x3T[:, k, :],
                                             start=(k == 0), stop=(k == KC - 1))
                last.then_inc(gr, 1)
                if e:
                    down_proj(e - 1)
            down_proj(MOE_E - 1)

        @block.scalar
        def _(act):
            act.wait_ge(tr, 1)
            act.activation(x3T[:, :, :], bank(0, 2).rearrange("p (k n) -> p k n", k=KC), ACT.Copy).then_inc(tc, 1)
            for e in range(MOE_E):
                act.wait_ge(gm, e + 1)
                act.activation(th[:, e % 2, :, :], gate[:, e % 2, :, :], ACT.Tanh, scale=ALPHA / 2).then_inc(gt, 1)

        @block.vector
        def _(dve):
            dve.wait_ge(ld, 16 * 8)
            dve.tensor_copy(rif[:, :, :], ri[:, :, :])
            dve.drain()
            for e in range(MOE_E):
                dve.tensor_scalar(gate[:, 0, 0, 2 * MT * e:2 * MT * (e + 1)], rif[:, :, :].rearrange("p i k -> p (i k)"),
                                  float(e), None, ALU.is_equal)
            dve.drain()
            for e in range(MOE_E):
                dve.tensor_reduce(cnt[:, :, e], gate[:, 0, 0, 2 * MT * e:2 * MT * (e + 1)]
                                  .rearrange("p (i k) -> p i k", k=2), AX.X, ALU.add)
            dve.drain()
            dve.scalar_tensor_tensor(cnt[:, :, :], cnt[:, :, :], 0.5, rwt[:, :, :], ALU.mult, ALU.mult)
            dve.drain()

            def collect(e):
                for i in range(MT):
                    dve.wait_ge(dr, MT * e + i + 1)
                    dve.scalar_tensor_tensor(tok[:, i, :], bank(4 + i)[:, 0:D], cnt[:, i, e:e + 1], tok[:, i, :],
                                             ALU.mult, ALU.add).then_inc(du, 1)

            for e in range(MOE_E):
                w = e % 2
                dve.wait_ge(gr, e + 1)
                for k in range(KC):
                    op = dve.tensor_scalar(gate[:, w, k, :], bank(k), gub[:, e, 0, k:k + 1], LIMIT, ALU.add, ALU.min)
                op.then_inc(gm, 1)
                for k in range(KC):
                    op = dve.tensor_scalar(up[:, w, k, :], bank(2 + k), gub[:, e, 1, k:k + 1], LIMIT, ALU.add,
                                           ALU.min)
                op.then_inc(iu, 1)
                dve.drain()
                dve.tensor_scalar(up[:, w, :, :], up[:, w, :, :], -LIMIT, 1.0, ALU.max, ALU.add)
                dve.wait_ge(gt, e + 1)
                dve.drain()
                dve.scalar_tensor_tensor(gate[:, w, :, :], th[:, w, :, :], 1.0, gate[:, w, :, :], ALU.add, ALU.mult)
                dve.drain()
                if e >= 2:
                    dve.wait_ge(dr, MT * (e - 1))
                dve.tensor_tensor(inter[:, w, :, :], gate[:, w, :, :], up[:, w, :, :], ALU.mult).then_inc(ir, 1)
                if e:
                    collect(e - 1)
            collect(MOE_E - 1)
            ln5.statistics(dve, 0)
            ln5.scale(dve, 0)


def _layout(x):
    import numpy as np

    a = {k: np.asarray(v) for k, v in x.items()}
    g = lambda n: a[n]
    gu, gub = g("L1_ffn_gate_up_proj"), g("L1_ffn_gate_up_proj_bias")
    qkv = np.concatenate([g("L0_ffn_q_proj"), g("L0_ffn_k_proj"), g("L0_ffn_v_proj")], axis=2)
    return {
        "x": g("L0_attn_x"),
        "xT": g("L0_attn_x").transpose(0, 2, 1),
        "WqkvgT": g("L0_attn_Wqkvg").T,
        "bqkvg": g("L0_attn_bqkvg"),
        "wave_frequency": g("L0_attn_wave_frequency"),
        "wave_damping": g("L0_attn_wave_damping"),
        "wave_phase": g("L0_attn_wave_phase"),
        "field_coupling": g("L0_attn_field_coupling"),
        "WoutT": g("L0_attn_Wout").T,
        "bout": g("L0_attn_bout"),
        "sim_matrix": g("L0_ffn_sim_matrix"),
        "gates": g("L0_ffn_gates"),
        "Wmoh": qkv.transpose(1, 0, 2).reshape(D, EXPERTS * QKV),
        "Wo": g("L0_ffn_o_proj").reshape(EXPERTS * EHD, D),
        "W_in": g("L1_attn_W_in"),
        "conv_w": g("L1_attn_conv_w").reshape(INNER, TAPS),
        "conv_b": g("L1_attn_conv_b"),
        "W_x": g("L1_attn_W_x"),
        "W_dt": g("L1_attn_W_dt"),
        "b_dt": g("L1_attn_b_dt"),
        "A_log": g("L1_attn_A_log"),
        "D": g("L1_attn_D"),
        "W_out": g("L1_attn_W_out"),
        "router_indices": g("L1_ffn_router_indices"),
        "routing_weights": g("L1_ffn_routing_weights"),
        "gate_up": gu.reshape(MOE_E, D, MOE_F, 2).transpose(0, 1, 3, 2).reshape(MOE_E, D, 2 * MOE_F),
        "gate_up_bias": gub.reshape(MOE_E, MOE_F, 2).transpose(0, 2, 1).reshape(-1),
        "down": g("L1_ffn_down_proj"),
        "down_bias": g("L1_ffn_down_proj_bias"),
    }


def kernel(**inputs):
    import concourse.bacc as _bacc
    import numpy as _np
    from concourse.bass_utils import run_bass_kernel_spmd as _run

    nc = _bacc.Bacc("TRN2", target_bir_lowering=False, num_devices=1)
    arrays, args = {}, {}
    for name, a in _layout(inputs).items():
        a = _np.ascontiguousarray(a)
        arrays[f"in_{name}"] = a
        args[name] = nc.dram_tensor(f"in_{name}", a.shape, mybir.dt.from_np(a.dtype), kind="ExternalInput").ap()
    out = nc.dram_tensor("out", (BATCH, SEQ, D), F32, kind="ExternalOutput").ap()
    build_program(nc, args, out)
    r = _run(nc, [arrays], core_ids=[0])
    return r.results[0]["out"]
```

```python
import math
from contextlib import ExitStack

import concourse.bass as bass
from concourse import mybir

F32 = mybir.dt.float32
F32R = mybir.dt.float32r
BF16 = mybir.dt.bfloat16
I32 = mybir.dt.int32
ALU = mybir.AluOpType
ACT = mybir.ActivationFunctionType
AX = mybir.AxisListType

P = 128
BATCH, SEQ, D = 4, 2048, 256
TILES = SEQ // P
CHUNK = 512
CHUNKS = SEQ // CHUNK
KC = D // P
EPS = 1e-5
HEADS, HD, FIELD = 16, 16, 512
LAST = FIELD - 2
EXPERTS, EHD = 16, 64
QKV = 3 * EHD
INNER, STATE, TAPS = 512, 16, 4
KI = INNER // P
MOE_E, MOE_TOK, MOE_F = 8, 512, 256
LIMIT, ALPHA = 7.0, 1.702
MASKED = -1e30
HALF = SEQ // 2


def build_program(nc, t, out):
    kpad = nc.dram_tensor("kernel_rows", (HEADS, 640), F32).ap()
    x2_dram = nc.dram_tensor("x_after_layer0", (BATCH, SEQ, D), F32).ap()
    x2T_dram = nc.dram_tensor("xT_after_layer0", (BATCH, D, SEQ), F32).ap()

    top = ExitStack()
    with top:
        def tile(stack, name, shape, dt=F32):
            return stack.enter_context(nc.sbuf_tensor(name, shape, dt))

        sems = {}

        def sem(name):
            if name not in sems:
                sems[name] = top.enter_context(nc.semaphore(name))
            return sems[name]

        def clear(names_before):
            numbers = [h.num for n, h in sems.items() if n not in names_before]
            nc.gpsimd.sem_clear(range(min(numbers), max(numbers) + 1))
            nc.all_engine_barrier(sem_only=True)

        PS = top.enter_context(nc.psum_tensor("PS", [P, 8 * CHUNK], F32))

        def bank(i, n=1):
            return PS[:, i * CHUNK:(i + n) * CHUNK]

        ident = tile(top, "ident", [P, P])
        ones = tile(top, "ones", [P, P])
        eps_pow = tile(top, "eps_pow", [P, TILES])
        half_pow = tile(top, "half_pow", [P, TILES])

        def layer_norm(name, s, tok, xT=None, tiles=TILES, tr_bank=6):
            stats = tile(s, name + "_stats", [P, tiles, 6])
            mv = tile(s, name + "_mv", [P, tiles, 2])
            var = tile(s, name + "_var", [P, tiles])
            rstd = tile(s, name + "_rstd", [P, tiles])
            var_ready, rstd_ready = sem(name + "_var_ready"), sem(name + "_rstd_ready")
            norm_done, tr_ready = sem(name + "_norm_done"), sem(name + "_tr_ready")
            tr_copied = sem(name + "_tr_copied")

            class Steps:
                done = norm_done
                copied = tr_copied

                @staticmethod
                def statistics(dve, g):
                    dve.drain()
                    for i in range(4 * g, 4 * g + 4):
                        dve.bn_stats(stats[:, i, :], tok[:, i, :])
                    dve.drain()
                    for i in range(4 * g, 4 * g + 4):
                        dve.bn_aggr(mv[:, i, :], stats[:, i, :])
                    dve.drain()
                    dve.tensor_scalar(var[:, 4 * g:4 * g + 4], mv[:, 4 * g:4 * g + 4, 1], EPS, None,
                                      ALU.add).then_inc(var_ready, 1)

                @staticmethod
                def root(pool, g):
                    pool.wait_ge(var_ready, g + 1)
                    w = slice(4 * g, 4 * g + 4)
                    pool.tensor_tensor(rstd[:, w], var[:, w], eps_pow[:, w], ALU.pow).then_inc(rstd_ready, 1)

                @staticmethod
                def scale(dve, g):
                    dve.wait_ge(rstd_ready, g + 1)
                    for i in range(4 * g, 4 * g + 4):
                        last = dve.tensor_scalar(tok[:, i, :], tok[:, i, :], mv[:, i, 0:1], rstd[:, i:i + 1],
                                                 ALU.subtract, ALU.mult)
                    last.then_inc(norm_done, 1)

                @staticmethod
                def transpose(pe, g):
                    pe.wait_ge(norm_done, g + 1)
                    for p in (2 * g, 2 * g + 1):
                        if p >= 2:
                            pe.wait_ge(tr_copied, p - 1)
                        for k in range(KC):
                            for j in range(2):
                                o = bank(tr_bank + p % 2)[:, k * 256 + j * P:k * 256 + (j + 1) * P]
                                last = pe.transpose(o, tok[:, 2 * p + j, k * P:(k + 1) * P], ident[:, :])
                        last.then_inc(tr_ready, 1)

                @staticmethod
                def copy(act, g):
                    for p in (2 * g, 2 * g + 1):
                        act.wait_ge(tr_ready, p + 1)
                        act.activation(xT[:, :, 256 * p:256 * p + 256],
                                       bank(tr_bank + p % 2).rearrange("p (k n) -> p k n", k=KC),
                                       ACT.Copy).then_inc(tr_copied, 1)

            return Steps

        with nc.Block() as block:
            c0, c1 = sem("const_zeroed"), sem("const_ready")

            @block.gpsimd
            def _(pool):
                pool.memset(ident[:, :], 0.0)
                pool.memset(ones[:, :], 1.0)
                pool.memset(eps_pow[:, :], -0.5)
                pool.memset(half_pow[:, :], 0.5).then_inc(c0, 1)
                pool.wait_ge(c0, 1)
                pool.affine_select(out=ident[:, :], in_=ident[:, :], compare_op=ALU.not_equal, fill=1.0,
                                   base=0, pattern=[[-1, P]], channel_multiplier=1).then_inc(c1, 1)

        layer0(nc, t, out, top, tile, sem, sems, clear, bank, ident, ones, half_pow, layer_norm, kpad, x2_dram,
               x2T_dram)
        layer1(nc, t, out, top, tile, sem, sems, clear, bank, ident, ones, layer_norm, x2_dram, x2T_dram)


def layer0(nc, t, out, top, tile, sem, sems, clear, bank, ident, ones, half_pow, layer_norm, kpad, x2_dram,
           x2T_dram):
    with ExitStack() as L:
        wqkvg = tile(L, "wqkvg", [P, KC, 4 * D])
        wout = tile(L, "wout", [P, KC, D])
        wmoh = [tile(L, "wmoh_" + part, [P, KC, EXPERTS * QKV], F32R) for part in ("hi", "lo")]
        wo = [tile(L, "wo_" + part, [P, EXPERTS * EHD // P, D], F32R) for part in ("hi", "lo")]
        bq = tile(L, "bq", [P, 4 * KC])
        bg_half = tile(L, "bg_half", [P, KC])
        bout = tile(L, "bout", [P, D])
        toep = tile(L, "toep", [P, HEADS, FIELD])
        cct = tile(L, "cct", [P, KC, D])
        simn = tile(L, "simn", [P, KC, P])
        gate_sig = tile(L, "gate_sig", [P, EXPERTS])
        causal = tile(L, "causal", [P, P], BF16)
        ident_bf = tile(L, "ident_bf", [P, P], BF16)

        with ExitStack() as s:
            freq, damp, phase = (tile(s, n, [HEADS, 1]) for n in ("freq", "damp", "phase"))
            ti = tile(s, "ti", [HEADS, FIELD], I32)
            tf = tile(s, "tf", [HEADS, FIELD])
            ang = tile(s, "ang", [HEADS, FIELD])
            turns = tile(s, "turns", [HEADS, FIELD])
            decay = tile(s, "decay", [HEADS, FIELD])
            krow = tile(s, "krow", [HEADS, 640])
            sm = tile(s, "sm", [HEADS, 8])
            fc = tile(s, "fc", [HEADS, HEADS])
            fcx = tile(s, "fcx", [HEADS, HEADS, HD])
            dm = tile(s, "dm", [P, HD])
            sim = tile(s, "sim", [P, KC, EXPERTS])
            simsq = tile(s, "simsq", [P, KC, EXPERTS])
            simr = tile(s, "simr", [P, EXPERTS])
            gts = tile(s, "gts", [P, EXPERTS])
            wmoh_in = tile(s, "wmoh_in", [P, KC, EXPERTS * QKV])
            wo_in = tile(s, "wo_in", [P, EXPERTS * EHD // P, D])
            hi_ready = sem("wmoh_hi_ready")
            small, big, c_zero, c_mask = sem("small_loaded"), sem("big_loaded"), sem("pads_zero"), sem("mask_ready")
            iota_ready, a1, v1 = sem("iota_ready"), sem("setup_act"), sem("setup_dve")
            sq_ready = sem("squares_ready")
            pw, m1, kst, tl = sem("setup_pow"), sem("setup_mm"), sem("kernel_stored"), sem("toep_loaded")
            with nc.Block() as block:
                @block.sync
                def _(sp):
                    for dst, name in ((freq, "wave_frequency"), (damp, "wave_damping"), (phase, "wave_phase")):
                        sp.dma_start(dst[:, :], t[name].rearrange("(h o) -> h o", o=1)).then_inc(small, 16)
                    sp.dma_start(fc[:, :], t["field_coupling"]).then_inc(small, 16)
                    sp.dma_start(sim[:, :, :], t["sim_matrix"].rearrange("(k p) e -> p k e", p=P)).then_inc(small, 16)
                    sp.dma_start(gts[:, :], t["gates"].partition_broadcast(P)).then_inc(small, 16)
                    with nc.allow_non_contiguous_dma(reason="a bias, once"):
                        sp.dma_start(bq[:, :], t["bqkvg"].rearrange("(m p) -> p m", p=P)).then_inc(small, 16)
                    sp.dma_start(bout[:, :], t["bout"].partition_broadcast(P)).then_inc(big, 16)
                    for dst, name in ((wmoh_in, "Wmoh"), (wqkvg, "WqkvgT"), (wout, "WoutT"), (wo_in, "Wo")):
                        sp.dma_start(dst[:, :, :], t[name].rearrange("(k p) n -> p k n", p=P)).then_inc(big, 16)
                    sp.wait_ge(v1, 6)
                    sp.dma_start(kpad, krow[:, :]).then_inc(kst, 16)
                    sp.wait_ge(kst, 16)
                    sp.dma_start(toep[:, :, :], bass.AP(tensor=kpad.tensor, offset=0,
                                                        ap=[[1, P], [640, HEADS], [1, FIELD]])).then_inc(tl, 16)
                    sp.wait_ge(tl, 16)
                    sp.wait_ge(big, 16 * 5)

                @block.gpsimd
                def _(pool):
                    pool.iota(ti[:, :], pattern=[[1, FIELD]], base=0, channel_multiplier=0).then_inc(iota_ready, 1)
                    pool.memset(simn[:, :, EXPERTS:P], 0.0)
                    pool.memset(krow[:, :], 0.0)
                    pool.memset(causal[:, :], 0.0).then_inc(c_zero, 1)
                    pool.wait_ge(c_zero, 1)
                    pool.affine_select(out=causal[:, :], in_=causal[:, :], compare_op=ALU.is_ge, fill=MASKED,
                                       base=0, pattern=[[-1, P]], channel_multiplier=1).then_inc(c_mask, 1)
                    pool.wait_ge(v1, 7)
                    pool.tensor_tensor(simr[:, :], simr[:, :], half_pow[:, 0:EXPERTS], ALU.pow).then_inc(pw, 1)

                @block.scalar
                def _(act):
                    act.wait_ge(small, 16 * 7)
                    act.mul(bg_half[:, :], bq[:, 3 * KC:4 * KC], 0.5)
                    act.activation(gate_sig[:, :], gts[:, :], ACT.Tanh, scale=0.5)
                    act.activation(sm[:, 0:1], damp[:, :], ACT.Abs).then_inc(a1, 1)
                    act.wait_ge(a1, 1)
                    act.activation(sm[:, 1:2], sm[:, 0:1], ACT.Exp, scale=-1.0).then_inc(a1, 1)
                    act.wait_ge(a1, 2)
                    act.activation(sm[:, 2:3], sm[:, 1:2], ACT.Ln, bias=1.0).then_inc(a1, 1)
                    act.wait_ge(v1, 2)
                    act.activation(decay[:, :], tf[:, :], ACT.Exp, scale=sm[:, 3:4]).then_inc(a1, 1)
                    act.wait_ge(v1, 3)
                    act.activation(fc[:, :], fc[:, :], ACT.Exp, accum_out=sm[:, 6:7]).then_inc(a1, 1)
                    act.wait_ge(v1, 4)
                    act.activation(ang[:, :], ang[:, :], ACT.Sin).then_inc(a1, 1)
                    act.wait_ge(big, 16 * 5)
                    act.activation(wmoh[0][:, :, :], wmoh_in[:, :, :], ACT.Copy).then_inc(hi_ready, 1)
                    act.activation(wo[0][:, :, :], wo_in[:, :, :], ACT.Copy).then_inc(hi_ready, 1)

                @block.vector
                def _(dve):
                    dve.tensor_copy(ident_bf[:, :], ident[:, :])
                    dve.wait_ge(iota_ready, 1)
                    dve.tensor_copy(tf[:, :], ti[:, :]).then_inc(v1, 1)
                    dve.wait_ge(small, 16 * 7)
                    dve.wait_ge(a1, 3)
                    dve.scalar_tensor_tensor(sm[:, 3:4], damp[:, :], 0.0, sm[:, 2:3], ALU.max, ALU.add)
                    dve.drain()
                    dve.tensor_scalar(sm[:, 3:4], sm[:, 3:4], -1.0, None, ALU.mult).then_inc(v1, 1)
                    dve.reduce_max(sm[:, 4:5], fc[:, :], axis=AX.X)
                    dve.drain()
                    dve.tensor_scalar(fc[:, :], fc[:, :], sm[:, 4:5], None, ALU.subtract).then_inc(v1, 1)
                    two_pi = 2 * math.pi
                    hi = 6.28125
                    mid = float(round((two_pi - hi) * 2 ** 21) / 2 ** 21)
                    lo = two_pi - hi - mid
                    magic = 1.5 * 2 ** 23
                    dve.tensor_scalar(ang[:, :], tf[:, :], freq[:, :], phase[:, :], ALU.mult, ALU.add)
                    dve.drain()
                    dve.tensor_scalar(turns[:, :], ang[:, :], 1 / two_pi, 0.25, ALU.mult, ALU.add)
                    dve.drain()
                    dve.tensor_scalar(turns[:, :], turns[:, :], magic, None, ALU.add)
                    dve.drain()
                    dve.tensor_scalar(turns[:, :], turns[:, :], magic, None, ALU.subtract)
                    for part in (hi, mid, lo):
                        dve.drain()
                        dve.scalar_tensor_tensor(ang[:, :], turns[:, :], -part, ang[:, :], ALU.mult, ALU.add)
                    dve.drain()
                    dve.tensor_scalar(ang[:, :], ang[:, :], math.pi / 2, 3.1415925, ALU.add, ALU.min)
                    dve.drain()
                    dve.tensor_scalar(ang[:, :], ang[:, :], -3.1415925, None, ALU.max).then_inc(v1, 1)
                    dve.wait_ge(a1, 5)
                    dve.reciprocal(sm[:, 6:7], sm[:, 6:7])
                    dve.drain()
                    dve.tensor_scalar(fc[:, :], fc[:, :], sm[:, 6:7], 0.5, ALU.mult, ALU.mult)
                    dve.drain()
                    dve.tensor_copy(fcx[:, :, :], fc[:, :].unsqueeze(2).broadcast_to([HEADS, HEADS, HD]))\
                       .then_inc(v1, 1)
                    dve.wait_ge(a1, 6)
                    dve.tensor_tensor(decay[:, :], decay[:, :], ang[:, :], ALU.mult)
                    dve.drain()
                    dve.tensor_reduce(sm[:, 7:8], decay[:, :], AX.X, ALU.add, apply_absolute_value=True)
                    dve.drain()
                    dve.tensor_scalar(sm[:, 7:8], sm[:, 7:8], 1e-8, None, ALU.max)
                    dve.drain()
                    dve.reciprocal(sm[:, 7:8], sm[:, 7:8])
                    dve.drain()
                    dve.wait_ge(c_zero, 1)
                    dve.tensor_scalar(krow[:, P - 1:P - 1 + FIELD], decay[:, :], sm[:, 7:8], None, ALU.mult)\
                       .then_inc(v1, 1)
                    dve.tensor_tensor(simsq[:, :, :], sim[:, :, :], sim[:, :, :], ALU.mult)
                    dve.tensor_scalar(gate_sig[:, :], gate_sig[:, :], 0.5, 0.5, ALU.mult, ALU.add)
                    dve.tensor_reduce(dm[:, :], ident[:, :].rearrange("p (j d) -> p d j", d=HD), AX.X, ALU.add)\
                       .then_inc(sq_ready, 1)
                    dve.wait_ge(m1, 1)
                    dve.tensor_copy(simr[:, :], bank(0)[:, 0:EXPERTS]).then_inc(v1, 1)
                    dve.wait_ge(pw, 1)
                    dve.tensor_scalar(simr[:, :], simr[:, :], 1e-12, None, ALU.max)
                    dve.drain()
                    dve.reciprocal(simr[:, :], simr[:, :])
                    dve.drain()
                    for k in range(KC):
                        dve.tensor_tensor(simn[:, k, 0:EXPERTS], sim[:, k, :], simr[:, :], ALU.mult)
                    dve.wait_ge(m1, 2)
                    for k in range(KC):
                        dve.tensor_tensor(cct[:, k, :].rearrange("p (i d) -> p i d", d=HD),
                                          bank(1 + k)[:, 0:HEADS].unsqueeze(2).broadcast_to([P, HEADS, HD]),
                                          dm[:, :].unsqueeze(1).broadcast_to([P, HEADS, HD]), ALU.mult)
                    dve.wait_ge(hi_ready, 1)
                    dve.tensor_tensor(wmoh[1][:, :, :], wmoh_in[:, :, :], wmoh[0][:, :, :].bitcast(F32), ALU.subtract)
                    dve.wait_ge(hi_ready, 2)
                    dve.tensor_tensor(wo[1][:, :, :], wo_in[:, :, :], wo[0][:, :, :].bitcast(F32), ALU.subtract)

                @block.tensor
                def _(pe):
                    pe.wait_ge(sq_ready, 1)
                    for k in range(KC):
                        last = pe.matmul(bank(0)[:, 0:EXPERTS], ones[:, :], simsq[:, k, :],
                                         start=(k == 0), stop=(k == KC - 1))
                    last.then_inc(m1, 1)
                    fr = fcx[:, :, :].rearrange("i j d -> i (j d)")
                    for k in range(KC):
                        last = pe.matmul(bank(1 + k)[:, 0:HEADS], fr[:, k * P:(k + 1) * P],
                                         ident[0:HEADS, 0:HEADS], start=True, stop=True)
                    last.then_inc(m1, 1)

        outside = set(sems)
        tok = tile(L, "tok", [P, TILES, D])
        xT = tile(L, "xT", [P, KC, SEQ])
        with nc.Fori(0, BATCH) as b:
            with ExitStack() as s:
                wave_branch(nc, t, b, s, tile, sem, bank, ident, tok, xT, wqkvg, bq, bg_half, bout, wout, toep,
                            cct, layer_norm)
            with ExitStack() as s:
                head_mixture(nc, b, s, tile, sem, bank, ident, half_pow, tok, xT, wmoh, wo, simn, gate_sig, causal,
                             ident_bf,
                             layer_norm, x2_dram, x2T_dram)
            clear(outside)


def wave_branch(nc, t, b, s, tile, sem, bank, ident, tok, xT, wqkvg, bq, bg_half, bout, wout, toep, cct,
                layer_norm):
    qg = tile(s, "qg", [P, KC, SEQ])
    dep = tile(s, "dep", [P, KC, FIELD])
    dep_late = tile(s, "dep_late", [P, 2, CHUNK])
    tmp = tile(s, "feat_tmp", [P, 2, 5, CHUNK])
    qf = tile(s, "qf", [P, 2, CHUNK])
    tail = tile(s, "tail", [P, KC, CHUNKS])
    dpad = tile(s, "dpad", [P, 4, HEADS, 32])
    conv = tile(s, "conv", [P, KC, FIELD])
    lastg = tile(s, "lastg", [P, KC])
    proj, feat, used = sem("proj_ready"), sem("feat_ready"), sem("proj_used")
    x_in = [sem(f"x_loaded{n}") for n in range(CHUNKS)]
    units = [(c, n) for c in range(KC) for n in range(CHUNKS)]
    with nc.Block() as block:
        @block.sync
        def _(sp):
            for n in range(CHUNKS):
                at = slice(n * CHUNK, (n + 1) * CHUNK)
                sp.dma_start(xT[:, :, at], t["xT"][b].rearrange("(k p) n -> p k n", p=P)[:, :, at])\
                  .then_inc(x_in[n], 16)
            sp.dma_start(tok[:, :, :], t["x"][b].rearrange("(i p) d -> p i d", p=P)).then_inc(sem("tok_in"), 16)
            sp.wait_ge(sem("tok_in"), 16)

        @block.gpsimd
        def _(pool):
            pool.memset(dpad[:, :, :, :], 0.0)
            pool.wait_ge(sem("tok_in"), 16)
            pool.tensor_tensor(tok[:, :, :], tok[:, :, :], bout[:, :].unsqueeze(1).broadcast_to([P, TILES, D]),
                               ALU.add)

        @block.tensor
        def _(pe):
            for u, (c, n) in enumerate(units):
                if c == 0:
                    pe.wait_ge(x_in[n], 16)
                if u >= 2:
                    pe.wait_ge(used, u - 1)
                for kind in range(4):
                    m = kind * KC + c
                    for k in range(KC):
                        last = pe.matmul(bank(4 * (u % 2) + kind), wqkvg[:, k, m * P:(m + 1) * P],
                                         xT[:, k, n * CHUNK:(n + 1) * CHUNK], start=(k == 0), stop=(k == KC - 1))
                last.then_inc(proj, 1)

        @block.scalar
        def _(act):
            for u, (c, n) in enumerate(units):
                act.wait_ge(proj, u + 1)
                if u >= 2:
                    act.wait_ge(used, u - 1)
                w = u % 2
                q, k, g = bank(4 * w), bank(4 * w + 1), bank(4 * w + 3)
                act.activation(tmp[:, w, 0, :], q, ACT.Exp, bias=bq[:, c:c + 1])
                act.activation(tmp[:, w, 1, :], q, ACT.Relu, bias=bq[:, c:c + 1])
                act.activation(tmp[:, w, 2, :], k, ACT.Exp, bias=bq[:, KC + c:KC + c + 1])
                act.activation(tmp[:, w, 3, :], k, ACT.Relu, bias=bq[:, KC + c:KC + c + 1])
                act.activation(tmp[:, w, 4, :], g, ACT.Tanh, bias=bg_half[:, c:c + 1], scale=0.5)\
                   .then_inc(feat, 1)

        @block.vector
        def _(dve):
            def reverse(c, sc):
                cells = dep[:, c, sc * P:(sc + 1) * P]
                dve.tensor_copy(conv[:, c, sc * P:(sc + 1) * P],
                                bass.AP(tensor=cells.tensor, offset=cells.offset + P - 1,
                                        ap=[list(cells.ap[0]), [-1, P]]))

            for u, (c, n) in enumerate(units):
                w, at = u % 2, slice(n * CHUNK, (n + 1) * CHUNK)
                dve.wait_ge(feat, u + 1)
                dve.drain()
                dve.scalar_tensor_tensor(qf[:, 0, :], tmp[:, w, 0, :], 1.0, tmp[:, w, 1, :], ALU.min, ALU.add)
                dve.scalar_tensor_tensor(qf[:, 1, :], tmp[:, w, 2, :], 1.0, tmp[:, w, 3, :], ALU.min, ALU.add)
                dve.drain()
                dve.scalar_tensor_tensor(qg[:, c, at], tmp[:, w, 4, :], 1.0, qf[:, 0, :], ALU.add, ALU.mult)
                deposit = dep[:, c, :] if n == 0 else dep_late[:, w, :]
                dve.scalar_tensor_tensor(deposit, bank(4 * w + 2), bq[:, 2 * KC + c:2 * KC + c + 1],
                                         qf[:, 1, :], ALU.add, ALU.mult).then_inc(used, 1)
                dve.drain()
                dve.tensor_reduce(tail[:, c, n:n + 1], deposit[:, LAST if n == 0 else 0:CHUNK], AX.X, ALU.add)
                if n == 0:
                    for sc in range(FIELD // P - 1):
                        reverse(c, sc)
                if n == CHUNKS - 1:
                    dve.drain()
                    dve.tensor_reduce(dep[:, c, LAST:LAST + 1], tail[:, c, :], AX.X, ALU.add)
                    dve.drain()
                    reverse(c, FIELD // P - 1)

    tr, trc, cv, cvc, fcr = (sem(n) for n in ("dep_tr", "dep_copied", "conv_ready", "conv_copied", "field_ready"))
    wd, mm, su = sem("wave_done"), sem("wout_ready"), sem("wout_used")
    ln1 = layer_norm("ln1", s, tok, xT)
    with nc.Block() as block:
        @block.tensor
        def _(pe):
            for sc in range(4):
                for c in range(KC):
                    last = pe.transpose(bank(sc)[:, c * P:(c + 1) * P], conv[:, c, sc * P:(sc + 1) * P], ident[:, :])
                last.then_inc(tr, 1)
            pe.wait_ge(trc, 4)
            for c in range(KC):
                for j in range(4):
                    steps = [(c * 8 + 2 * j, 0)] + [(c * 8 + 2 * j + e, sc) for sc in range(1, 4) for e in range(2)]
                    steps += [(c * 8 + 2 * j + 1, 0)]
                    for q, (h, sc) in enumerate(steps):
                        last = pe.matmul(bank(4 + c)[32 * j:32 * j + 32, sc * P:FIELD], dpad[:, sc, h, :],
                                         toep[:, h, 0:FIELD - sc * P], start=(q == 0), stop=(q == len(steps) - 1),
                                         tile_position=(0, 32 * j))
                last.then_inc(cv, 1)
            pe.wait_ge(cvc, KC)
            for m in range(KC):
                for k in range(KC):
                    last = pe.matmul(bank(6 + m), cct[:, k, m * P:(m + 1) * P], conv[:, k, :],
                                     start=(k == 0), stop=(k == KC - 1))
                last.then_inc(fcr, 1)
            for i in range(TILES):
                pe.wait_ge(wd, i // 4 + 1)
                if i >= 6:
                    pe.wait_ge(su, i - 5)
                for k in range(KC):
                    last = pe.matmul(bank(i % 6)[:, 0:D],
                                     qg[:, k, i * P:(i + 1) * P], wout[:, k, :], start=(k == 0), stop=(k == KC - 1))
                last.then_inc(mm, 1)
                if i in (10, 14):
                    ln1.transpose(pe, (i - 10) // 4)
            ln1.transpose(pe, 2)
            ln1.transpose(pe, 3)

        @block.scalar
        def _(act):
            for c in range(KC):
                act.wait_ge(cv, c + 1)
                act.activation(conv[:, c, :], bank(4 + c), ACT.Copy).then_inc(cvc, 1)
            for g in range(TILES // 4):
                ln1.copy(act, g)

        @block.gpsimd
        def _(pool):
            for g in range(TILES // 4):
                ln1.root(pool, g)

        @block.vector
        def _(dve):
            for sc in range(4):
                dve.wait_ge(tr, sc + 1)
                src = bank(sc)[:, 0:D].rearrange("p (j e d) -> p j e d", e=2, d=HD)
                dst = dpad[:, sc, :, :].rearrange("p (j e) c -> p j e c", e=2)
                dve.tensor_copy(dst[:, :, 0, 0:HD], src[:, :, 0, :])
                dve.tensor_copy(dst[:, :, 1, HD:2 * HD], src[:, :, 1, :]).then_inc(trc, 1)
            for m in range(KC):
                dve.wait_ge(fcr, m + 1)
                dve.tensor_copy(lastg[:, m:m + 1], bank(6 + m)[:, LAST:LAST + 1])
                dve.tensor_tensor(qg[:, m, 0:LAST + 1], qg[:, m, 0:LAST + 1], bank(6 + m)[:, 0:LAST + 1], ALU.mult)
            dve.drain()
            for n in range(CHUNKS):
                at = slice(max(LAST + 1, n * CHUNK), (n + 1) * CHUNK)
                for m in range(KC):
                    op = dve.tensor_scalar(qg[:, m, at], qg[:, m, at], lastg[:, m:m + 1], None, ALU.mult)
                op.then_inc(wd, 1)
            for g in range(TILES // 4):
                for i in range(4 * g, 4 * g + 4):
                    dve.wait_ge(mm, i + 1)
                    dve.tensor_tensor(tok[:, i, :], tok[:, i, :], bank(i % 6)[:, 0:D], ALU.add).then_inc(su, 1)
                ln1.statistics(dve, g)
                if g:
                    ln1.scale(dve, g - 1)
            ln1.scale(dve, TILES // 4 - 1)


def head_mixture(nc, b, s, tile, sem, bank, ident, half_pow, tok, xT, wmoh, wo, simn, gate_sig, causal, ident_bf,
                 layer_norm, x2_dram, x2T_dram):
    rw = tile(s, "rw", [P, TILES, EXPERTS])
    q_parts = tile(s, "q_parts", [P, SEQ], F32R)
    k_hi2 = tile(s, "k_hi2", [P, SEQ], F32R)
    k_lo = tile(s, "k_lo", [EHD, SEQ], F32R)
    v = tile(s, "v", [P, TILES, P])
    attn = tile(s, "attn", [P, TILES, EHD])
    with ExitStack() as g:
        lg, ex, fb, rep = (tile(g, n, [P, TILES, EXPERTS]) for n in ("lg", "ex", "fb", "rep"))
        top8 = tile(g, "top8", [P, TILES, 8])
        best = tile(g, "best", [P, TILES])
        ss, rs = tile(g, "ss", [P, TILES]), tile(g, "rs", [P, TILES])
        sq = tile(g, "sq", [P, 2, D])
        sr, sp_, lr, le, lx = (sem(n) for n in ("norm_sums", "norm_root", "logits_mm", "logits", "logits_exp"))
        with nc.Block() as block:
            @block.tensor
            def _(pe):
                for i in range(TILES):
                    for k in range(KC):
                        last = pe.matmul(bank(0, 4)[:, i * P:(i + 1) * P], xT[:, k, i * P:(i + 1) * P],
                                         simn[:, k, :], start=(k == 0), stop=(k == KC - 1))
                last.then_inc(lr, 1)

            @block.scalar
            def _(act):
                for i in range(TILES):
                    if i >= 2:
                        act.wait_ge(sr, i - 1)
                    act.activation(sq[:, i % 2, :], tok[:, i, :], ACT.Square, accum_out=ss[:, i:i + 1])\
                       .then_inc(sr, 1)
                act.wait_ge(le, 1)
                act.activation(ex[:, :, :], lg[:, :, :], ACT.Exp).then_inc(lx, 1)

            @block.gpsimd
            def _(pool):
                pool.wait_ge(sr, TILES)
                pool.tensor_tensor(rs[:, :], ss[:, :], half_pow[:, :], ALU.pow).then_inc(sp_, 1)

            @block.vector
            def _(dve):
                def wide(a):
                    return a.unsqueeze(2).broadcast_to([P, TILES, EXPERTS])

                dve.wait_ge(sp_, 1)
                dve.tensor_scalar(rs[:, :], rs[:, :], 1e-12, None, ALU.max)
                dve.drain()
                dve.reciprocal(rs[:, :], rs[:, :])
                dve.drain()
                dve.wait_ge(lr, 1)
                dve.tensor_tensor(lg[:, :, :], bank(0, 4).rearrange("p (i e) -> p i e", e=P)[:, :, 0:EXPERTS],
                                  wide(rs[:, :]), ALU.mult)
                dve.drain()
                dve.tensor_tensor(lg[:, :, :], lg[:, :, :],
                                  gate_sig[:, :].unsqueeze(1).broadcast_to([P, TILES, EXPERTS]), ALU.subtract)\
                   .then_inc(le, 1)
                dve.drain()
                for i in range(TILES):
                    dve.max(top8[:, i, :], lg[:, i, :])
                dve.drain()
                dve.tensor_copy(best[:, :], top8[:, :, 0])
                dve.drain()
                dve.memset(top8[:, :, 2:8], -3e38)
                dve.drain()
                for i in range(TILES):
                    dve.match_replace(rep[:, i, :], top8[:, i, :], lg[:, i, :], 1e30)
                dve.drain()
                dve.tensor_scalar(fb[:, :, :], rep[:, :, :], 1e29, None, ALU.is_gt)
                dve.tensor_scalar(best[:, :], best[:, :], 0.0, None, ALU.is_le)
                dve.drain()
                dve.tensor_tensor(fb[:, :, :], fb[:, :, :], wide(best[:, :]), ALU.mult)
                dve.wait_ge(lx, 1)
                dve.scalar_tensor_tensor(ex[:, :, :], lg[:, :, :], 0.0, ex[:, :, :], ALU.is_gt, ALU.mult)
                dve.drain()
                dve.tensor_tensor(ex[:, :, :], ex[:, :, :], fb[:, :, :], ALU.add)
                dve.drain()
                dve.tensor_reduce(ss[:, :], ex[:, :, :], AX.X, ALU.add)
                dve.drain()
                dve.reciprocal(ss[:, :], ss[:, :])
                dve.drain()
                dve.tensor_tensor(rw[:, :, :], ex[:, :, :], wide(ss[:, :]), ALU.mult)

    with ExitStack() as g:
        acc = tile(g, "acc", [P, 4, QKV])
        acc2 = tile(g, "acc2", [P, 2, QKV])
        qk = tile(g, "qk", [P, 2, 2, 2, EHD])
        xhi, xlo = (tile(g, n, [P, 2, KC, P], F32R) for n in ("xhi", "xlo"))
        pairs = EXPERTS // 2
        pr, pu, qr, qt, qc, ql, hi, lo = (sem(n) for n in (
            "pair_ready", "pair_used", "qk_ready", "qk_tr", "qk_hi_ready", "qk_lo_ready", "x_hi_ready", "x_lo_ready"))
        with nc.Block() as block:
            @block.gpsimd
            def _(pool):
                pool.memset(v[:, :, EHD:P], 0.0)
                for i in range(TILES):
                    pool.wait_ge(hi, i + 1)
                    if i >= 2:
                        pool.wait_ge(pr, pairs * (i - 1))
                    pool.tensor_tensor(xlo[:, i % 2, :, :], xT[:, :, i * P:(i + 1) * P],
                                       xhi[:, i % 2, :, :].bitcast(F32), ALU.subtract).then_inc(lo, 1)

            @block.tensor
            def _(pe):
                def flip(i):
                    pe.wait_ge(qr, i + 1)
                    if i >= 2:
                        pe.wait_ge(ql, i - 1)
                    for w in range(2):
                        last = pe.transpose(bank(6 + i % 2)[:, w * P:(w + 1) * P],
                                            qk[:, i % 2, w, :, :].rearrange("p r d -> p (r d)"), ident[:, :])
                    last.then_inc(qt, 1)

                passes = [(x, part, k) for x, part in ((xhi, 0), (xhi, 1), (xlo, 0)) for k in range(KC)]
                for i in range(TILES):
                    pe.wait_ge(lo, i + 1)
                    for j in range(pairs):
                        n = i * pairs + j
                        if n >= 6:
                            pe.wait_ge(pu, n - 5)
                        for q, (x, part, k) in enumerate(passes):
                            last = pe.matmul(bank(n % 6)[:, 0:2 * QKV], x[:, i % 2, k, :],
                                             wmoh[part][:, k, 2 * j * QKV:(2 * j + 2) * QKV],
                                             start=(q == 0), stop=(q == len(passes) - 1))
                        last.then_inc(pr, 1)
                    if i:
                        flip(i - 1)
                flip(TILES - 1)

            @block.vector
            def _(dve):
                def low_parts(i):
                    at = slice(i * P, (i + 1) * P)
                    dve.wait_ge(qc, i + 1)
                    dve.tensor_tensor(q_parts[EHD:P, at], bank(6 + i % 2)[EHD:P, 0:P], q_parts[EHD:P, at].bitcast(F32),
                                      ALU.subtract)
                    dve.tensor_tensor(k_lo[:, at], bank(6 + i % 2)[0:EHD, P:2 * P], k_hi2[0:EHD, at].bitcast(F32),
                                      ALU.subtract).then_inc(ql, 1)

                for i in range(TILES):
                    for e in range(EXPERTS):
                        n = i * pairs + e // 2
                        if e % 2 == 0:
                            dve.wait_ge(pr, n + 1)
                        if e % 4 == 0:
                            dve.drain()
                        src = bank(n % 6)[:, (e % 2) * QKV:(e % 2 + 1) * QKV]
                        if e < 4:
                            op = dve.tensor_scalar(acc[:, e, :], src, rw[:, i, e:e + 1], None, ALU.mult)
                        else:
                            op = dve.scalar_tensor_tensor(acc[:, e % 4, :], src, rw[:, i, e:e + 1], acc[:, e % 4, :],
                                                          ALU.mult, ALU.add)
                        if e % 2:
                            op.then_inc(pu, 1)
                    dve.drain()
                    dve.tensor_tensor(acc2[:, :, :], acc[:, 0:2, :], acc[:, 2:4, :], ALU.add)
                    dve.drain()
                    if i >= 2:
                        dve.wait_ge(qt, i - 1)
                    dve.tensor_tensor(v[:, i, 0:EHD], acc2[:, 0, 2 * EHD:QKV], acc2[:, 1, 2 * EHD:QKV], ALU.add)
                    twice = [acc2[:, j, 0:2 * EHD].rearrange("p (w d) -> p w d", d=EHD).unsqueeze(2)
                             .broadcast_to([P, 2, 2, EHD]) for j in range(2)]
                    dve.tensor_tensor(qk[:, i % 2, :, :, :], twice[0], twice[1], ALU.add).then_inc(qr, 1)
                    if i >= 2:
                        low_parts(i - 2)
                low_parts(TILES - 2)
                low_parts(TILES - 1)

            @block.scalar
            def _(act):
                def round_x(i):
                    if i >= 2:
                        act.wait_ge(pr, pairs * (i - 1))
                    act.activation(xhi[:, i % 2, :, :], xT[:, :, i * P:(i + 1) * P], ACT.Copy).then_inc(hi, 1)

                round_x(0)
                round_x(1)
                for i in range(TILES):
                    if i + 2 < TILES:
                        round_x(i + 2)
                    act.wait_ge(qt, i + 1)
                    act.activation(q_parts[:, i * P:(i + 1) * P], bank(6 + i % 2)[:, 0:P], ACT.Copy)
                    act.activation(k_hi2[:, i * P:(i + 1) * P], bank(6 + i % 2)[:, P:2 * P], ACT.Copy)\
                       .then_inc(qc, 1)

    with ExitStack() as g:
        prob = tile(g, "prob", [P, 2, SEQ])
        probT = tile(g, "probT", [P, 2, CHUNK])
        mx, den = tile(g, "mx", [P, TILES, CHUNKS]), tile(g, "den", [P, TILES, CHUNKS])
        mneg, dsum = tile(g, "mneg", [P, TILES]), tile(g, "dsum", [P, TILES])
        scale = 1.0 / math.sqrt(EHD)
        sr, mr, pr, tr, tc, pv, ou = (sem(n) for n in (
            "scores_ready", "max_ready", "probs_ready", "probs_tr", "probs_copied", "pv_done", "attn_used"))
        chunks = [(i, c, min(CHUNK, (i + 1) * P - c * CHUNK)) for i in range(TILES)
                  for c in range(-(-(i + 1) * P // CHUNK))]
        first = {i: min(n for n, x in enumerate(chunks) if x[0] == i) for i in range(TILES)}
        first[TILES] = len(chunks)
        with nc.Block() as block:
            @block.tensor
            def _(pe):
                def scores(i):
                    tile_q = slice(i * P, (i + 1) * P)
                    for n in range(first[i], first[i + 1]):
                        _, c, keys = chunks[n]
                        if i and c < first[i] - first[i - 1]:
                            pe.wait_ge(pr, first[i - 1] + c + 1)
                        at = slice(c * CHUNK, c * CHUNK + keys)
                        pe.matmul(bank(c)[:, 0:keys], q_parts[:, tile_q], k_hi2[:, at], start=True, stop=False)
                        diagonal = n == first[i + 1] - 1
                        last = pe.matmul(bank(c)[:, 0:keys], q_parts[0:EHD, tile_q], k_lo[:, at], start=False,
                                         stop=not diagonal)
                        if diagonal:
                            last = pe.matmul(bank(c)[:, keys - P:keys], ident_bf[:, :], causal[:, :], start=False,
                                             stop=True)
                        last.then_inc(sr, 1)

                def values(n):
                    i, c, keys = chunks[n]
                    pe.wait_ge(tc, n + 1)
                    if c == 0 and i >= 2:
                        pe.wait_ge(ou, i - 1)
                    for j in range(keys // P):
                        a = c * (CHUNK // P) + j
                        last = pe.matmul(bank(6 + i % 2)[:, 0:P], probT[:, n % 2, j * P:(j + 1) * P],
                                         v[:, a, :], start=(a == 0), stop=(a == i))
                    last.then_inc(pv, 1)

                scores(0)
                for i in range(TILES):
                    if i + 1 < TILES:
                        scores(i + 1)
                    for n in range(first[i], first[i + 1]):
                        _, c, keys = chunks[n]
                        pe.wait_ge(pr, n + 1)
                        if n >= 2:
                            pe.wait_ge(tc, n - 1)
                        for j in range(keys // P):
                            a = c * CHUNK + j * P
                            last = pe.transpose(bank(4 + n % 2)[:, j * P:(j + 1) * P], prob[:, i % 2, a:a + P],
                                                ident[:, :])
                        last.then_inc(tr, 1)
                        if n:
                            values(n - 1)
                values(len(chunks) - 1)

            @block.vector
            def _(dve):
                def maximum(i):
                    for n in range(first[i], first[i + 1]):
                        _, c, keys = chunks[n]
                        dve.wait_ge(sr, n + 1)
                        dve.reduce_max(mx[:, i, c:c + 1], bank(c)[:, 0:keys], axis=AX.X)
                    dve.drain()
                    top = mx[:, i, 0:1]
                    if first[i + 1] - first[i] > 1:
                        top = mneg[:, i:i + 1]
                        dve.reduce_max(top, mx[:, i, 0:first[i + 1] - first[i]], axis=AX.X)
                        dve.drain()
                    dve.tensor_scalar(mneg[:, i:i + 1], top, -scale, None, ALU.mult).then_inc(mr, 1)

                def result(i):
                    dve.wait_ge(pr, first[i + 1])
                    dve.reduce_sum(dsum[:, i:i + 1], den[:, i, 0:first[i + 1] - first[i]], axis=AX.X)
                    dve.drain()
                    dve.reciprocal(dsum[:, i:i + 1], dsum[:, i:i + 1])
                    dve.drain()
                    dve.wait_ge(pv, first[i + 1])
                    dve.tensor_scalar(attn[:, i, :], bank(6 + i % 2)[:, 0:EHD], dsum[:, i:i + 1], None, ALU.mult)\
                       .then_inc(ou, 1)

                maximum(0)
                for i in range(TILES):
                    if i + 1 < TILES:
                        maximum(i + 1)
                    for n in range(first[i], first[i + 1]):
                        keys = chunks[n][2]
                        dve.wait_ge(tr, n + 1)
                        if n >= 2:
                            dve.wait_ge(pv, n - 1)
                        dve.tensor_copy(probT[:, n % 2, 0:keys], bank(4 + n % 2)[:, 0:keys]).then_inc(tc, 1)
                        if i and n == first[i]:
                            result(i - 1)
                result(TILES - 1)

            @block.scalar
            def _(act):
                for i in range(TILES):
                    act.wait_ge(mr, i + 1)
                    for n in range(first[i], first[i + 1]):
                        _, c, keys = chunks[n]
                        act.activation(prob[:, i % 2, c * CHUNK:c * CHUNK + keys], bank(c)[:, 0:keys], ACT.Exp,
                                       bias=mneg[:, i:i + 1], scale=scale, accum_out=den[:, i, c:c + 1])\
                           .then_inc(pr, 1)

    with ExitStack() as g:
        mix = tile(g, "mix", [P, 2, EXPERTS, EHD])
        mix_hi, mix_lo = (tile(g, n, [P, 2, 8, P], F32R) for n in ("mix_hi", "mix_lo"))
        mr, tr, th, tc, yr, yu, st = (sem(n) for n in (
            "mix_ready", "mix_tr", "mix_hi_ready", "mix_lo_ready", "o_ready", "o_used", "x2_stored"))
        passes = [(x, part, k) for k in range(8) for x, part in ((mix_hi, 0), (mix_hi, 1), (mix_lo, 0))]
        ln2 = layer_norm("ln2", g, tok, xT)
        with nc.Block() as block:
            @block.sync
            def _(sp):
                for g in range(TILES // 4):
                    rows = slice(4 * g * P, 4 * (g + 1) * P)
                    sp.wait_ge(ln2.done, g + 1)
                    sp.dma_start(x2_dram[b][rows, :].rearrange("(i p) d -> p i d", p=P),
                                 tok[:, 4 * g:4 * g + 4, :]).then_inc(st, 16)
                    sp.wait_ge(ln2.copied, 2 * g + 2)
                    sp.dma_start(x2T_dram[b].rearrange("(k p) n -> p k n", p=P)[:, :, rows],
                                 xT[:, :, rows]).then_inc(st, 16)
                sp.wait_ge(st, 2 * 16 * TILES // 4)

            @block.gpsimd
            def _(pool):
                for i in range(TILES):
                    if i >= 2:
                        pool.wait_ge(tr, 2 * i - 2)
                    pool.tensor_tensor(mix[:, i % 2, :, :],
                                       attn[:, i, :].unsqueeze(1).broadcast_to([P, EXPERTS, EHD]),
                                       rw[:, i, :].unsqueeze(2).broadcast_to([P, EXPERTS, EHD]), ALU.mult)\
                        .then_inc(mr, 1)
                    if i >= 6 and i % 4 == 2:
                        ln2.root(pool, (i - 6) // 4)
                ln2.root(pool, TILES // 4 - 1)

            @block.tensor
            def _(pe):
                def project(i):
                    pe.wait_ge(tc, 2 * i + 2)
                    if i >= 2:
                        pe.wait_ge(yu, i - 1)
                    for q, (x, part, k) in enumerate(passes):
                        last = pe.matmul(bank(4 + i % 2)[:, 0:D], x[:, i % 2, k, :], wo[part][:, k, :],
                                         start=(q == 0), stop=(q == len(passes) - 1))
                    last.then_inc(yr, 1)

                for i in range(TILES):
                    pe.wait_ge(mr, i + 1)
                    if i >= 2:
                        pe.wait_ge(tc, 2 * i - 2)
                    flat = mix[:, i % 2, :, :].rearrange("p e d -> p (e d)")
                    for h in range(2):
                        for k in range(4 * h, 4 * h + 4):
                            last = pe.transpose(bank(2 * (i % 2) + h)[:, (k % 4) * P:(k % 4 + 1) * P],
                                                flat[:, k * P:(k + 1) * P], ident[:, :])
                        last.then_inc(tr, 1)
                    if i:
                        project(i - 1)
                    if i >= 9 and i % 4 == 1:
                        ln2.transpose(pe, (i - 9) // 4)
                project(TILES - 1)
                ln2.transpose(pe, 2)
                ln2.transpose(pe, 3)

            @block.vector
            def _(dve):
                def add(i):
                    dve.wait_ge(yr, i + 1)
                    dve.tensor_tensor(tok[:, i, :], tok[:, i, :], bank(4 + i % 2)[:, 0:D], ALU.add).then_inc(yu, 1)

                def low_parts(i):
                    for h in range(2):
                        dve.wait_ge(th, 2 * i + h + 1)
                        if i >= 2:
                            dve.wait_ge(yr, i - 1)
                        dve.tensor_tensor(mix_lo[:, i % 2, 4 * h:4 * h + 4, :],
                                          bank(2 * (i % 2) + h).rearrange("p (k n) -> p k n", k=4),
                                          mix_hi[:, i % 2, 4 * h:4 * h + 4, :].bitcast(F32), ALU.subtract)\
                           .then_inc(tc, 1)

                for i in range(TILES):
                    low_parts(i)
                    if i:
                        add(i - 1)
                    if i and i % 4 == 0:
                        ln2.statistics(dve, i // 4 - 1)
                        if i > 4:
                            ln2.scale(dve, i // 4 - 2)
                add(TILES - 1)
                ln2.statistics(dve, TILES // 4 - 1)
                ln2.scale(dve, TILES // 4 - 2)
                ln2.scale(dve, TILES // 4 - 1)

            @block.scalar
            def _(act):
                for i in range(TILES):
                    for h in range(2):
                        act.wait_ge(tr, 2 * i + h + 1)
                        if i >= 2:
                            act.wait_ge(yr, i - 1)
                        act.activation(mix_hi[:, i % 2, 4 * h:4 * h + 4, :],
                                       bank(2 * (i % 2) + h).rearrange("p (k n) -> p k n", k=4),
                                       ACT.Copy).then_inc(th, 1)
                    if i >= 9 and i % 4 == 1:
                        ln2.copy(act, (i - 9) // 4)
                ln2.copy(act, 2)
                ln2.copy(act, 3)


def layer1(nc, t, out, top, tile, sem, sems, clear, bank, ident, ones, layer_norm, x2_dram, x2T_dram):
    with ExitStack() as L:
        kept = tile(L, "kept", [P, MOE_TOK // P, D])
        with ExitStack() as W:
            w_in = tile(W, "w_in", [P, KC, 2 * INNER])
            w_dt = tile(W, "w_dt", [P, KI, INNER])
            w_x = tile(W, "w_x", [P, KI, 2 * STATE])
            w_out = tile(W, "w_out", [P, KI, D])
            cw = tile(W, "cw", [P, KI, TAPS])
            cb, bdt, dskip = (tile(W, n, [P, KI]) for n in ("cb", "bdt", "dskip"))
            a_neg = tile(W, "a_neg", [P, STATE])
            pick = tile(W, "pick", [P, 2 * STATE, P], BF16)
            bc3 = tile(W, "bc3", [P, SEQ], BF16)
            zero_bf = tile(W, "zero_bf", [P, P], BF16)
            tok = tile(W, "tok1", [P, TILES, D])
            ld, pz, pk, av = sem("l1_loaded"), sem("pick_zeroed"), sem("pick_ready"), sem("a_ready")
            with nc.Block() as block:
                @block.sync
                def _(sp):
                    for dst, name in ((w_in, "W_in"), (w_dt, "W_dt"), (w_x, "W_x"), (w_out, "W_out")):
                        sp.dma_start(dst[:, :, :], t[name].rearrange("(k p) n -> p k n", p=P)).then_inc(ld, 16)
                    with nc.allow_non_contiguous_dma(reason="vectors, once"):
                        sp.dma_start(cw[:, :, :], t["conv_w"].rearrange("(m p) j -> p m j", p=P)).then_inc(ld, 16)
                        for dst, name in ((cb, "conv_b"), (bdt, "b_dt"), (dskip, "D")):
                            sp.dma_start(dst[:, :], t[name].rearrange("(m p) -> p m", p=P)).then_inc(ld, 16)
                    sp.dma_start(a_neg[:, :], t["A_log"].partition_broadcast(P)).then_inc(ld, 16)

                @block.gpsimd
                def _(pool):
                    pool.memset(pick[:, :, :], 0.0)
                    pool.memset(zero_bf[:, :], 0.0)
                    pool.memset(bc3[:, :], 0.0).then_inc(pz, 1)
                    for part in range(3):
                        pool.wait_ge(pz, part + 1)
                        pool.affine_select(out=pick[:, :, :], in_=pick[:, :, :], compare_op=ALU.not_equal,
                                           fill=1.0, base=-32 * part, pattern=[[-1, 2 * STATE], [0, P]],
                                           channel_multiplier=1).then_inc(pz, 1)

                @block.scalar
                def _(act):
                    act.wait_ge(ld, 16 * 9)
                    act.activation(a_neg[:, :], a_neg[:, :], ACT.Exp).then_inc(av, 1)
                    act.mul(cw[:, :, :], cw[:, :, :], 0.5)
                    act.mul(cb[:, :], cb[:, :], 0.5)
                    act.mul(w_out[:, :, :], w_out[:, :, :], 0.5)

                @block.vector
                def _(dve):
                    dve.wait_ge(av, 1)
                    dve.tensor_scalar(a_neg[:, :], a_neg[:, :], -1.0, None, ALU.mult)

            outside = set(sems)
            with nc.Fori(0, BATCH) as it:
                b = BATCH - 1 - it
                with ExitStack() as s:
                    state_space(nc, b, s, tile, sem, bank, ident, tok, w_in, w_dt, w_x, w_out, cw, cb, bdt, dskip,
                                a_neg, pick, bc3, zero_bf, x2_dram, x2T_dram, kept, layer_norm, out)
                clear(outside)
        with ExitStack() as s:
            experts(nc, t, out, s, tile, sem, bank, ident, ones, kept, layer_norm)


def state_space(nc, b, s, tile, sem, bank, ident, tok, w_in, w_dt, w_x, w_out, cw, cb, bdt, dskip, a_neg, pick, bc3,
                zero_bf, x2_dram, x2T_dram, kept, layer_norm, out):
    xT = tile(s, "x2T", [P, KC, SEQ])
    u = tile(s, "u", [P, KI, SEQ])
    dt = tile(s, "dt", [P, KI, SEQ])
    dtu = tile(s, "dtu", [P, KI, SEQ])
    with ExitStack() as g:
        xin = tile(g, "xin", [P, 3, TAPS - 1 + HALF])
        xc = tile(g, "xc", [P, 3, HALF])
        th = tile(g, "th", [P, 2, HALF])
        halo = tile(g, "halo", [P, KI, TAPS - 1])
        bc = tile(g, "bc", [2 * STATE, HALF])
        mid = tile(g, "mid", [2 * STATE, HALF], BF16)
        x_in = [sem(f"x2_loaded{n}") for n in range(CHUNKS)]
        pr, cp, cv, tr, uu, z = (sem(n) for n in (
            "in_proj", "in_copied", "conv_done", "tanh_ready", "u_ready", "pad_zeroed"))
        bcr, bcc, bs, dr, mn, ln, du = (sem(n) for n in (
            "bc_ready", "bc_copied", "bc_split", "dt_mm", "dt_min", "dt_ln", "dt_used"))
        units = [(half, m) for half in range(2) for m in range(KI)]
        U, AHEAD = 2 * KI, KI + 2
        bc_bank, dt_bank = [4, 6], [6, 4, 6, 4, 0, 2, 4, 6]
        with nc.Block() as block:
            @block.sync
            def _(sp):
                for n in range(CHUNKS):
                    at = slice(n * CHUNK, (n + 1) * CHUNK)
                    sp.dma_start(xT[:, :, at], x2T_dram[b].rearrange("(k p) n -> p k n", p=P)[:, :, at])\
                      .then_inc(x_in[n], 16)
                sp.dma_start(tok[:, :, :], x2_dram[b].rearrange("(i p) d -> p i d", p=P))\
                  .then_inc(sem("tok2_in"), 16)
                sp.wait_ge(sem("tok2_in"), 16)

            @block.gpsimd
            def _(pool):
                pool.memset(xin[:, :, 0:TAPS - 1], 0.0).then_inc(z, 1)

            @block.tensor
            def _(pe):
                def in_proj(v):
                    half, m = units[v]
                    if v >= 2:
                        pe.wait_ge(cp, v - 1)
                    for j in range(2):
                        n = 2 * half + j
                        if m == 0:
                            pe.wait_ge(x_in[n], 16)
                        for k in range(KC):
                            last = pe.matmul(bank(2 * (v % 2) + j), w_in[:, k, m * P:(m + 1) * P],
                                             xT[:, k, n * CHUNK:(n + 1) * CHUNK], start=(k == 0), stop=(k == KC - 1))
                    last.then_inc(pr, 1)

                def u_proj(where, rows, weights, half, ready):
                    for j in range(2):
                        n = 2 * half + j
                        for k in range(KI):
                            last = pe.matmul(bank(where + j)[0:rows, :], weights(k),
                                             u[:, k, n * CHUNK:(n + 1) * CHUNK], start=(k == 0), stop=(k == KI - 1))
                    last.then_inc(ready, 1)

                def bc_proj(half):
                    pe.wait_ge(uu, KI * (half + 1))
                    if half:
                        pe.wait_ge(du, KI - 1)
                    u_proj(bc_bank[half], 2 * STATE, lambda k: w_x[:, k, :], half, bcr)

                def dt_proj(v):
                    half, m = units[v]
                    if dt_bank[v] == bc_bank[half]:
                        pe.wait_ge(bcc, half + 1)
                    if half == 0 and m >= 2:
                        pe.wait_ge(du, v - 1)
                    if half and dt_bank[v] < 4:
                        pe.wait_ge(cp, U - 1 + m)
                    if half and dt_bank[v] == 4:
                        pe.wait_ge(du, KI)
                    u_proj(dt_bank[v], P, lambda k: w_dt[:, k, m * P:(m + 1) * P], half, dr)

                for v in range(AHEAD):
                    in_proj(v)
                bc_proj(0)
                for v in range(KI):
                    dt_proj(v)
                    if AHEAD + v < U:
                        in_proj(AHEAD + v)
                bc_proj(1)
                for v in range(KI, U):
                    dt_proj(v)

            @block.scalar
            def _(act):
                def taps_in(v):
                    half, m = units[v]
                    w, src = v % 3, bank(2 * (v % 2), 2)
                    act.wait_ge(pr, v + 1)
                    if v >= 3:
                        act.wait_ge(uu, v - 2)
                    act.activation(xc[:, w, :], src, ACT.Identity, bias=cb[:, m:m + 1], scale=cw[:, m, TAPS - 1:TAPS])
                    if half == 0:
                        act.activation(halo[:, m, :], src[:, HALF - TAPS + 1:HALF], ACT.Copy)
                    else:
                        act.wait_ge(cp, m + 1)
                        act.activation(xin[:, w, 0:TAPS - 1], halo[:, m, :], ACT.Copy)
                    act.activation(xin[:, w, TAPS - 1:], src, ACT.Copy).then_inc(cp, 1)

                def tanh(v):
                    act.wait_ge(cv, v + 1)
                    act.activation(th[:, v % 2, :], xc[:, v % 3, :], ACT.Tanh).then_inc(tr, 1)

                def copy_bc(half):
                    act.wait_ge(bcr, half + 1)
                    if half:
                        act.wait_ge(bs, half)
                    act.activation(bc[:, :], bank(bc_bank[half], 2)[0:2 * STATE, :], ACT.Copy).then_inc(bcc, 1)

                def exp_ln(v):
                    half, m = units[v]
                    x = dtu[:, m, half * HALF:(half + 1) * HALF]
                    act.wait_ge(mn, v + 1)
                    act.activation(x, x, ACT.Exp).then_inc(ln, 1)
                    act.wait_ge(ln, 2 * v + 1)
                    act.activation(x, x, ACT.Ln, bias=1.0).then_inc(ln, 1)

                taps_in(0)
                for v in range(1, AHEAD):
                    taps_in(v)
                    tanh(v - 1)
                copy_bc(0)
                for v in range(AHEAD, U):
                    taps_in(v)
                    tanh(v - 1)
                    exp_ln(v - AHEAD)
                tanh(U - 1)
                for v in range(U - AHEAD, KI):
                    exp_ln(v)
                copy_bc(1)
                for v in range(KI, U):
                    exp_ln(v)

            @block.vector
            def _(dve):
                def conv(v):
                    m, w = units[v][1], v % 3
                    dve.wait_ge(cp, v + 1)
                    for j in range(TAPS - 1):
                        op = dve.scalar_tensor_tensor(xc[:, w, :], xin[:, w, j:j + HALF], cw[:, m, j:j + 1],
                                                      xc[:, w, :], ALU.mult, ALU.add)
                        if j < TAPS - 2:
                            dve.drain()
                    op.then_inc(cv, 1)

                def silu(v):
                    half, m = units[v]
                    dve.wait_ge(tr, v + 1)
                    dve.scalar_tensor_tensor(u[:, m, half * HALF:(half + 1) * HALF], th[:, v % 2, :], 1.0,
                                             xc[:, v % 3, :], ALU.add, ALU.mult).then_inc(uu, 1)

                def split_bc(half):
                    at = slice(half * HALF, (half + 1) * HALF)
                    dve.wait_ge(bcc, half + 1)
                    dve.tensor_copy(bc3[0:32, at], bc[:, :])
                    dve.drain()
                    dve.tensor_tensor(bc[:, :], bc[:, :], bc3[0:32, at], ALU.subtract)
                    dve.drain()
                    dve.tensor_copy(mid[:, :], bc[:, :])
                    dve.drain()
                    dve.tensor_copy(bc3[32:64, at], mid[:, :])
                    dve.tensor_tensor(bc3[64:96, at], bc[:, :], mid[:, :], ALU.subtract).then_inc(bs, 1)

                def clip(v):
                    half, m = units[v]
                    dve.wait_ge(dr, v + 1)
                    dve.tensor_scalar(dtu[:, m, half * HALF:(half + 1) * HALF], bank(dt_bank[v], 2), bdt[:, m:m + 1],
                                      40.0, ALU.add, ALU.min).then_inc(mn, 1)

                def softplus(v):
                    half, m = units[v]
                    at = slice(half * HALF, (half + 1) * HALF)
                    dve.wait_ge(ln, 2 * v + 2)
                    dve.scalar_tensor_tensor(dt[:, m, at], bank(dt_bank[v], 2), bdt[:, m:m + 1], dtu[:, m, at],
                                             ALU.add, ALU.max).then_inc(du, 1)
                    dve.drain()
                    dve.tensor_tensor(dtu[:, m, at], dt[:, m, at], u[:, m, at], ALU.mult)

                dve.wait_ge(z, 1)
                conv(0)
                for v in range(1, AHEAD):
                    conv(v)
                    silu(v - 1)
                clip(0)
                split_bc(0)
                for v in range(AHEAD, U):
                    conv(v)
                    silu(v - 1)
                    clip(v - AHEAD + 1)
                    softplus(v - AHEAD)
                silu(U - 1)
                for v in range(U - AHEAD, KI):
                    if v + 1 < KI:
                        clip(v + 1)
                    softplus(v)
                clip(KI)
                split_bc(1)
                for v in range(KI + 1, U):
                    clip(v)
                    softplus(v - 1)
                softplus(U - 1)

    with ExitStack() as g:
        da, bb, h, hc = (tile(g, n, [P, 2, HALF]) for n in ("da", "bb", "h", "hc"))
        c_sb = tile(g, "c_sb", [P, HALF])
        state = tile(g, "state", [P, KI, STATE])
        br, cr, cc, yz, yd = (sem(n) for n in (
            "b_spread", "c_spread", "c_copied", "y_ready", "y_done"))
        bd = [sem(f"b_times_u{d}") for d in range(2)]
        sd = [sem(f"scan_done{d}") for d in range(2)]
        ar = [sem(f"decay_ready{d}") for d in range(2)]
        sv = [sem(f"state_free{d}") for d in range(2)]
        hr = [sem(f"product{d}") for d in range(2)]
        yr = [sem(f"product_free{d}") for d in range(2)]
        Y, BS, CS = 0, 4, 6
        rounds = [(pair, half) for pair in range(KI // 2) for half in range(2)]
        N = STATE
        with nc.Block() as block:
            @block.tensor
            def _(pe):
                for d in range(2):
                    pe.sem_inc(yr[d], 1)
                def spread(row, half, where, ready):
                    for j in range(2):
                        last = pe.matmul(bank(where + j), pick[:, row, :],
                                         bc3[:, half * HALF + j * CHUNK:half * HALF + (j + 1) * CHUNK],
                                         start=True, stop=True)
                    last.then_inc(ready, 1)

                def next_b(n, row, half):
                    pe.wait_ge(bd[0], n)
                    spread(row, half, BS, br)

                def next_c(n, row, half):
                    pe.wait_ge(cc, n)
                    pe.wait_ge(hr[0], n + 1)
                    spread(row + N, half, CS, cr)

                def gather(now, d):
                    pe.wait_ge(hr[d], now + 1)
                    for j in range(2):
                        last = pe.matmul(bank(Y + 2 * d + j), ident[:, :], hc[:, d, j * CHUNK:(j + 1) * CHUNK],
                                         start=False, stop=False)
                    last.then_inc(yr[d], 1)

                spread(0, 0, BS, br)
                spread(N, 0, CS, cr)
                for g_, (pair, half) in enumerate(rounds):
                    o = g_ * N
                    if g_:
                        pe.wait_ge(yd, g_)
                    for j in range(4):
                        pe.matmul(bank(Y + j), zero_bf[:, :], bc3[:, 0:CHUNK], start=True, stop=False)
                    next_b(o + 1, 1, half)
                    with pe.Fori(0, N - 2) as n:
                        gather(n + (o + 1), 1)
                        next_c(n + (o + 1), n + 1, half)
                        gather(n + (o + 1), 0)
                        next_b(n + (o + 2), n + 2, half)
                    gather(o + N - 1, 1)
                    next_c(o + N - 1, N - 1, half)
                    gather(o + N - 1, 0)
                    if g_ + 1 < len(rounds):
                        next_b(o + N, 0, rounds[g_ + 1][1])
                    gather(o + N, 1)
                    if g_ + 1 < len(rounds):
                        next_c(o + N, 0, rounds[g_ + 1][1])
                    gather(o + N, 0)
                    for j in range(4):
                        last = pe.matmul(bank(Y + j), zero_bf[:, :], bc3[:, 0:CHUNK], start=False, stop=True)
                    last.then_inc(yz, 1)

            @block.scalar
            def _(act):
                for d in range(2):
                    act.sem_inc(sv[d], 1)
                for g_, (pair, half) in enumerate(rounds):
                    o = g_ * N

                    def decay(n, d):
                        act.activation(da[:, d, :], dt[:, 2 * pair + d, half * HALF:(half + 1) * HALF], ACT.Exp,
                                       scale=a_neg[:, bass.ds(n, 1)]).then_inc(ar[d], 1)

                    def save(n, d, o=o, pair=pair):
                        act.wait_ge(sd[d], n + (o + 1))
                        act.activation(state[:, 2 * pair + d, bass.ds(n, 1)], h[:, d, HALF - 1:HALF], ACT.Copy)\
                           .then_inc(sv[d], 1)

                    def copy_c(n):
                        act.wait_ge(cr, n + (o + 1))
                        act.wait_ge(hr[1], n + (o + 1))
                        act.activation(c_sb[:, :], bank(CS, 2), ACT.Copy).then_inc(cc, 1)

                    decay(0, 1)
                    if g_:
                        save_last()
                    decay(0, 0)
                    copy_c(0)
                    with act.Fori(0, N - 1) as n:
                        for d in (1, 0):
                            save(n, d)
                            decay(n + 1, d)
                        copy_c(n + 1)
                    save(N - 1, 1)

                    def save_last(save=save):
                        save(N - 1, 0)
                save_last()

            @block.gpsimd
            def _(pool):
                for d in range(2):
                    pool.sem_inc(hr[d], 1)
                for g_ in range(len(rounds)):
                    o = g_ * N
                    with pool.Fori(0, N) as n:
                        now = pool.snap(n + (o + 1))
                        pool.wait_ge(cc, now)
                        pool.wait_ge(sd[1], now)
                        pool.wait_ge(yr[1], now)
                        pool.tensor_tensor(hc[:, 1, :], h[:, 1, :], c_sb[:, :], ALU.mult).then_inc(hr[1], 1)

            @block.vector
            def _(dve):
                def spread_u(now, d, g_):
                    pair, half = rounds[g_]
                    dve.wait_ge(br, now)
                    dve.tensor_tensor(bb[:, d, :], dtu[:, 2 * pair + d, half * HALF:(half + 1) * HALF], bank(BS, 2),
                                      ALU.mult).then_inc(bd[d], 1)

                def collect_y(g_):
                    pair, half = rounds[g_]
                    at = slice(half * HALF, (half + 1) * HALF)
                    dve.wait_ge(yz, g_ + 1)
                    for d in range(2):
                        m = 2 * pair + d
                        op = dve.scalar_tensor_tensor(dt[:, m, at], u[:, m, at], dskip[:, m:m + 1],
                                                      bank(Y + 2 * d, 2), ALU.mult, ALU.add)
                    op.then_inc(yd, 1)

                spread_u(1, 1, 0)
                spread_u(1, 0, 0)
                for g_, (pair, half) in enumerate(rounds):
                    o = g_ * N

                    def scan(n, now, d):
                        dve.wait_ge(ar[d], now)
                        dve.wait_ge(sv[d], now)
                        dve.wait_ge(bd[d], now)
                        dve.wait_ge(hr[d], now)
                        first = 0.0 if half == 0 else state[:, 2 * pair + d, bass.ds(n, 1)]
                        dve.tensor_tensor_scan(h[:, d, :], da[:, d, :], bb[:, d, :], first, ALU.mult, ALU.add)\
                           .then_inc(sd[d], 1)

                    def product(now):
                        dve.wait_ge(cc, now)
                        dve.wait_ge(yr[0], now)
                        dve.wait_ge(sd[0], now)
                        dve.tensor_tensor(hc[:, 0, :], h[:, 0, :], bank(CS, 2), ALU.mult).then_inc(hr[0], 1)

                    def product_and_next(now, after):
                        dve.wait_ge(sd[1], now)
                        spread_u(after, 1, g_)
                        product(now)
                        spread_u(after, 0, g_)

                    scan(0, o + 1, 1)
                    scan(0, o + 1, 0)
                    if g_:
                        collect_y(g_ - 1)
                    product_and_next(o + 1, o + 2)
                    with dve.Fori(1, N - 1) as n:
                        now = dve.snap(n + (o + 1))
                        after = dve.snap(n + (o + 2))
                        scan(n, now, 1)
                        scan(n, now, 0)
                        product_and_next(now, after)
                    scan(N - 1, o + N, 1)
                    scan(N - 1, o + N, 0)
                    dve.wait_ge(sd[1], o + N)
                    if g_ + 1 < len(rounds):
                        spread_u(o + N + 1, 1, g_ + 1)
                    product(o + N)
                    if g_ + 1 < len(rounds):
                        spread_u(o + N + 1, 0, g_ + 1)
                collect_y(len(rounds) - 1)

    with ExitStack() as g:
        th = tile(g, "thz", [P, 2, 2, CHUNK])
        pr, tr, zu, mm, su, kp, st = (sem(n) for n in ("z_proj", "z_tanh", "z_used", "out_mm", "out_used",
                                                       "tokens_kept", "out_stored"))
        ln3 = layer_norm("ln3", g, tok)
        ln4 = layer_norm("ln4", g, tok)
        units = [(n, h) for n in range(CHUNKS) for h in range(KI // 2)]
        with nc.Block() as block:
            @block.tensor
            def _(pe):
                def project(n):
                    pe.wait_ge(zu, 2 * n + 2)
                    for i in range(4 * n, 4 * n + 4):
                        if i >= 2:
                            pe.wait_ge(su, i - 1)
                        for k in range(KI):
                            last = pe.matmul(bank(6 + i % 2)[:, 0:D], dt[:, k, i * P:(i + 1) * P], w_out[:, k, :],
                                             start=(k == 0), stop=(k == KI - 1))
                        last.then_inc(mm, 1)

                for u, (n, h) in enumerate(units):
                    if u >= 3:
                        pe.wait_ge(zu, u - 2)
                    for j in range(2):
                        m = 2 * h + j
                        for k in range(KC):
                            last = pe.matmul(bank(2 * (u % 3) + j), w_in[:, k, INNER + m * P:INNER + (m + 1) * P],
                                             xT[:, k, n * CHUNK:(n + 1) * CHUNK], start=(k == 0), stop=(k == KC - 1))
                    last.then_inc(pr, 1)
                    if n and h:
                        project(n - 1)
                project(CHUNKS - 1)

            @block.scalar
            def _(act):
                def keep():
                    act.wait_ge(ln3.done, 1)
                    act.activation(kept[:, :, :], tok[:, 0:MOE_TOK // P, :], ACT.Copy).then_inc(kp, 1)

                for u in range(len(units)):
                    act.wait_ge(pr, u + 1)
                    if u >= 2:
                        act.wait_ge(zu, u - 1)
                    act.activation(th[:, u % 2, :, :], bank(2 * (u % 3), 2).rearrange("p (j n) -> p j n", j=2),
                                   ACT.Tanh, scale=0.5).then_inc(tr, 1)
                    if u == 5:
                        keep()

            @block.gpsimd
            def _(pool):
                for g in range(TILES // 4):
                    ln3.root(pool, g)
                    if g:
                        ln4.root(pool, g - 1)
                ln4.root(pool, TILES // 4 - 1)

            @block.vector
            def _(dve):
                def gate(u):
                    n, h = units[u]
                    at = slice(n * CHUNK, (n + 1) * CHUNK)
                    dve.wait_ge(tr, u + 1)
                    dve.scalar_tensor_tensor(th[:, u % 2, :, :], th[:, u % 2, :, :], 1.0,
                                             bank(2 * (u % 3), 2).rearrange("p (j n) -> p j n", j=2),
                                             ALU.add, ALU.mult)
                    dve.drain()
                    dve.tensor_tensor(dt[:, 2 * h:2 * h + 2, at], dt[:, 2 * h:2 * h + 2, at], th[:, u % 2, :, :],
                                      ALU.mult).then_inc(zu, 1)

                def second_statistics(g):
                    if g == 0:
                        dve.wait_ge(kp, 1)
                    ln4.statistics(dve, g)

                gate(0)
                gate(1)
                for g in range(TILES // 4):
                    if g + 1 < CHUNKS:
                        gate(2 * g + 2)
                        gate(2 * g + 3)
                    for i in range(4 * g, 4 * g + 4):
                        dve.wait_ge(mm, i + 1)
                        dve.tensor_tensor(tok[:, i, :], tok[:, i, :], bank(6 + i % 2)[:, 0:D], ALU.add)\
                           .then_inc(su, 1)
                        if g and i % 4 == 0:
                            ln3.scale(dve, g - 1)
                        if g and i % 4 == 1:
                            second_statistics(g - 1)
                        if g > 1 and i % 4 == 2:
                            ln4.scale(dve, g - 2)
                    ln3.statistics(dve, g)
                last = TILES // 4 - 1
                ln4.scale(dve, last - 1)
                ln3.scale(dve, last)
                second_statistics(last)
                ln4.scale(dve, last)

            @block.sync
            def _(sp):
                for g in range(TILES // 4):
                    sp.wait_ge(ln4.done, g + 1)
                    sp.dma_start(out[b][4 * g * P:4 * (g + 1) * P, :].rearrange("(i p) d -> p i d", p=P),
                                 tok[:, 4 * g:4 * g + 4, :]).then_inc(st, 16)
                sp.wait_ge(st, 16 * TILES // 4)


def experts(nc, t, out, s, tile, sem, bank, ident, ones, tok, layer_norm):
    MT = MOE_TOK // P
    st = sem("moe_out_stored")
    ln5 = layer_norm("ln5", s, tok, tiles=MT)
    el = [sem(f"expert_loaded{e}") for e in range(MOE_E)]
    gup = tile(s, "gup", [P, KC, MOE_E, 2, MOE_F])
    down = tile(s, "down", [P, MOE_F // P, MOE_E, D])
    gub = tile(s, "gub", [P, MOE_E, 2, KC])
    db = tile(s, "db", [1, MOE_E, D])
    two = tile(s, "two", [1, P])
    ri = tile(s, "ri", [P, MT, 2], I32)
    rif = tile(s, "rif", [P, MT, 2])
    rwt = tile(s, "rwt", [P, MT, MOE_E])
    cnt = tile(s, "cnt", [P, MT, MOE_E])
    x3T = tile(s, "x3T", [P, KC, MOE_TOK])
    gate = tile(s, "gate", [P, 2, KC, MOE_TOK])
    up = tile(s, "up", [P, 2, KC, MOE_TOK])
    th = tile(s, "moe_th", [P, 2, KC, MOE_TOK])
    inter = tile(s, "inter", [P, 2, KC, MOE_TOK])
    ld, tr, tc = sem("moe_loaded"), sem("x3_tr"), sem("x3_copied")
    gr, gm, gt, iu, ir, dr, du, rt = (sem(n) for n in (
        "gu_ready", "gate_clipped", "gate_tanh", "gu_used", "inter_ready", "down_ready", "down_used", "route_ready"))
    with nc.Block() as block:
        @block.sync
        def _(sp):
            with nc.allow_non_contiguous_dma(reason="biases, once"):
                sp.dma_start(gub[:, :, :, :].rearrange("p e g k -> p (e g k)"),
                             t["gate_up_bias"].rearrange("(x p) -> p x", p=P)).then_inc(ld, 16)
            sp.dma_start(db[:, :, :], t["down_bias"].rearrange("(o e) d -> o e d", o=1)).then_inc(ld, 16)
            sp.dma_start(ri[:, :, :], t["router_indices"].rearrange("(i p) k -> p i k", p=P)).then_inc(ld, 16)
            sp.dma_start(rwt[:, :, :], t["routing_weights"].rearrange("(i p) e -> p i e", p=P)).then_inc(ld, 16)
            for e in range(MOE_E):
                sp.dma_start(gup[:, :, e, :, :].rearrange("p k g f -> p k (g f)"),
                             t["gate_up"][e].rearrange("(k p) n -> p k n", p=P)).then_inc(el[e], 16)
                sp.dma_start(down[:, :, e, :], t["down"][e].rearrange("(k p) n -> p k n", p=P)).then_inc(el[e], 16)
            sp.wait_ge(ln5.done, 1)
            sp.dma_start(out[0, 0:MOE_TOK, :].rearrange("(i p) d -> p i d", p=P), tok[:, 0:MT, :]).then_inc(st, 16)
            sp.wait_ge(st, 16)

        @block.gpsimd
        def _(pool):
            pool.memset(two[:, :], 2.0).then_inc(sem("two_ready"), 1)
            ln5.root(pool, 0)

        @block.tensor
        def _(pe):
            for k in range(KC):
                for i in range(MT):
                    last = pe.transpose(bank(k)[:, i * P:(i + 1) * P], tok[:, i, k * P:(k + 1) * P], ident[:, :])
            last.then_inc(tr, 1)
            pe.wait_ge(tc, 1)
            pe.wait_ge(ld, 16 * 4)
            pe.wait_ge(sem("two_ready"), 1)

            def down_proj(e):
                pe.wait_ge(ir, e + 1)
                for i in range(MT):
                    if e >= 1:
                        pe.wait_ge(du, MT * (e - 1) + i + 1)
                    o = bank(4 + i)[:, 0:D]
                    for k in range(KC):
                        pe.matmul(o, inter[:, e % 2, k, i * P:(i + 1) * P], down[:, k, e, :], start=(k == 0),
                                  stop=False)
                    pe.matmul(o, two[:, :], db[:, e, :], start=False, stop=True).then_inc(dr, 1)

            for e in range(MOE_E):
                pe.wait_ge(el[e], 2 * 16)
                if e >= 1:
                    pe.wait_ge(iu, e)
                for g in range(2):
                    for m in range(KC):
                        for k in range(KC):
                            last = pe.matmul(bank(2 * g + m), gup[:, k, e, g, m * P:(m + 1) * P], x3T[:, k, :],
                                             start=(k == 0), stop=(k == KC - 1))
                last.then_inc(gr, 1)
                if e:
                    down_proj(e - 1)
            down_proj(MOE_E - 1)

        @block.scalar
        def _(act):
            act.wait_ge(tr, 1)
            act.activation(x3T[:, :, :], bank(0, 2).rearrange("p (k n) -> p k n", k=KC), ACT.Copy).then_inc(tc, 1)
            for e in range(MOE_E):
                act.wait_ge(gm, e + 1)
                act.activation(th[:, e % 2, :, :], gate[:, e % 2, :, :], ACT.Tanh, scale=ALPHA / 2).then_inc(gt, 1)

        @block.vector
        def _(dve):
            dve.wait_ge(ld, 16 * 4)
            dve.tensor_copy(rif[:, :, :], ri[:, :, :])
            dve.drain()
            for e in range(MOE_E):
                dve.tensor_scalar(gate[:, 0, 0, 2 * MT * e:2 * MT * (e + 1)], rif[:, :, :].rearrange("p i k -> p (i k)"),
                                  float(e), None, ALU.is_equal)
            dve.drain()
            for e in range(MOE_E):
                dve.tensor_reduce(cnt[:, :, e], gate[:, 0, 0, 2 * MT * e:2 * MT * (e + 1)]
                                  .rearrange("p (i k) -> p i k", k=2), AX.X, ALU.add)
            dve.drain()
            dve.scalar_tensor_tensor(cnt[:, :, :], cnt[:, :, :], 0.5, rwt[:, :, :], ALU.mult, ALU.mult)
            dve.drain()

            def collect(e):
                for i in range(MT):
                    dve.wait_ge(dr, MT * e + i + 1)
                    dve.scalar_tensor_tensor(tok[:, i, :], bank(4 + i)[:, 0:D], cnt[:, i, e:e + 1], tok[:, i, :],
                                             ALU.mult, ALU.add).then_inc(du, 1)

            for e in range(MOE_E):
                w = e % 2
                dve.wait_ge(gr, e + 1)
                for k in range(KC):
                    op = dve.tensor_scalar(gate[:, w, k, :], bank(k), gub[:, e, 0, k:k + 1], LIMIT, ALU.add, ALU.min)
                op.then_inc(gm, 1)
                for k in range(KC):
                    op = dve.tensor_scalar(up[:, w, k, :], bank(2 + k), gub[:, e, 1, k:k + 1], LIMIT, ALU.add,
                                           ALU.min)
                op.then_inc(iu, 1)
                dve.drain()
                dve.tensor_scalar(up[:, w, :, :], up[:, w, :, :], -LIMIT, 1.0, ALU.max, ALU.add)
                dve.wait_ge(gt, e + 1)
                dve.drain()
                dve.scalar_tensor_tensor(gate[:, w, :, :], th[:, w, :, :], 1.0, gate[:, w, :, :], ALU.add, ALU.mult)
                dve.drain()
                if e >= 2:
                    dve.wait_ge(dr, MT * (e - 1))
                dve.tensor_tensor(inter[:, w, :, :], gate[:, w, :, :], up[:, w, :, :], ALU.mult).then_inc(ir, 1)
                if e:
                    collect(e - 1)
            collect(MOE_E - 1)
            ln5.statistics(dve, 0)
            ln5.scale(dve, 0)


def _layout(x):
    import numpy as np

    a = {k: np.asarray(v) for k, v in x.items()}
    g = lambda n: a[n]
    gu, gub = g("L1_ffn_gate_up_proj"), g("L1_ffn_gate_up_proj_bias")
    qkv = np.concatenate([g("L0_ffn_q_proj"), g("L0_ffn_k_proj"), g("L0_ffn_v_proj")], axis=2)
    return {
        "x": g("L0_attn_x"),
        "xT": g("L0_attn_x").transpose(0, 2, 1),
        "WqkvgT": g("L0_attn_Wqkvg").T,
        "bqkvg": g("L0_attn_bqkvg"),
        "wave_frequency": g("L0_attn_wave_frequency"),
        "wave_damping": g("L0_attn_wave_damping"),
        "wave_phase": g("L0_attn_wave_phase"),
        "field_coupling": g("L0_attn_field_coupling"),
        "WoutT": g("L0_attn_Wout").T,
        "bout": g("L0_attn_bout"),
        "sim_matrix": g("L0_ffn_sim_matrix"),
        "gates": g("L0_ffn_gates"),
        "Wmoh": qkv.transpose(1, 0, 2).reshape(D, EXPERTS * QKV),
        "Wo": g("L0_ffn_o_proj").reshape(EXPERTS * EHD, D),
        "W_in": g("L1_attn_W_in"),
        "conv_w": g("L1_attn_conv_w").reshape(INNER, TAPS),
        "conv_b": g("L1_attn_conv_b"),
        "W_x": g("L1_attn_W_x"),
        "W_dt": g("L1_attn_W_dt"),
        "b_dt": g("L1_attn_b_dt"),
        "A_log": g("L1_attn_A_log"),
        "D": g("L1_attn_D"),
        "W_out": g("L1_attn_W_out"),
        "router_indices": g("L1_ffn_router_indices"),
        "routing_weights": g("L1_ffn_routing_weights"),
        "gate_up": gu.reshape(MOE_E, D, MOE_F, 2).transpose(0, 1, 3, 2).reshape(MOE_E, D, 2 * MOE_F),
        "gate_up_bias": gub.reshape(MOE_E, MOE_F, 2).transpose(0, 2, 1).reshape(-1),
        "down": g("L1_ffn_down_proj"),
        "down_bias": g("L1_ffn_down_proj_bias"),
    }


def kernel(**inputs):
    import concourse.bacc as _bacc
    import numpy as _np
    from concourse.bass_utils import run_bass_kernel_spmd as _run

    nc = _bacc.Bacc("TRN2", target_bir_lowering=False, num_devices=1)
    arrays, args = {}, {}
    for name, a in _layout(inputs).items():
        a = _np.ascontiguousarray(a)
        arrays[f"in_{name}"] = a
        args[name] = nc.dram_tensor(f"in_{name}", a.shape, mybir.dt.from_np(a.dtype), kind="ExternalInput").ap()
    out = nc.dram_tensor("out", (BATCH, SEQ, D), F32, kind="ExternalOutput").ap()
    build_program(nc, args, out)
    r = _run(nc, [arrays], core_ids=[0])
    return r.results[0]["out"]
```
